# Optimizing a Trainium2 kernel written in Bass

```python
import numpy as np
import jax
import jax.numpy as jnp

def _softmax(x, axis=-1):
    return jax.nn.softmax(x, axis=axis)

def _gelu(x):
    return jax.nn.gelu(x, approximate=True)

def _silu(x):
    return jax.nn.silu(x)

def _sigmoid(x):
    return jax.nn.sigmoid(x)

def _layernorm(x, axis=-1, eps=1e-05):
    m = jnp.mean(x, axis=axis, keepdims=True)
    v = jnp.var(x, axis=axis, keepdims=True)
    return (x - m) / jnp.sqrt(v + eps)

def _scatter_add(tgt, idx, src, axis=0):
    return tgt.at[idx].add(src)

def _segment_sum(src, seg, n):
    return jax.ops.segment_sum(src, seg, n)
kernel_name = 'mk_decoder_postln_d2_seqx_r4_8d17c4'

def setup_inputs(seed: int=0):
    np.random.seed(seed)
    _w = jnp.asarray

    def _rec_inputs():
        import jax
        import jax.numpy as jnp
        _rk = jax.random.key(seed)
        x = 7.22e-05 + 1 * jax.random.normal(jax.random.fold_in(_rk, 1), (8, 256, 256), jnp.float32)
        _lenS = 256 - jax.random.randint(jax.random.fold_in(_rk, 7), (8,), 0, max(1, 256 // 4) + 1, jnp.int32)
        _lenS2 = 256 - jax.random.randint(jax.random.fold_in(_rk, 8), (8,), 0, max(1, 256 // 4) + 1, jnp.int32)
        _ctx_768P = jax.random.normal(jax.random.fold_in(_rk, 11), (8, 16, 192), jnp.float32)
        _ctx_768c = jax.random.dirichlet(jax.random.fold_in(_rk, 511), 0.3 * jnp.ones((16,), jnp.float32), (8, 256))
        _ctx_768t = jnp.einsum('bsk,bkd->bsd', _ctx_768c, _ctx_768P)
        _ctx_768t = _ctx_768t * jax.lax.rsqrt(jnp.mean(jnp.square(_ctx_768t)) + 1e-12) * 0.953939
        ctx_768 = -0.000191848 + 0.999787 * (_ctx_768t + 0.3 * jax.random.normal(jax.random.fold_in(_rk, 611), (8, 256, 192), jnp.float32))
        _validS = jnp.arange(256)[None, :] < _lenS[:, None]
        _validS2 = jnp.arange(256)[None, :] < _lenS2[:, None]
        _causal = jnp.tril(jnp.ones((256, 256), dtype=bool))
        mask_BxS_bf1 = jnp.ones((8, 256), dtype=bool)
        mask_BxS2_bf1 = jnp.ones((8, 256), dtype=bool)
        return (x, ctx_768, mask_BxS_bf1, mask_BxS2_bf1)
    x, ctx_768, mask_BxS_bf1, mask_BxS2_bf1 = _rec_inputs()

    def _L0_attn_setup():
        import jax, jax.numpy as jnp
        import numpy as np
        B_, L_, DM_, DS_, DC_, EXP_ = (2, 512, 256, 16, 4, 2)
        DI_ = EXP_ * DM_
        key = jax.random.key(seed)
        ks = jax.random.split(key, 8)
        rn = lambda k, shape, s: jax.random.normal(k, shape, dtype=jnp.float32) * s
        return {'x': rn(ks[0], (B_, L_, DM_), 1.0), 'in_proj_w': rn(ks[1], (2 * DI_, DM_), 0.02), 'conv_w': rn(ks[2], (DI_, 1, DC_), 0.1), 'conv_b': jnp.zeros((DI_,), dtype=jnp.float32), 'x_proj_w': rn(ks[3], (2 * DS_ + 1, DI_), 0.02), 'dt_proj_w': rn(ks[4], (DI_, 1), 0.02), 'dt_proj_b': jnp.full((DI_,), -2.0, dtype=jnp.float32), 'A_log': rn(ks[5], (DI_, DS_), 1.0), 'D': jnp.ones((DI_,), dtype=jnp.float32), 'out_proj_w': rn(ks[6], (DM_, DI_), 0.02)}
    _L0_attn_all = _L0_attn_setup()
    _L0_attn_in = {k: v for k, v in _L0_attn_all.items() if k in ('in_proj_w', 'conv_w', 'conv_b', 'x_proj_w', 'dt_proj_w', 'dt_proj_b', 'A_log', 'D', 'out_proj_w')}
    del _L0_attn_all

    def _L0_xattn_setup():
        import jax, jax.numpy as jnp
        import numpy as np
        HEADS = 8
        DIM_HEAD = 64
        SCALE = DIM_HEAD ** (-0.5)
        key = jax.random.key(seed)
        ks = jax.random.split(key, 7)
        B, Nq, Nc = (4, 512, 512)
        Dq, Dc = (256, 192)
        inner = HEADS * DIM_HEAD
        x = jax.random.normal(ks[0], (B, Nq, Dq), dtype=jnp.float32)
        context = jax.random.normal(ks[1], (B, Nc, Dc), dtype=jnp.float32)
        Wq = jax.random.normal(ks[2], (Dq, inner), dtype=jnp.float32) * Dq ** (-0.5)
        Wk = jax.random.normal(ks[3], (Dc, inner), dtype=jnp.float32) * Dc ** (-0.5)
        Wv = jax.random.normal(ks[4], (Dc, inner), dtype=jnp.float32) * Dc ** (-0.5)
        Wo = jax.random.normal(ks[5], (inner, Dq), dtype=jnp.float32) * inner ** (-0.5)
        bo = jax.random.normal(ks[6], (Dq,), dtype=jnp.float32) * 0.01
        return {'x': x, 'context': context, 'Wq': Wq, 'Wk': Wk, 'Wv': Wv, 'Wo': Wo, 'bo': bo}
    _L0_xattn_all = _L0_xattn_setup()
    _L0_xattn_in = {k: v for k, v in _L0_xattn_all.items() if k in ('Wq', 'Wk', 'Wv', 'Wo', 'bo')}
    del _L0_xattn_all

    def _L0_ffn_setup():
        import jax, jax.numpy as jnp
        import numpy as np
        CAPACITY_FACTOR = 1.25
        key = jax.random.key(seed)
        k1, k2, k3, k4 = jax.random.split(key, 4)
        B, S, D, E, H = (2, 512, 256, 16, 1024)
        inputs = jax.random.normal(k1, (B, S, D), dtype=jnp.float32)
        gate_w = jax.random.normal(k2, (E, D), dtype=jnp.float32) / np.float32(np.sqrt(D))
        w1 = jax.random.normal(k3, (E, D, H), dtype=jnp.float32) / np.float32(np.sqrt(D))
        w2 = jax.random.normal(k4, (E, H, D), dtype=jnp.float32) / np.float32(np.sqrt(H))
        return {'inputs': inputs, 'gate_w': gate_w, 'w1': w1, 'w2': w2}
    _L0_ffn_all = _L0_ffn_setup()
    _L0_ffn_in = {k: v for k, v in _L0_ffn_all.items() if k in ('gate_w', 'w1', 'w2')}
    del _L0_ffn_all

    def _L1_attn_setup():
        import jax, jax.numpy as jnp
        import numpy as np
        B, S, D, H, MLP = (2, 512, 256, 16, 1024)
        DH = D // H
        EPS_LN = 1e-06
        KERNEL_EPS = 0.001

        def layer_norm(x, scale, bias):
            m = jnp.mean(x, axis=-1, keepdims=True)
            v = jnp.mean(jnp.square(x - m), axis=-1, keepdims=True)
            return (x - m) * jax.lax.rsqrt(v + EPS_LN) * scale + bias

        def performer_causal_attention(q, k, v):
            phi_q = jax.nn.relu(q) + KERNEL_EPS
            phi_k = jax.nn.relu(k) + KERNEL_EPS
            kv = jnp.cumsum(jnp.einsum('bshm,bshd->bshmd', phi_k, v), axis=1)
            num = jnp.einsum('bshm,bshmd->bshd', phi_q, kv)
            den = jnp.einsum('bshm,bshm->bsh', phi_q, jnp.cumsum(phi_k, axis=1))
            return num / den[..., None]
        key = jax.random.key(seed)
        ks = jax.random.split(key, 7)

        def w(k, shape, scale):
            return jax.random.normal(k, shape, jnp.float32) * scale
        s_in = 1.0 / np.sqrt(D)
        return {'inputs': jax.random.normal(ks[0], (B, S, D), jnp.float32), 'ln1_scale': jnp.ones((D,), jnp.float32), 'ln1_bias': jnp.zeros((D,), jnp.float32), 'wq': w(ks[1], (D, H, DH), s_in), 'wk': w(ks[2], (D, H, DH), s_in), 'wv': w(ks[3], (D, H, DH), s_in), 'wo': w(ks[4], (H, DH, D), s_in), 'ln2_scale': jnp.ones((D,), jnp.float32), 'ln2_bias': jnp.zeros((D,), jnp.float32), 'w1': w(ks[5], (D, MLP), s_in), 'b1': jnp.zeros((MLP,), jnp.float32), 'w2': w(ks[6], (MLP, D), 1.0 / np.sqrt(MLP)), 'b2': jnp.zeros((D,), jnp.float32)}
    _L1_attn_all = _L1_attn_setup()
    _L1_attn_in = {k: v for k, v in _L1_attn_all.items() if k in ('ln1_scale', 'ln1_bias', 'wq', 'wk', 'wv', 'wo', 'ln2_scale', 'ln2_bias', 'w1', 'b1', 'w2', 'b2')}
    del _L1_attn_all

    def _L1_xattn_setup():
        import jax, jax.numpy as jnp
        import numpy as np
        B, T, DT, G, DV = (16, 128, 256, 144, 192)
        H, DH = (4, 32)
        INNER = H * DH
        HID = 4 * DT
        N_STATE = 64
        K_TOP = 32

        def layernorm(x, g, b, eps=1e-05):
            m = x.mean(-1, keepdims=True)
            v = x.var(-1, keepdims=True)
            return (x - m) * jax.lax.rsqrt(v + eps) * g + b

        def s4d(x, log_dt, A_re, A_im, C_re, C_im, D_skip):
            Bb, L, D = x.shape
            dt = jnp.exp(log_dt)
            A = A_re + 1j * A_im
            C = C_re + 1j * C_im
            dtA = dt[:, None] * A
            dC = C * (jnp.exp(dtA) - 1.0) / A
            powers = jnp.exp(dtA[:, :, None] * jnp.arange(L))
            K = 2.0 * jnp.einsum('dn,dnl->dl', dC, powers).real
            n = 2 * L
            Kf = jnp.fft.rfft(K, n=n, axis=-1)
            xf = jnp.fft.rfft(x, n=n, axis=1)
            y = jnp.fft.irfft(xf * Kf.T[None], n=n, axis=1)[:, :L]
            return y + x * D_skip
        key = jax.random.key(seed)
        ks = jax.random.split(key, 16)
        s = 0.02
        inp = {'x_text': jax.random.normal(ks[0], (B, T, DT), jnp.float32), 'x_vision': jax.random.normal(ks[1], (B, G, DV), jnp.float32), 'text_mask': jnp.ones((B, T), bool), 'vision_mask': jnp.ones((B, G), bool), 'Wq': jax.random.normal(ks[2], (DT, INNER), jnp.float32) * s, 'Wk': jax.random.normal(ks[3], (DV, INNER), jnp.float32) * s, 'Wv': jax.random.normal(ks[4], (DV, DT), jnp.float32) * s, 'W_film_in': jax.random.normal(ks[5], (DT, 2 * DT), jnp.float32) * s, 'b_film_in': jnp.zeros((2 * DT,), jnp.float32), 'W_film_out': jax.random.normal(ks[6], (DT, 2 * DT), jnp.float32) * s, 'b_film_out': jnp.zeros((2 * DT,), jnp.float32), 'g_norm_in': jnp.ones((DT,), jnp.float32), 'b_norm_in': jnp.zeros((DT,), jnp.float32), 'g_norm_out': jnp.ones((DT,), jnp.float32), 'b_norm_out': jnp.zeros((DT,), jnp.float32), 'g_ffn': jnp.ones((DT,), jnp.float32), 'b_ffn': jnp.zeros((DT,), jnp.float32), 'W1': jax.random.normal(ks[7], (DT, HID), jnp.float32) * s, 'b1': jnp.zeros((HID,), jnp.float32), 'W2': jax.random.normal(ks[8], (HID, DT), jnp.float32) * s, 'b2': jnp.zeros((DT,), jnp.float32), 'log_dt': jnp.log(0.001) + jax.random.uniform(ks[9], (DT,), jnp.float32) * (jnp.log(0.1) - jnp.log(0.001)), 'A_re': -0.5 * jnp.ones((DT, N_STATE), jnp.float32), 'A_im': jnp.tile(jnp.pi * jnp.arange(N_STATE, dtype=jnp.float32), (DT, 1)), 'C_re': jax.random.normal(ks[10], (DT, N_STATE), jnp.float32) * 0.5 ** 0.5, 'C_im': jax.random.normal(ks[11], (DT, N_STATE), jnp.float32) * 0.5 ** 0.5, 'D_skip': jax.random.normal(ks[12], (DT,), jnp.float32), 'mod_gate': jnp.array(0.5, jnp.float32)}
        return inp
    _L1_xattn_all = _L1_xattn_setup()
    _L1_xattn_in = {k: v for k, v in _L1_xattn_all.items() if k in ('Wq', 'Wk', 'Wv', 'W_film_in', 'b_film_in', 'W_film_out', 'b_film_out', 'g_norm_in', 'b_norm_in', 'g_norm_out', 'b_norm_out', 'g_ffn', 'b_ffn', 'W1', 'b1', 'W2', 'b2', 'log_dt', 'A_re', 'A_im', 'C_re', 'C_im', 'D_skip', 'mod_gate')}
    del _L1_xattn_all

    def _L1_ffn_setup():
        import jax, jax.numpy as jnp
        import numpy as np
        H = 8
        KD = 128
        TOPK = 8
        NUM_KEYS = 64
        N_EXPERTS = NUM_KEYS * NUM_KEYS
        N_DIM = 256
        BN_EPS = 1e-05

        def gelu_new(x):
            c = jnp.sqrt(jnp.asarray(2.0 / jnp.pi, x.dtype))
            return 0.5 * x * (1.0 + jnp.tanh(c * (x + 0.044715 * x * x * x)))
        key = jax.random.key(seed)
        ks = jax.random.split(key, 5)
        b, s = (2, 256)
        x = jax.random.normal(ks[0], (b, s, N_DIM), dtype=jnp.float32)
        w_q = jax.random.normal(ks[1], (N_DIM, 2 * H * KD), dtype=jnp.float32) * 0.02
        bn_gamma = jnp.ones((2 * H * KD,), dtype=jnp.float32)
        bn_beta = jnp.zeros((2 * H * KD,), dtype=jnp.float32)
        keys = jax.random.normal(ks[2], (H, NUM_KEYS, 2, KD), dtype=jnp.float32) * 0.02
        down_embed = jax.random.normal(ks[3], (N_EXPERTS, N_DIM), dtype=jnp.float32) * 0.02
        up_embed = jax.random.normal(ks[4], (N_EXPERTS, N_DIM), dtype=jnp.float32) * 0.02
        return {'x': x, 'w_q': w_q, 'bn_gamma': bn_gamma, 'bn_beta': bn_beta, 'keys': keys, 'down_embed': down_embed, 'up_embed': up_embed}
    _L1_ffn_all = _L1_ffn_setup()
    _L1_ffn_in = {k: v for k, v in _L1_ffn_all.items() if k in ('w_q', 'bn_gamma', 'bn_beta', 'keys', 'down_embed', 'up_embed')}
    del _L1_ffn_all
    return {'x': x, 'ctx_768': ctx_768, 'mask_BxS_bf1': mask_BxS_bf1, 'mask_BxS2_bf1': mask_BxS2_bf1, 'L0_attn_in_proj_w': _L0_attn_in['in_proj_w'], 'L0_attn_conv_w': _L0_attn_in['conv_w'], 'L0_attn_conv_b': _L0_attn_in['conv_b'], 'L0_attn_x_proj_w': _L0_attn_in['x_proj_w'], 'L0_attn_dt_proj_w': _L0_attn_in['dt_proj_w'], 'L0_attn_dt_proj_b': _L0_attn_in['dt_proj_b'], 'L0_attn_A_log': _L0_attn_in['A_log'], 'L0_attn_D': _L0_attn_in['D'], 'L0_attn_out_proj_w': _L0_attn_in['out_proj_w'], 'L0_xattn_Wq': _L0_xattn_in['Wq'], 'L0_xattn_Wk': _L0_xattn_in['Wk'], 'L0_xattn_Wv': _L0_xattn_in['Wv'], 'L0_xattn_Wo': _L0_xattn_in['Wo'], 'L0_xattn_bo': _L0_xattn_in['bo'], 'L0_ffn_gate_w': _L0_ffn_in['gate_w'], 'L0_ffn_w1': _L0_ffn_in['w1'], 'L0_ffn_w2': _L0_ffn_in['w2'], 'L1_attn_ln1_scale': _L1_attn_in['ln1_scale'], 'L1_attn_ln1_bias': _L1_attn_in['ln1_bias'], 'L1_attn_wq': _L1_attn_in['wq'], 'L1_attn_wk': _L1_attn_in['wk'], 'L1_attn_wv': _L1_attn_in['wv'], 'L1_attn_wo': _L1_attn_in['wo'], 'L1_attn_ln2_scale': _L1_attn_in['ln2_scale'], 'L1_attn_ln2_bias': _L1_attn_in['ln2_bias'], 'L1_attn_w1': _L1_attn_in['w1'], 'L1_attn_b1': _L1_attn_in['b1'], 'L1_attn_w2': _L1_attn_in['w2'], 'L1_attn_b2': _L1_attn_in['b2'], 'L1_xattn_Wq': _L1_xattn_in['Wq'], 'L1_xattn_Wk': _L1_xattn_in['Wk'], 'L1_xattn_Wv': _L1_xattn_in['Wv'], 'L1_xattn_W_film_in': _L1_xattn_in['W_film_in'], 'L1_xattn_b_film_in': _L1_xattn_in['b_film_in'], 'L1_xattn_W_film_out': _L1_xattn_in['W_film_out'], 'L1_xattn_b_film_out': _L1_xattn_in['b_film_out'], 'L1_xattn_g_norm_in': _L1_xattn_in['g_norm_in'], 'L1_xattn_b_norm_in': _L1_xattn_in['b_norm_in'], 'L1_xattn_g_norm_out': _L1_xattn_in['g_norm_out'], 'L1_xattn_b_norm_out': _L1_xattn_in['b_norm_out'], 'L1_xattn_g_ffn': _L1_xattn_in['g_ffn'], 'L1_xattn_b_ffn': _L1_xattn_in['b_ffn'], 'L1_xattn_W1': _L1_xattn_in['W1'], 'L1_xattn_b1': _L1_xattn_in['b1'], 'L1_xattn_W2': _L1_xattn_in['W2'], 'L1_xattn_b2': _L1_xattn_in['b2'], 'L1_xattn_log_dt': _L1_xattn_in['log_dt'], 'L1_xattn_A_re': _L1_xattn_in['A_re'], 'L1_xattn_A_im': _L1_xattn_in['A_im'], 'L1_xattn_C_re': _L1_xattn_in['C_re'], 'L1_xattn_C_im': _L1_xattn_in['C_im'], 'L1_xattn_D_skip': _L1_xattn_in['D_skip'], 'L1_xattn_mod_gate': _L1_xattn_in['mod_gate'], 'L1_ffn_w_q': _L1_ffn_in['w_q'], 'L1_ffn_bn_gamma': _L1_ffn_in['bn_gamma'], 'L1_ffn_bn_beta': _L1_ffn_in['bn_beta'], 'L1_ffn_keys': _L1_ffn_in['keys'], 'L1_ffn_down_embed': _L1_ffn_in['down_embed'], 'L1_ffn_up_embed': _L1_ffn_in['up_embed']}

def reference(x, ctx_768, mask_BxS_bf1, mask_BxS2_bf1, L0_attn_in_proj_w, L0_attn_conv_w, L0_attn_conv_b, L0_attn_x_proj_w, L0_attn_dt_proj_w, L0_attn_dt_proj_b, L0_attn_A_log, L0_attn_D, L0_attn_out_proj_w, L0_xattn_Wq, L0_xattn_Wk, L0_xattn_Wv, L0_xattn_Wo, L0_xattn_bo, L0_ffn_gate_w, L0_ffn_w1, L0_ffn_w2, L1_attn_ln1_scale, L1_attn_ln1_bias, L1_attn_wq, L1_attn_wk, L1_attn_wv, L1_attn_wo, L1_attn_ln2_scale, L1_attn_ln2_bias, L1_attn_w1, L1_attn_b1, L1_attn_w2, L1_attn_b2, L1_xattn_Wq, L1_xattn_Wk, L1_xattn_Wv, L1_xattn_W_film_in, L1_xattn_b_film_in, L1_xattn_W_film_out, L1_xattn_b_film_out, L1_xattn_g_norm_in, L1_xattn_b_norm_in, L1_xattn_g_norm_out, L1_xattn_b_norm_out, L1_xattn_g_ffn, L1_xattn_b_ffn, L1_xattn_W1, L1_xattn_b1, L1_xattn_W2, L1_xattn_b2, L1_xattn_log_dt, L1_xattn_A_re, L1_xattn_A_im, L1_xattn_C_re, L1_xattn_C_im, L1_xattn_D_skip, L1_xattn_mod_gate, L1_ffn_w_q, L1_ffn_bn_gamma, L1_ffn_bn_beta, L1_ffn_keys, L1_ffn_down_embed, L1_ffn_up_embed):
    import jax
    import jax.numpy as jnp

    def _L0_attn_ref(x, in_proj_w, conv_w, conv_b, x_proj_w, dt_proj_w, dt_proj_b, A_log, D, out_proj_w):
        import jax, jax.numpy as jnp
        import numpy as np
        B_, L_, DM_, DS_, DC_, EXP_ = (2, 512, 256, 16, 4, 2)
        DI_ = EXP_ * DM_
        b, l, dm = x.shape
        di, ds = A_log.shape
        dc = conv_w.shape[-1]
        xz = x @ in_proj_w.T
        u, z = (xz[..., :di], xz[..., di:])
        uc = jnp.transpose(u, (0, 2, 1))
        uc = jax.lax.conv_general_dilated(uc, conv_w, window_strides=(1,), padding=[(dc - 1, 0)], feature_group_count=di, dimension_numbers=('NCH', 'OIH', 'NCH'))
        uc = uc + conv_b[None, :, None]
        u = jnp.transpose(uc, (0, 2, 1)) * jax.nn.silu(z)
        proj = u @ x_proj_w.T
        delta = proj[..., :1]
        Bm = proj[..., 1:1 + ds]
        Cm = proj[..., 1 + ds:]
        delta = jax.nn.softplus(delta @ dt_proj_w.T + dt_proj_b)
        A = -jnp.exp(A_log)

        def step(h, inp):
            ut, dt, Bt, Ct = inp
            dte = jnp.exp(dt)
            A_bar = jnp.exp(A[None] * dte[..., None])
            h = A_bar * h + Bt[:, None, :] * dte[..., None] * ut[..., None]
            yt = jnp.einsum('bis,bs->bi', h, Ct) + D * ut
            return (h, yt)
        h0 = jnp.zeros((b, di, ds), dtype=x.dtype)
        xs = (jnp.transpose(u, (1, 0, 2)), jnp.transpose(delta, (1, 0, 2)), jnp.transpose(Bm, (1, 0, 2)), jnp.transpose(Cm, (1, 0, 2)))
        _, ys = jax.lax.scan(step, h0, xs)
        y = jnp.transpose(ys, (1, 0, 2))
        return y @ out_proj_w.T

    def _L0_xattn_ref(x, context, Wq, Wk, Wv, Wo, bo):
        import jax, jax.numpy as jnp
        import numpy as np
        HEADS = 8
        DIM_HEAD = 64
        SCALE = DIM_HEAD ** (-0.5)
        B, Nq, _ = x.shape
        q = (x @ Wq).reshape(B, Nq, HEADS, DIM_HEAD)
        k = (context @ Wk).reshape(B, context.shape[1], HEADS, DIM_HEAD)
        v = (context @ Wv).reshape(B, context.shape[1], HEADS, DIM_HEAD)
        sim = jnp.einsum('bihd,bjhd->bhij', q, k) * SCALE
        attn = jax.nn.softmax(sim, axis=-1)
        out = jnp.einsum('bhij,bjhd->bihd', attn, v)
        out = out.reshape(B, Nq, HEADS * DIM_HEAD)
        return out @ Wo + bo

    def _L0_ffn_ref(inputs, gate_w, w1, w2):
        import jax, jax.numpy as jnp
        import numpy as np
        CAPACITY_FACTOR = 1.25
        orig_shape = inputs.shape
        D = orig_shape[-1]
        tokens = inputs.reshape(-1, D)
        T = tokens.shape[0]
        E = gate_w.shape[0]
        C = int(CAPACITY_FACTOR * T / E)
        logits = tokens @ gate_w.T
        probs = jax.nn.softmax(logits, axis=-1)
        expert_idx = jnp.argmax(probs, axis=-1)
        mask = jax.nn.one_hot(expert_idx, E, dtype=jnp.int32)
        locations = jnp.cumsum(mask, axis=0) - 1
        mask = mask * (locations < C)
        loc_oh = jax.nn.one_hot(locations, C, dtype=probs.dtype)
        sec_mask = mask[:, :, None].astype(probs.dtype) * loc_oh
        combine_weights = probs[:, :, None] * sec_mask
        dispatch = jnp.einsum('tec,td->ecd', sec_mask, tokens)
        h = jax.nn.relu(jnp.einsum('ecd,edh->ech', dispatch, w1))
        expert_out = jnp.einsum('ech,ehd->ecd', h, w2)
        ans = jnp.einsum('tec,ecd->td', combine_weights, expert_out)
        return ans.reshape(orig_shape)

    def _L1_attn_ref(inputs, ln1_scale, ln1_bias, wq, wk, wv, wo, ln2_scale, ln2_bias, w1, b1, w2, b2):
        import jax, jax.numpy as jnp
        import numpy as np
        B, S, D, H, MLP = (2, 512, 256, 16, 1024)
        DH = D // H
        EPS_LN = 1e-06
        KERNEL_EPS = 0.001

        def layer_norm(x, scale, bias):
            m = jnp.mean(x, axis=-1, keepdims=True)
            v = jnp.mean(jnp.square(x - m), axis=-1, keepdims=True)
            return (x - m) * jax.lax.rsqrt(v + EPS_LN) * scale + bias

        def performer_causal_attention(q, k, v):
            phi_q = jax.nn.relu(q) + KERNEL_EPS
            phi_k = jax.nn.relu(k) + KERNEL_EPS
            kv = jnp.cumsum(jnp.einsum('bshm,bshd->bshmd', phi_k, v), axis=1)
            num = jnp.einsum('bshm,bshmd->bshd', phi_q, kv)
            den = jnp.einsum('bshm,bshm->bsh', phi_q, jnp.cumsum(phi_k, axis=1))
            return num / den[..., None]
        x = layer_norm(inputs, ln1_scale, ln1_bias)
        q = jnp.einsum('bsd,dhm->bshm', x, wq)
        k = jnp.einsum('bsd,dhm->bshm', x, wk)
        v = jnp.einsum('bsd,dhm->bshm', x, wv)
        attn = performer_causal_attention(q, k, v)
        attn_out = jnp.einsum('bshm,hmd->bsd', attn, wo)
        x = attn_out + inputs
        y = layer_norm(x, ln2_scale, ln2_bias)
        y = jax.nn.gelu(y @ w1 + b1) @ w2 + b2
        return x + y

    def _L1_xattn_ref(x_text, x_vision, text_mask, vision_mask, Wq, Wk, Wv, W_film_in, b_film_in, W_film_out, b_film_out, g_norm_in, b_norm_in, g_norm_out, b_norm_out, g_ffn, b_ffn, W1, b1, W2, b2, log_dt, A_re, A_im, C_re, C_im, D_skip, mod_gate):
        import jax, jax.numpy as jnp
        import numpy as np
        B, T, DT, G, DV = (16, 128, 256, 144, 192)
        H, DH = (4, 32)
        INNER = H * DH
        HID = 4 * DT
        N_STATE = 64
        K_TOP = 32

        def layernorm(x, g, b, eps=1e-05):
            m = x.mean(-1, keepdims=True)
            v = x.var(-1, keepdims=True)
            return (x - m) * jax.lax.rsqrt(v + eps) * g + b

        def s4d(x, log_dt, A_re, A_im, C_re, C_im, D_skip):
            Bb, L, D = x.shape
            dt = jnp.exp(log_dt)
            A = A_re + 1j * A_im
            C = C_re + 1j * C_im
            dtA = dt[:, None] * A
            dC = C * (jnp.exp(dtA) - 1.0) / A
            powers = jnp.exp(dtA[:, :, None] * jnp.arange(L))
            K = 2.0 * jnp.einsum('dn,dnl->dl', dC, powers).real
            n = 2 * L
            Kf = jnp.fft.rfft(K, n=n, axis=-1)
            xf = jnp.fft.rfft(x, n=n, axis=1)
            y = jnp.fft.irfft(xf * Kf.T[None], n=n, axis=1)[:, :L]
            return y + x * D_skip
        Bb, Tt, D = x_text.shape
        Gg = x_vision.shape[1]
        Q = (x_text @ Wq).reshape(Bb, Tt, H, DH)
        K = (x_vision @ Wk).reshape(Bb, Gg, H, DH)
        scores = jnp.einsum('bthd,bghd->bhtg', Q, K) / np.sqrt(DH).astype(np.float32)
        scores = jnp.where(vision_mask[:, None, None, :], scores, -jnp.inf)
        topv, topi = jax.lax.top_k(scores, K_TOP)
        probs = jax.nn.softmax(topv, axis=-1)
        bi = jnp.arange(Bb)[:, None, None, None]
        hi = jnp.arange(H)[None, :, None, None]
        ti = jnp.arange(Tt)[None, None, :, None]
        attn = jnp.zeros_like(scores).at[bi, hi, ti, topi].set(probs)
        attn_mean = attn.mean(axis=1)
        V = x_vision @ Wv
        c_t = jnp.einsum('btg,bgd->btd', attn_mean, V)
        c_t = c_t * text_mask[..., None]
        x = layernorm(x_text, g_norm_in, b_norm_in)
        scale_in, shift_in = jnp.split(c_t @ W_film_in + b_film_in, 2, axis=-1)
        x = x * (1.0 + mod_gate * scale_in) + mod_gate * shift_in
        y = s4d(x, log_dt, A_re, A_im, C_re, C_im, D_skip)
        scale_out, shift_out = jnp.split(c_t @ W_film_out + b_film_out, 2, axis=-1)
        y = y * (1.0 + mod_gate * scale_out) + mod_gate * shift_out
        xt = x_text + y
        h = layernorm(xt, g_ffn, b_ffn)
        h = jax.nn.gelu(h @ W1 + b1, approximate=False) @ W2 + b2
        xt = xt + h
        return layernorm(xt, g_norm_out, b_norm_out)

    def _L1_ffn_ref(x, w_q, bn_gamma, bn_beta, keys, down_embed, up_embed):
        import jax, jax.numpy as jnp
        import numpy as np
        H = 8
        KD = 128
        TOPK = 8
        NUM_KEYS = 64
        N_EXPERTS = NUM_KEYS * NUM_KEYS
        N_DIM = 256
        BN_EPS = 1e-05

        def gelu_new(x):
            c = jnp.sqrt(jnp.asarray(2.0 / jnp.pi, x.dtype))
            return 0.5 * x * (1.0 + jnp.tanh(c * (x + 0.044715 * x * x * x)))
        b, n, d = x.shape
        q = jnp.einsum('bnd,de->bne', x, w_q)
        mean = jnp.mean(q, axis=(0, 1))
        var = jnp.var(q, axis=(0, 1))
        q = (q - mean) * jax.lax.rsqrt(var + BN_EPS) * bn_gamma + bn_beta
        q = q.reshape(b, n, 2, H, KD).transpose(2, 0, 1, 3, 4)
        sim = jnp.einsum('pbnhd,hkpd->pbnhk', q, keys)
        sx, ix = jax.lax.top_k(sim[0], TOPK)
        sy, iy = jax.lax.top_k(sim[1], TOPK)
        all_scores = (sx[..., :, None] + sy[..., None, :]).reshape(b, n, H, TOPK * TOPK)
        all_indices = (ix[..., :, None] * NUM_KEYS + iy[..., None, :]).reshape(b, n, H, TOPK * TOPK)
        scores, pk = jax.lax.top_k(all_scores, TOPK)
        indices = jnp.take_along_axis(all_indices, pk, axis=-1)
        wd = down_embed[indices]
        wu = up_embed[indices]
        h = jnp.einsum('bnd,bnhkd->bnhk', x, wd)
        h = gelu_new(h)
        h = jax.nn.softmax(scores, axis=-1) * h
        out = jnp.einsum('bnhk,bnhkd->bnd', h, wu)
        return out
    x = _layernorm(x + _L0_attn_ref(x, L0_attn_in_proj_w, L0_attn_conv_w, L0_attn_conv_b, L0_attn_x_proj_w, L0_attn_dt_proj_w, L0_attn_dt_proj_b, L0_attn_A_log, L0_attn_D, L0_attn_out_proj_w), axis=-1)
    x = _layernorm(x + _L0_xattn_ref(x, ctx_768, L0_xattn_Wq, L0_xattn_Wk, L0_xattn_Wv, L0_xattn_Wo, L0_xattn_bo), axis=-1)
    x = _layernorm(x + _L0_ffn_ref(x, L0_ffn_gate_w, L0_ffn_w1, L0_ffn_w2), axis=-1)
    x = _layernorm(x + _L1_attn_ref(x, L1_attn_ln1_scale, L1_attn_ln1_bias, L1_attn_wq, L1_attn_wk, L1_attn_wv, L1_attn_wo, L1_attn_ln2_scale, L1_attn_ln2_bias, L1_attn_w1, L1_attn_b1, L1_attn_w2, L1_attn_b2), axis=-1)
    x = _layernorm(x + _L1_xattn_ref(x, ctx_768, mask_BxS_bf1, mask_BxS2_bf1, L1_xattn_Wq, L1_xattn_Wk, L1_xattn_Wv, L1_xattn_W_film_in, L1_xattn_b_film_in, L1_xattn_W_film_out, L1_xattn_b_film_out, L1_xattn_g_norm_in, L1_xattn_b_norm_in, L1_xattn_g_norm_out, L1_xattn_b_norm_out, L1_xattn_g_ffn, L1_xattn_b_ffn, L1_xattn_W1, L1_xattn_b1, L1_xattn_W2, L1_xattn_b2, L1_xattn_log_dt, L1_xattn_A_re, L1_xattn_A_im, L1_xattn_C_re, L1_xattn_C_im, L1_xattn_D_skip, L1_xattn_mod_gate), axis=-1)
    x = _layernorm(x + _L1_ffn_ref(x, L1_ffn_w_q, L1_ffn_bn_gamma, L1_ffn_bn_beta, L1_ffn_keys, L1_ffn_down_embed, L1_ffn_up_embed), axis=-1)
    return x

_drawn_inputs = setup_inputs


def setup_inputs(seed=0):
    import zlib

    import numpy as np

    out = dict(_drawn_inputs(seed))
    spreads = {'L0_attn_conv_b': (0.0, 0.364),
     'L0_attn_dt_proj_b': (-2.0, 0.6),
     'L0_attn_D': (1.0, 0.6),
     'L1_attn_ln1_scale': (1.0, 0.2),
     'L1_attn_ln1_bias': (0.0, 0.1),
     'L1_attn_ln2_scale': (1.0, 0.2),
     'L1_attn_ln2_bias': (0.0, 0.1),
     'L1_attn_b1': (0.0, 0.1),
     'L1_attn_b2': (0.0, 0.1),
     'L1_xattn_b_film_in': (0.0, 0.1),
     'L1_xattn_b_film_out': (0.0, 0.291),
     'L1_xattn_g_norm_in': (1.0, 0.2),
     'L1_xattn_b_norm_in': (0.0, 0.1),
     'L1_xattn_g_norm_out': (1.0, 0.2),
     'L1_xattn_b_norm_out': (0.0, 0.1),
     'L1_xattn_g_ffn': (1.0, 0.6),
     'L1_xattn_b_ffn': (0.0, 0.8),
     'L1_xattn_b1': (0.0, 0.757),
     'L1_xattn_b2': (0.0, 0.1),
     'L1_xattn_A_re': (-0.5, 0.2),
     'L1_ffn_bn_gamma': (1.0, 0.6),
     'L1_ffn_bn_beta': (0.0, 0.8)}
    factors = {'L0_attn_in_proj_w': 3.209,
     'L0_attn_conv_w': 4.016,
     'L0_attn_x_proj_w': 8.0,
     'L0_attn_dt_proj_w': 8.0,
     'L0_attn_A_log': 8.0,
     'L0_attn_out_proj_w': 2.973,
     'L1_xattn_Wq': 7.983,
     'L1_xattn_Wk': 7.96,
     'L1_xattn_Wv': 2.731,
     'L1_xattn_W_film_in': 3.433,
     'L1_xattn_W_film_out': 4.38,
     'L1_ffn_w_q': 8.0,
     'L1_ffn_keys': 8.0,
     'L1_ffn_down_embed': 8.0,
     'L1_ffn_up_embed': 8.0}
    for name, (base, spread) in spreads.items():
        noise = np.random.default_rng([zlib.crc32(name.encode()), seed]).standard_normal(out[name].shape)
        drawn = base * np.exp(spread * noise) if base else spread * noise
        out[name] = jnp.asarray(drawn.astype(out[name].dtype))
    for name, factor in factors.items():
        out[name] = (out[name] * factor).astype(out[name].dtype)
    return out
```

```python
from contextlib import ExitStack, contextmanager

import numpy as np

import concourse.bass as bass
from concourse import mybir

P = 128
B, S, D = 8, 256, 256
T = B * S
NT = T // P
KD = D // P
G4 = 512

F32 = mybir.dt.float32
BF16 = mybir.dt.bfloat16
I32 = mybir.dt.int32
U32 = mybir.dt.uint32
U8 = mybir.dt.uint8
ALU = mybir.AluOpType
ACT = mybir.ActivationFunctionType
AX_X = mybir.AxisListType.X
LN_EPS = 1e-5


class Chain:

    def __init__(self, eng, sem):
        self.eng, self.sem, self.n, self.base = eng, sem, 0, 0

    def link(self, ins):
        self.n += 1
        ins.then_inc(self.sem, 1)
        self.eng.wait_ge(self.sem, self.base + self.n)

    @contextmanager
    def loop(self, count, per):
        n0 = self.n
        with self.eng.Fori(0, count) as i:
            self.base, self.n = i * per + n0, 0
            yield i
            assert self.n == per, f"{self.n} links in a turn"
        self.base, self.n = 0, n0 + count * per


class Stage:

    semaphores = []

    def __init__(self, nc, name):
        self.nc, self.name, self.ctx, self.dmas = nc, name, ExitStack(), 0

    def __enter__(self):
        self.ctx.__enter__()
        return self

    def __exit__(self, *e):
        return self.ctx.__exit__(*e)

    def sb(self, name, shape, dt=F32):
        return self.ctx.enter_context(self.nc.sbuf_tensor(f"{self.name}_{name}", shape, dt))

    def ps(self, name, shape, dt=F32):
        return self.ctx.enter_context(self.nc.psum_tensor(f"{self.name}_{name}", shape, dt))

    def sem(self, name):
        self.semaphores.append(self.nc.alloc_semaphore(f"{self.name}_{name}"))
        return self.semaphores[-1]

    def block(self):
        return self.nc.Block(f"{self.name}_block")


def norm_stats(v, chain, x, raw, mean_var):
    chain.link(v.bn_stats(raw, x))
    return v.bn_aggr(mean_var, raw)


EPS5, EPS6 = P, P + 1
ONES = P + 2
NI = ONES + P


def stage_load(nc, io, X, XT, ident):
    with Stage(nc, "load") as st:
        loaded = st.sem("loaded")
        with st.block() as block:
            @block.sync
            def _(sp):
                sp.dma_start(X[:], io["x"].rearrange("b (h p) d -> p (b h) d", p=P)).then_inc(loaded, 16)
                sp.dma_start(XT[:], io["xT"].rearrange("(k p) t -> p k t", p=P)).then_inc(loaded, 16)
                sp.dma_start(ident[:], io["ident"]).then_inc(loaded, 16)
                sp.wait_ge(loaded, 48)


def stage_store(nc, out, X, stored):
    with Stage(nc, "store") as st:
        with st.block() as block:
            @block.sync
            def _(sp):
                sp.dma_start(out.rearrange("b (h p) d -> p (b h) d", p=P), X[:]).then_inc(stored, 16)
                sp.wait_ge(stored, 16)


def add_bias(pe, ident, out, row):
    return pe.matmul(out, ident[0:1, ONES:ONES + P], row, start=False, stop=True)


def products(nc, name, jobs, loads=(), dve_only=False):
    with Stage(nc, name) as st:
        BANKS = 8
        ring = st.ps("ring", [P, BANKS, 512])
        loaded = st.sem("loaded")
        product_ready = st.sem("product_ready")
        even_read = st.sem("even_read")
        odd_read = st.sem("odd_read")

        def bank(n, out):
            size = 1
            for d in out.shape[1:]:
                size *= d
            return ring[0:out.shape[0], n % BANKS, 0:size]

        def by_vector(n):
            return dve_only or n % 2 == 1

        with st.block() as block:
            @block.sync
            def _(sp):
                for dst, src in loads:
                    sp.dma_start(dst, src).then_inc(loaded, 16)

            @block.tensor
            def _(pe):
                if loads:
                    pe.wait_ge(loaded, 16 * len(loads))
                for n, (out, pairs, _) in enumerate(jobs):
                    m = n - BANKS
                    if m >= 0:
                        if dve_only:
                            pe.wait_ge(odd_read, m + 1)
                        else:
                            pe.wait_ge(odd_read if by_vector(m) else even_read, m // 2 + 1)
                    for i, (lhsT, rhs) in enumerate(pairs):
                        ins = pe.matmul(bank(n, out), lhsT, rhs, start=(i == 0), stop=(i == len(pairs) - 1))
                    ins.then_inc(product_ready, 1)

            @block.scalar
            def _(act):
                if loads:
                    act.wait_ge(loaded, 16 * len(loads))
                for n, (out, _, evacuate) in enumerate(jobs):
                    if not by_vector(n):
                        act.wait_ge(product_ready, n + 1)
                        evacuate(act, out, bank(n, out)).then_inc(even_read, 1)

            @block.vector
            def _(v):
                if loads:
                    v.wait_ge(loaded, 16 * len(loads))
                for n, (out, _, evacuate) in enumerate(jobs):
                    if by_vector(n):
                        v.wait_ge(product_ready, n + 1)
                        evacuate(v, out, bank(n, out)).then_inc(odd_read, 1)


def copy_out(eng, out, product):
    if len(out.shape) == 3:
        product = product.rearrange("p (a b) -> p a b", a=out.shape[1])
    if eng.engine == mybir.EngineType.Activation:
        return eng.activation(out, product, ACT.Copy)
    return eng.tensor_copy(out, product)


def finish_norm(nc, name, X, XT, ident, residual, total=None, base=None, out=None, also=None, eps=EPS5,
                scale=None, bias=None, loads=(), last=False):
    XT = None if last else XT
    total = total or (lambda t: X[:, t, :])
    base = base or (lambda t: X[:, t, :])
    out = out or (lambda t: X[:, t, :])
    RB, LAG = 4, 3
    with Stage(nc, name) as st:
        R = st.ps("R", [P, RB, 512])
        TP = st.ps("TP", [P, 2, 512])
        raw = st.sb("raw", [P, 6])
        MV = st.sb("MV", [P, NT, 2])
        RS = st.sb("RS", [P, NT])
        loaded = st.sem("loaded")
        stats_ready = st.sem("stats_ready")
        std_ready = st.sem("std_ready")
        residual_ready = st.sem("residual_ready")
        residual_read = st.sem("residual_read")
        normed = st.sem("normed")
        turned = st.sem("turned")
        turned_read = st.sem("turned_read")
        dve_chain = st.sem("dve_chain")
        with st.block() as block:
            @block.sync
            def _(sp):
                for dst, src in loads:
                    sp.dma_start(dst, src).then_inc(loaded, 16)

            @block.tensor
            def _(pe):
                if loads:
                    pe.wait_ge(loaded, 16 * len(loads))
                for t in range(NT + LAG):
                    if t < NT and residual:
                        if t >= RB:
                            pe.wait_ge(residual_read, t - RB + 1)
                        residual(pe, t, R[:, t % RB, 0:D]).then_inc(residual_ready, 1)
                    if t >= LAG and XT is not None:
                        u = t - LAG
                        pe.wait_ge(normed, u + 1)
                        if u >= 2:
                            pe.wait_ge(turned_read, u - 1)
                        for k in range(KD):
                            ins = pe.transpose(TP[:, u % 2, k * P:(k + 1) * P], out(u)[:, k * P:(k + 1) * P], ident[:, 0:P])
                        ins.then_inc(turned, 1)

            @block.vector
            def _(v):
                ch = Chain(v, dve_chain)
                for t in range(NT + 1):
                    if t < NT:
                        if residual:
                            v.wait_ge(residual_ready, t + 1)
                            v.tensor_tensor(total(t), R[:, t % RB, 0:D], base(t), ALU.add).then_inc(residual_read, 1)
                            v.wait_ge(residual_read, t + 1)
                        elif base(t) is not None:
                            ch.link(v.tensor_tensor(total(t), X[:, t, :], base(t), ALU.add))
                        if also:
                            ch.link(v.tensor_tensor(also(t), also(t), total(t), ALU.add))
                        norm_stats(v, ch, total(t), raw[:], MV[:, t, :]).then_inc(stats_ready, 1)
                        v.wait_ge(stats_ready, t + 1)
                    if t >= 1:
                        u = t - 1
                        v.wait_ge(std_ready, u + 1)
                        ch.link(v.reciprocal(RS[:, u:u + 1], RS[:, u:u + 1]))
                        v.tensor_scalar(out(u), total(u), MV[:, u, 0:1], RS[:, u:u + 1], ALU.subtract, ALU.mult).then_inc(normed, 1)

            @block.scalar
            def _(act):
                if loads:
                    act.wait_ge(loaded, 16 * len(loads))
                for t in range(NT + 2):
                    if t < NT:
                        act.wait_ge(stats_ready, t + 1)
                        act.activation(RS[:, t:t + 1], MV[:, t, 1:2], ACT.Sqrt, bias=ident[:, eps:eps + 1]).then_inc(std_ready, 1)
                    if t >= 2 and XT is not None:
                        u = t - 2
                        act.wait_ge(turned, u + 1)
                        if scale is None:
                            act.activation(XT[:, :, u * P:(u + 1) * P], TP[:, u % 2, 0:D].rearrange("p (k n) -> p k n", k=KD),
                                           ACT.Copy).then_inc(turned_read, 1)
                        else:
                            for k in range(KD):
                                ins = act.activation(XT[:, k, u * P:(u + 1) * P], TP[:, u % 2, k * P:(k + 1) * P],
                                                     ACT.Identity, scale=scale[:, k:k + 1], bias=bias[:, k:k + 1])
                            ins.then_inc(turned_read, 1)


DI, DS, DC = 512, 16, 4
NCH = DI // P
HALF = T // 2
NPASS = NCH * 2
BF16_ONE = 0x3F80


def stage_mamba(nc, io, X, XT, ident):
    with ExitStack() as outer:
        U = outer.enter_context(nc.sbuf_tensor("mamba_U", [P, NPASS, HALF], F32))
        WO = outer.enter_context(nc.sbuf_tensor("mamba_WO", [P, NCH, D], F32))
        with Stage(nc, "mamba") as st:
            DU = st.sb("DU", [P, NPASS, HALF])
            E = st.sb("E", [P, NPASS, HALF])
            BC = st.sb("BC", [96, T], BF16)
            WD = st.sb("WD", [P, NCH, P])
            WBC = st.sb("WBC", [P, NCH, 96])
            SEL = st.sb("SEL", [96, 2 * DS, P], BF16)
            CW = st.sb("CW", [P, NCH, DC])
            VEC = st.sb("VEC", [P, 4, NCH])
            AA = st.sb("AA", [P, NPASS, DS])
            DV = st.sb("DV", [P, NPASS])
            with Stage(nc, "mamba_in") as s2:
                W = s2.sb("W", [P, KD, 2 * DI])
                SIL = s2.sb("SIL", [P, 2, G4])
                CV = s2.sb("CV", [P, 2, G4])
                R1 = s2.sb("R1", [96, 2, G4])
                MID = s2.sb("MID", [96, G4], BF16)
                UP = s2.ps("UP", [P, 2, G4])
                ZP = s2.ps("ZP", [P, 2, G4])
                PP = s2.ps("PP", [P, G4])
                DP = s2.ps("DP", [P, G4])
                loaded = s2.sem("loaded")
                uz_ready = s2.sem("uz_ready")
                u_read = s2.sem("u_read")
                silu_ready = s2.sem("silu_ready")
                gated = s2.sem("gated")
                proj_ready = s2.sem("proj_ready")
                bc_read = s2.sem("bc_read")
                exp_ready = s2.sem("exp_ready")
                a_exp = s2.sem("a_exp")
                dve_chain = s2.sem("dve_chain")
                NG = T // G4

                def group(buf, c, g):
                    return buf[:, 2 * c + g // 2, (g % 2) * G4:(g % 2 + 1) * G4]

                with s2.block() as block:
                    @block.sync
                    def _(sp):
                        sp.dma_start(W[:], io["L0_attn_in_projT"].rearrange("(k p) n -> p k n", p=P)).then_inc(loaded, 16)
                        sp.dma_start(WO[:], io["L0_attn_out_projT"].rearrange("(k p) n -> p k n", p=P)).then_inc(loaded, 16)
                        sp.dma_start(WD[:], io["L0_attn_x_delta"].rearrange("(k p) n -> p k n", p=P)).then_inc(loaded, 16)
                        sp.dma_start(WBC[:], io["L0_attn_x_bc"].rearrange("(k p) n -> p k n", p=P)).then_inc(loaded, 16)
                        sp.dma_start(SEL[:].bitcast(mybir.dt.uint16), io["sel_bc"]).then_inc(loaded, 16)
                        sp.dma_start(CW[:], io["L0_attn_conv_w"].rearrange("(k p) o n -> p k (o n)", p=P)).then_inc(loaded, 16)
                        sp.dma_start(VEC[:], io["L0_attn_vec"]).then_inc(loaded, 16)
                        for h in range(2):
                            sp.dma_start(AA[:].rearrange("p (c h) s -> p h c s", h=2)[:, h],
                                         io["L0_attn_A_log"].rearrange("(k p) s -> p k s", p=P)).then_inc(loaded, 16)

                    NLOAD = 9 * 16

                    @block.tensor
                    def _(pe):
                        pe.wait_ge(loaded, NLOAD)
                        for g in range(NG):
                            for c in range(NCH):
                                n = g * NCH + c
                                if n >= 2:
                                    pe.wait_ge(u_read, n - 1)
                                    pe.wait_ge(silu_ready, n - 1)
                                for dst, col in ((UP, c * P), (ZP, DI + c * P)):
                                    for k in range(KD):
                                        ins = pe.matmul(dst[:, n % 2, :], W[:, k, col:col + P], XT[:, k, g * G4:(g + 1) * G4],
                                                        start=(k == 0), stop=(k == KD - 1))
                                ins.then_inc(uz_ready, 1)
                            pe.wait_ge(gated, (g + 1) * NCH)
                            if g:
                                pe.wait_ge(bc_read, g)
                                pe.wait_ge(exp_ready, g * NCH)
                            for dst, w, m in ((PP, WBC, 96), (DP, WD, P)):
                                for c in range(NCH):
                                    ins = pe.matmul(dst[0:m, :], w[:, c, :], group(U, c, g), start=(c == 0), stop=(c == NCH - 1))
                            ins.then_inc(proj_ready, 1)

                    @block.scalar
                    def _(act):
                        act.wait_ge(loaded, NLOAD)
                        act.activation(AA[:], AA[:], ACT.Exp).then_inc(a_exp, 1)
                        for g in range(NG):
                            for c in range(NCH):
                                n = g * NCH + c
                                act.wait_ge(uz_ready, n + 1)
                                if n >= 2:
                                    act.wait_ge(gated, n - 1)
                                act.activation(SIL[:, n % 2, :], ZP[:, n % 2, :], ACT.Silu).then_inc(silu_ready, 1)
                            act.wait_ge(proj_ready, g + 1)
                            for c in range(NCH):
                                act.activation(group(E, c, g), DP[:], ACT.Exp, scale=VEC[:, 1, c:c + 1],
                                               bias=VEC[:, 2, c:c + 1]).then_inc(exp_ready, 1)

                    @block.vector
                    def _(v):
                        ch = Chain(v, dve_chain)
                        v.wait_ge(loaded, NLOAD)
                        v.wait_ge(a_exp, 1)
                        ch.link(v.tensor_scalar(AA[:], AA[:], -1.0, -3e38, ALU.mult, ALU.max))
                        for h in range(2):
                            ch.link(v.tensor_copy(DV[:].rearrange("p (c h) -> p h c", h=2)[:, h], VEC[:, 3, :]))
                        for g in range(NG):
                            for c in range(NCH):
                                n = g * NCH + c
                                v.wait_ge(uz_ready, n + 1)
                                cv = CV[:, n % 2, :]
                                ch.link(v.tensor_scalar(cv, UP[:, n % 2, :], CW[:, c, DC - 1:DC], VEC[:, 0, c:c + 1], ALU.mult, ALU.add))
                                for s in range(1, DC):
                                    o = cv.rearrange("p (b t) -> p b t", t=S)[:, :, s:]
                                    i = UP[:, n % 2, :].rearrange("p (b t) -> p b t", t=S)[:, :, 0:S - s]
                                    ch.link(v.scalar_tensor_tensor(o, i, CW[:, c, DC - 1 - s:DC - s], o, ALU.mult, ALU.add))
                                v.sem_inc(u_read, 1)
                                v.wait_ge(silu_ready, n + 1)
                                v.tensor_tensor(group(U, c, g), cv, SIL[:, n % 2, :], ALU.mult).then_inc(gated, 1)
                            v.wait_ge(gated, (g + 1) * NCH)
                            v.wait_ge(proj_ready, g + 1)
                            bc = BC[:, g * G4:(g + 1) * G4]
                            ch.link(v.tensor_copy(bc, PP[0:96, :]))
                            ch.link(v.tensor_tensor(R1[:, 0, :], PP[0:96, :], bc, ALU.subtract))
                            v.sem_inc(bc_read, 1)
                            ch.link(v.tensor_copy(MID[:], R1[:, 0, :]))
                            ch.link(v.tensor_tensor(R1[:, 1, :], R1[:, 0, :], MID[:], ALU.subtract))
                            ch.link(v.tensor_copy(bc[32:64], MID[32:64, :]))
                            ch.link(v.tensor_copy(bc[64:96], R1[64:96, 1, :]))
                            for c in range(NCH):
                                v.wait_ge(exp_ready, g * NCH + c + 1)
                                ch.link(v.scalar_tensor_tensor(group(DU, c, g), group(E, c, g), 1.0, group(U, c, g), ALU.add, ALU.mult))

            with Stage(nc, "scan") as s3:
                AB = s3.sb("AB", [P, 2, HALF])
                BU = s3.sb("BU", [P, 2, HALF])
                H = s3.sb("H", [P, 3, HALF])
                CS = s3.sb("CS", [P, 3, HALF])
                HC = s3.sb("HC", [P, 2, HALF])
                YP = s3.ps("YP", [P, HALF])
                BP = s3.ps("BP", [P, 2, HALF])
                CP = s3.ps("CP", [P, HALF])
                zeroed = s3.sem("zeroed")
                b_ready = s3.sem("b_ready")
                c_ready = s3.sem("c_ready")
                decay_ready = s3.sem("decay_ready")
                c_copied = s3.sem("c_copied")
                bu_ready = s3.sem("bu_ready")
                h_ready = s3.sem("h_ready")
                hc_ready = s3.sem("hc_ready")
                y_added = s3.sem("y_added")
                y_read = s3.sem("y_read")
                NH = HALF // G4
                with s3.block() as block:
                    @block.gpsimd
                    def _(pool):
                        pool.memset(AB[:], 0.0).then_inc(zeroed, 1)
                        for i in range(NPASS):
                            for s in range(DS):
                                n = i * DS + s
                                pool.wait_ge(h_ready, n + 1)
                                pool.wait_ge(c_copied, n + 1)
                                if n >= 2:
                                    pool.wait_ge(y_added, n - 1)
                                pool.tensor_tensor(HC[:, n % 2, :], H[:, n % 3, :], CS[:, n % 3, :], ALU.mult).then_inc(hc_ready, 1)

                    @block.tensor
                    def _(pe):
                        def spread(n):
                            i, s = n // DS, n % DS
                            tok = (i % 2) * HALF
                            if n >= 2:
                                pe.wait_ge(bu_ready, n - 1)
                            for q in range(NH):
                                ins = pe.matmul(BP[:, n % 2, q * G4:(q + 1) * G4], SEL[:, s, :], BC[:, tok + q * G4:tok + (q + 1) * G4],
                                                start=True, stop=True)
                            ins.then_inc(b_ready, 1)
                            if n >= 1:
                                pe.wait_ge(c_copied, n)
                            for q in range(NH):
                                ins = pe.matmul(CP[:, q * G4:(q + 1) * G4], SEL[:, DS + s, :], BC[:, tok + q * G4:tok + (q + 1) * G4],
                                                start=True, stop=True)
                            ins.then_inc(c_ready, 1)

                        N = NPASS * DS
                        spread(0)
                        spread(1)
                        for n in range(N):
                            i, s = n // DS, n % DS
                            if n + 2 < N:
                                spread(n + 2)
                            pe.wait_ge(hc_ready, n + 1)
                            if i and s == 0:
                                pe.wait_ge(y_read, i)
                            for q in range(NH):
                                ins = pe.matmul(YP[:, q * G4:(q + 1) * G4], ident[:, 0:P], HC[:, n % 2, q * G4:(q + 1) * G4],
                                                start=(s == 0), stop=(s == DS - 1))
                            ins.then_inc(y_added, 1)

                    @block.scalar
                    def _(act):
                        act.wait_ge(zeroed, 1)
                        for i in range(NPASS):
                            for s in range(DS):
                                n = i * DS + s
                                if n >= 2:
                                    act.wait_ge(h_ready, n - 1)
                                ab = AB[:, n % 2, :].rearrange("p (b t) -> p b t", t=S)[:, :, 1:]
                                e = E[:, i, :].rearrange("p (b t) -> p b t", t=S)[:, :, 1:]
                                act.activation(ab, e, ACT.Exp, scale=AA[:, i, s:s + 1], bias=AA[:, i, s:s + 1]).then_inc(decay_ready, 1)
                                act.wait_ge(c_ready, n + 1)
                                if n >= 3:
                                    act.wait_ge(hc_ready, n - 2)
                                act.activation(CS[:, n % 3, :], CP[:], ACT.Copy).then_inc(c_copied, 1)

                    @block.vector
                    def _(v):
                        for i in range(NPASS):
                            for s in range(DS):
                                n = i * DS + s
                                v.wait_ge(b_ready, n + 1)
                                if n >= 2:
                                    v.wait_ge(h_ready, n - 1)
                                v.tensor_tensor(BU[:, n % 2, :], DU[:, i, :], BP[:, n % 2, :], ALU.mult).then_inc(bu_ready, 1)
                                v.wait_ge(bu_ready, n + 1)
                                v.wait_ge(decay_ready, n + 1)
                                if n >= 3:
                                    v.wait_ge(hc_ready, n - 2)
                                v.tensor_tensor_scan(H[:, n % 3, :], AB[:, n % 2, :], BU[:, n % 2, :], 0.0, ALU.mult, ALU.add).then_inc(h_ready, 1)
                            v.wait_ge(y_added, (i + 1) * DS)
                            v.scalar_tensor_tensor(U[:, i, :], U[:, i, :], DV[:, i:i + 1], YP[:], ALU.mult, ALU.add).then_inc(y_read, 1)

        def out_product(pe, t, out):
            h, col = t // (NT // 2), (t % (NT // 2)) * P
            for c in range(NCH):
                ins = pe.matmul(out, U[:, 2 * c + h, col:col + P], WO[:, c, :], start=(c == 0), stop=(c == NCH - 1))
            return ins

        finish_norm(nc, "mamba_norm", X, XT, ident, out_product)


NHEAD, DH = 8, 64
INNER = NHEAD * DH
NIN = INNER // P
DCTX = 192
KC = [P, DCTX - P]


def load_context(io, CT):
    return [(CT[0:KC[k], k, :], io["ctxT"][k * P:k * P + KC[k], :]) for k in range(2)]


def load_split(W, src):
    return [(W[0:KC[k], k, :], src[k * P:k * P + KC[k], :]) for k in range(2)]


def stage_xattn(nc, io, X, XT, ident):
    with Stage(nc, "xa") as st:
        QT = st.sb("QT", [P, NIN, T])
        WO = st.sb("WO", [P, NIN, D])
        BO = st.sb("BO", [1, D])
        with Stage(nc, "xb") as s1:
            KT = s1.sb("KT", [P, NIN, T])
            V = s1.sb("V", [P, NT, INNER])
            with Stage(nc, "xc") as s2:
                CT = s2.sb("CT", [P, 2, T])
                WQ = s2.sb("WQ", [P, KD, INNER])
                WK = s2.sb("WK", [P, 2, INNER])
                WV = s2.sb("WV", [P, 2, INNER])
                loads = load_context(io, CT) + load_split(WK, io["L0_xattn_Wk"]) + load_split(WV, io["L0_xattn_Wv"]) + [
                    (WQ[:], io["L0_xattn_Wq"].rearrange("(k p) n -> p k n", p=P)),
                    (WO[:], io["L0_xattn_Wo"].rearrange("(k p) n -> p k n", p=P)), (BO[:], io["L0_xattn_bo"])]
                jobs = []
                for g in range(T // G4):
                    tok = slice(g * G4, (g + 1) * G4)
                    for c in range(NIN):
                        col = slice(c * P, (c + 1) * P)
                        jobs.append((QT[:, c, tok], [(WQ[:, k, col], XT[:, k, tok]) for k in range(KD)], copy_out))
                        jobs.append((KT[:, c, tok], [(WK[0:KC[k], k, col], CT[0:KC[k], k, tok]) for k in range(2)], copy_out))
                for t in range(NT):
                    jobs.append((V[:, t, :], [(CT[0:KC[k], k, t * P:(t + 1) * P], WV[0:KC[k], k, :]) for k in range(2)], copy_out))
                products(nc, "xproj", jobs, loads)

            attention(nc, ident, QT, KT, V)

        def out_product(pe, t, out):
            for c in range(NIN):
                pe.matmul(out, QT[:, c, t * P:(t + 1) * P], WO[:, c, :], start=(c == 0), stop=False)
            return add_bias(pe, ident, out, BO[:])

        finish_norm(nc, "xnorm", X, XT, ident, out_product)


def attention(nc, ident, QT, KT, V):
    NU = B * NIN
    SCALE = float(DH) ** -0.5
    with Stage(nc, "attn") as st:
        PR = st.sb("PR", [P, 2, 4, S])
        PN = st.sb("PN", [P, 2, 4, S])
        PT = st.sb("PT", [P, 2, 2, 2, S])
        MX = st.sb("MX", [P, NU, 4])
        SM = st.sb("SM", [P, NU, 4])
        SC = st.ps("SC", [P, 2, 4, S])
        TP = st.ps("TP", [P, 2, 2, S])
        OT = st.ps("OT", [P, 2, 512])
        scores_ready = st.sem("scores_ready")
        max_ready = st.sem("max_ready")
        exp_ready = st.sem("exp_ready")
        sum_ready = st.sem("sum_ready")
        probs_ready = st.sem("probs_ready")
        turned = st.sem("turned")
        turned_act = st.sem("turned_act")
        turned_dve = st.sem("turned_dve")
        out_ready = st.sem("out_ready")
        out_copied = st.sem("out_copied")
        dve_chain = st.sem("dve_chain")
        with st.block() as block:
            @block.tensor
            def _(pe):
                def scores(m):
                    b, c = m // NIN, m % NIN
                    if m >= 2:
                        pe.wait_ge(exp_ready, m - 1)
                    for t in range(2):
                        for h in range(2):
                            r = slice(h * DH, (h + 1) * DH)
                            ins = pe.matmul(SC[:, m % 2, 2 * h + t, :], QT[r, c, b * S + t * P:b * S + (t + 1) * P],
                                            KT[r, c, b * S:(b + 1) * S], start=True, stop=True)
                    ins.then_inc(scores_ready, 1)

                def values(m):
                    b, c = m // NIN, m % NIN
                    pe.wait_ge(turned_act, m + 1)
                    pe.wait_ge(turned_dve, m + 1)
                    if m >= 2:
                        pe.wait_ge(out_copied, m - 1)
                    for h in range(2):
                        for k in range(2):
                            ins = pe.matmul(OT[h * DH:(h + 1) * DH, m % 2, 0:S], V[:, 2 * b + k, c * P + h * DH:c * P + (h + 1) * DH],
                                            PT[:, m % 2, h, k, :], start=(k == 0), stop=(k == 1))
                    ins.then_inc(out_ready, 1)

                scores(0)
                scores(1)
                for m in range(NU):
                    if m + 2 < NU:
                        scores(m + 2)
                    pe.wait_ge(probs_ready, m + 1)
                    if m:
                        pe.wait_ge(turned_act, m)
                        pe.wait_ge(turned_dve, m)
                    for h in range(2):
                        for k in range(2):
                            for t in range(2):
                                ins = pe.transpose(TP[:, h, k, t * P:(t + 1) * P], PN[:, m % 2, 2 * h + t, k * P:(k + 1) * P], ident[:, 0:P])
                        ins.then_inc(turned, 1)
                    if m:
                        values(m - 1)
                values(NU - 1)

            @block.scalar
            def _(act):
                def exps(m):
                    act.wait_ge(max_ready, m + 1)
                    if m >= 2:
                        act.wait_ge(probs_ready, m - 1)
                    for j in range(4):
                        ins = act.activation(PR[:, m % 2, j, :], SC[:, m % 2, j, :], ACT.Exp, scale=SCALE,
                                             bias=MX[:, m, j:j + 1], accum_out=SM[:, m, j:j + 1])
                    ins.then_inc(exp_ready, 1)

                def out_copy(m):
                    act.wait_ge(out_ready, m + 1)
                    b, c = m // NIN, m % NIN
                    act.activation(QT[:, c, b * S:(b + 1) * S], OT[:, m % 2, 0:S], ACT.Copy).then_inc(out_copied, 1)

                exps(0)
                for m in range(NU):
                    if m + 1 < NU:
                        exps(m + 1)
                    act.wait_ge(turned, 2 * m + 1)
                    if m >= 2:
                        act.wait_ge(out_ready, m - 1)
                    act.activation(PT[:, m % 2, 0], TP[:, 0], ACT.Copy).then_inc(turned_act, 1)
                    if m:
                        out_copy(m - 1)
                out_copy(NU - 1)


            @block.gpsimd
            def _(pool):
                for m in range(NU):
                    pool.wait_ge(sum_ready, m + 1)
                    if m >= 2:
                        pool.wait_ge(turned, 2 * (m - 1))
                    pool.tensor_tensor(PN[:, m % 2], PR[:, m % 2], SM[:, m, :].rearrange("p (j o) -> p j o", o=1).to_broadcast([P, 4, S]),
                                       ALU.mult).then_inc(probs_ready, 1)

            @block.vector
            def _(v):
                ch = Chain(v, dve_chain)

                def maxima(m):
                    v.wait_ge(scores_ready, m + 1)
                    ch.link(v.tensor_reduce(MX[:, m, :], SC[:, m % 2], AX_X, ALU.max))
                    v.tensor_scalar(MX[:, m, :], MX[:, m, :], -SCALE, None, ALU.mult).then_inc(max_ready, 1)

                def sums(m):
                    v.wait_ge(exp_ready, m + 1)
                    v.reciprocal(SM[:, m, :], SM[:, m, :]).then_inc(sum_ready, 1)

                maxima(0)
                maxima(1)
                sums(0)
                for m in range(NU):
                    if m + 2 < NU:
                        maxima(m + 2)
                    if m + 1 < NU:
                        sums(m + 1)
                    v.wait_ge(turned, 2 * m + 2)
                    if m >= 2:
                        v.wait_ge(out_ready, m - 1)
                    v.tensor_copy(PT[:, m % 2, 1], TP[:, 1]).then_inc(turned_dve, 1)


NE, HID = 16, 1024
CAP = int(1.25 * T / NE)
SLOTS = NE * CAP
HC_ = CAP // 2
NHID = HID // P


def stage_moe(nc, io, X, XT, ident):
    dispatch = nc.dram_tensor("moe_dispatch", (SLOTS + T, D), F32).ap()
    answers = nc.dram_tensor("moe_answers", (SLOTS, D), F32).ap()
    with Stage(nc, "moe") as st:
        TO = st.sb("TO", [P, NT], I32)
        FROM = st.sb("FROM", [P, NT], I32)
        WT = st.sb("WT", [P, NT])
        moe_route(nc, io, X, XT, ident, TO, FROM, WT, dispatch)
        moe_experts(nc, io, ident, dispatch, answers)
        GA = st.sb("GA", [P, NT, D])
        with Stage(nc, "combine") as s2:
            gathered = s2.sem("gathered")
            with s2.block() as block:
                @block.gpsimd
                def _(pool):
                    for t in range(NT):
                        pool.indirect_dma_start(out=GA[:, t, :], out_offset=None, in_=answers,
                                                in_offset=bass.IndirectOffsetOnAxis(ap=FROM[:, t:t + 1], axis=0)).then_inc(gathered, 16)
                    pool.wait_ge(gathered, 16 * NT)

                @block.scalar
                def _(act):
                    act.wait_ge(gathered, 16 * NT)
                    for t in range(NT):
                        act.activation(GA[:, t, :], GA[:, t, :], ACT.Copy, scale=WT[:, t:t + 1])
        finish_norm(nc, "moenorm", X, XT, ident, None, base=lambda t: GA[:, t, :])


def moe_route(nc, io, X, XT, ident, TO, FROM, WT, dispatch):
    with Stage(nc, "route") as st:
        GW = st.sb("GW", [P, KD, NE])
        TRI = st.sb("TRI", [P, 2, P])
        EI = st.sb("EI", [P, NE])
        TI = st.sb("TI", [P, NT])
        ZERO = st.sb("ZERO", [P, SLOTS // P * D])
        MX = st.sb("MX", [P, NT, 8])
        MI = st.sb("MI", [P, NT, 8], U32)
        NM = st.sb("NM", [P, NT])
        EX = st.sb("EX", [P, NT, NE])
        SM = st.sb("SM", [P, NT])
        OH = st.sb("OH", [P, NT, NE])
        RUN = st.sb("RUN", [P, NT, NE])
        TMP = st.sb("TMP", [P, NE])
        FI = st.sb("FI", [P, NT])
        LOC = st.sb("LOC", [P, NT])
        KEEP = st.sb("KEEP", [P, NT])
        FT = st.sb("FT", [P, NT])
        LG = st.ps("LG", [P, NT, NE])
        CS = st.ps("CS", [P, NT, NE])
        loaded = st.sem("loaded")
        zero_ready = st.sem("zero_ready")
        zeroed = st.sem("zeroed")
        logits_ready = st.sem("logits_ready")
        max_ready = st.sem("max_ready")
        exp_ready = st.sem("exp_ready")
        onehot_ready = st.sem("onehot_ready")
        counted = st.sem("counted")
        routed = st.sem("routed")
        sent = st.sem("sent")
        dve_chain = st.sem("dve_chain")
        with st.block() as block:
            @block.sync
            def _(sp):
                sp.dma_start(GW[:], io["L0_ffn_gateT"].rearrange("(k p) n -> p k n", p=P)).then_inc(loaded, 16)
                sp.dma_start(TRI[:], io["tri"]).then_inc(loaded, 16)
                sp.dma_start(EI[:], io["expert_numbers"]).then_inc(loaded, 16)
                sp.dma_start(TI[:], io["spill_rows"]).then_inc(loaded, 16)
                sp.wait_ge(zero_ready, 1)
                sp.dma_start(dispatch[0:SLOTS, :].rearrange("(p r) d -> p (r d)", p=P), ZERO[:]).then_inc(zeroed, 16)

            @block.tensor
            def _(pe):
                pe.wait_ge(loaded, 64)
                for t in range(NT):
                    for k in range(KD):
                        ins = pe.matmul(LG[:, t, :], XT[:, k, t * P:(t + 1) * P], GW[:, k, :], start=(k == 0), stop=(k == KD - 1))
                ins.then_inc(logits_ready, 1)
                pe.wait_ge(onehot_ready, 1)
                for t in range(NT):
                    if t:
                        pe.matmul(CS[:, t, :], TRI[:, 1, :], RUN[:, t, :], start=True, stop=False)
                    ins = pe.matmul(CS[:, t, :], TRI[:, 0, :], OH[:, t, :], start=(t == 0), stop=True)
                ins.then_inc(counted, 1)

            @block.scalar
            def _(act):
                act.wait_ge(max_ready, 1)
                for t in range(NT):
                    ins = act.activation(EX[:, t, :], LG[:, t, :], ACT.Exp, bias=NM[:, t:t + 1], accum_out=SM[:, t:t + 1])
                ins.then_inc(exp_ready, 1)

            @block.vector
            def _(v):
                ch = Chain(v, dve_chain)
                v.memset(ZERO[:], 0.0).then_inc(zero_ready, 1)
                v.wait_ge(loaded, 64)
                v.wait_ge(logits_ready, 1)
                for t in range(NT):
                    ch.link(v.max(MX[:, t, :], LG[:, t, :]))
                    ch.link(v.max_index(MI[:, t, :], MX[:, t, :], LG[:, t, :]))
                v.tensor_scalar(NM[:], MX[:, :, 0], -1.0, None, ALU.mult).then_inc(max_ready, 1)
                ch.link(v.tensor_copy(FI[:], MI[:, :, 0]))
                for t in range(NT):
                    ch.link(v.tensor_scalar(OH[:, t, :], EI[:], FI[:, t:t + 1], None, ALU.is_equal))
                ch.link(v.memset(RUN[:, 0, :], 0.0))
                for t in range(1, NT):
                    ins = v.tensor_tensor(RUN[:, t, :], RUN[:, t - 1, :], OH[:, t - 1, :], ALU.add)
                    ch.link(ins)
                v.sem_inc(onehot_ready, 1)
                v.wait_ge(counted, 1)
                for t in range(NT):
                    ch.link(v.tensor_tensor(TMP[:], OH[:, t, :], CS[:, t, :], ALU.mult))
                    ch.link(v.tensor_reduce(LOC[:, t:t + 1], TMP[:], AX_X, ALU.add))
                ch.link(v.tensor_scalar(LOC[:], LOC[:], 1.0, None, ALU.subtract))
                ch.link(v.tensor_scalar(KEEP[:], LOC[:], float(CAP), None, ALU.is_lt))
                ch.link(v.scalar_tensor_tensor(FI[:], FI[:], float(CAP), LOC[:], ALU.mult, ALU.add))
                ch.link(v.tensor_tensor(FT[:], FI[:], KEEP[:], ALU.mult))
                ch.link(v.tensor_copy(FROM[:], FT[:]))
                ch.link(v.tensor_tensor(FI[:], FI[:], TI[:], ALU.subtract))
                ch.link(v.tensor_tensor(FI[:], FI[:], KEEP[:], ALU.mult))
                ch.link(v.tensor_tensor(FI[:], FI[:], TI[:], ALU.add))
                v.tensor_copy(TO[:], FI[:]).then_inc(routed, 1)
                v.wait_ge(exp_ready, 1)
                ch.link(v.reciprocal(SM[:], SM[:]))
                ch.link(v.tensor_tensor(WT[:], SM[:], KEEP[:], ALU.mult))

            @block.gpsimd
            def _(pool):
                pool.wait_ge(routed, 1)
                pool.wait_ge(zeroed, 16)
                for t in range(NT):
                    pool.indirect_dma_start(out=dispatch, out_offset=bass.IndirectOffsetOnAxis(ap=TO[:, t:t + 1], axis=0),
                                            in_=X[:, t, :], in_offset=None).then_inc(sent, 16)
                pool.wait_ge(sent, 16 * NT)


def moe_experts(nc, io, ident, dispatch, answers):
    with Stage(nc, "experts") as st:
        W1 = st.sb("W1", [P, 2, KD, HID])
        W2 = st.sb("W2", [P, 2, NHID, D])
        XE = st.sb("XE", [HC_, 2, 2, D])
        XET = st.sb("XET", [P, 2, KD, CAP])
        HT = st.sb("HT", [P, 2, NHID, CAP])
        YE = st.sb("YE", [HC_, 2, 2, D])
        TP = st.ps("TP", [P, 2, 512])
        HP = st.ps("HP", [P, 4, 512])
        YP = st.ps("YP", [HC_, 2, 2, D])
        w_loaded = [st.sem(f"w_loaded{i}") for i in range(2)]
        x_loaded = [st.sem(f"x_loaded{i}") for i in range(2)]
        stored = [st.sem(f"stored{i}") for i in range(2)]
        turned = st.sem("turned")
        turned_read = st.sem("turned_read")
        hid_ready = st.sem("hid_ready")
        relu_act = st.sem("relu_act")
        relu_dve = st.sem("relu_dve")
        y_ready = st.sem("y_ready")
        y_copied = st.sem("y_copied")
        with st.block() as block:
            @block.sync
            def _(sp):
                def store(e):
                    sp.wait_ge(y_copied, e + 1)
                    sp.dma_start(answers[e * CAP:(e + 1) * CAP, :].rearrange("(a p) d -> p a d", p=HC_), YE[:, e % 2]).then_inc(stored[e % 2], 16)

                for e in range(NE):
                    if e >= 2:
                        sp.wait_ge(y_ready, e - 1)
                    sp.dma_start(XE[:, e % 2], dispatch[e * CAP:(e + 1) * CAP, :].rearrange("(a p) d -> p a d", p=HC_)).then_inc(x_loaded[e % 2], 16)
                    sp.dma_start(W1[:, e % 2], io["L0_ffn_w1"][e].rearrange("(k p) n -> p k n", p=P)).then_inc(w_loaded[e % 2], 16)
                    sp.dma_start(W2[:, e % 2], io["L0_ffn_w2"][e].rearrange("(k p) n -> p k n", p=P)).then_inc(w_loaded[e % 2], 16)
                    if e >= 2:
                        store(e - 2)
                store(NE - 2)
                store(NE - 1)
                for i in range(2):
                    sp.wait_ge(stored[i], 16 * (NE // 2))

            @block.tensor
            def _(pe):
                def turn(e):
                    pe.wait_ge(x_loaded[e % 2], 16 * (e // 2 + 1))
                    for k in range(KD):
                        if 2 * e + k >= 2:
                            pe.wait_ge(turned_read, 2 * e + k - 1)
                        for a in range(2):
                            ins = pe.transpose(TP[:, k, a * HC_:(a + 1) * HC_], XE[:, e % 2, a, k * P:(k + 1) * P], ident[0:HC_, 0:HC_])
                        ins.then_inc(turned, 1)

                turn(0)
                for e in range(NE):
                    pe.wait_ge(w_loaded[e % 2], 32 * (e // 2 + 1))
                    pe.wait_ge(turned_read, 2 * (e + 1))
                    for q in range(NHID // 2):
                        n = e * 4 + q
                        if n >= 4:
                            pe.wait_ge(relu_dve if q % 2 else relu_act, (n - 4) // 2 + 1)
                        for a in range(2):
                            c = 2 * q + a
                            for k in range(KD):
                                ins = pe.matmul(HP[:, q, a * CAP:(a + 1) * CAP], W1[:, e % 2, k, c * P:(c + 1) * P], XET[:, e % 2, k, :],
                                                start=(k == 0), stop=(k == KD - 1))
                        ins.then_inc(hid_ready, 1)
                    if e + 1 < NE:
                        turn(e + 1)
                    pe.wait_ge(relu_act, 2 * (e + 1))
                    pe.wait_ge(relu_dve, 2 * (e + 1))
                    if e >= 2:
                        pe.wait_ge(y_copied, e - 1)
                    for a in range(2):
                        for c in range(NHID):
                            ins = pe.matmul(YP[:, e % 2, a, :], HT[:, e % 2, c, a * HC_:(a + 1) * HC_], W2[:, e % 2, c, :],
                                            start=(c == 0), stop=(c == NHID - 1))
                    ins.then_inc(y_ready, 1)

            def relu_out(e, q):
                return HT[:, e % 2, 2 * q:2 * q + 2, :], HP[:, q, 0:2 * CAP].rearrange("p (a n) -> p a n", a=2)

            @block.scalar
            def _(act):
                for e in range(NE):
                    for q in (0, 2):
                        act.wait_ge(hid_ready, 4 * e + q + 1)
                        if e >= 2:
                            act.wait_ge(y_ready, e - 1)
                        out, hid = relu_out(e, q)
                        act.activation(out, hid, ACT.Relu).then_inc(relu_act, 1)
                    act.wait_ge(y_ready, e + 1)
                    if e >= 2:
                        act.wait_ge(stored[e % 2], 16 * (e // 2))
                    act.activation(YE[:, e % 2], YP[:, e % 2], ACT.Copy).then_inc(y_copied, 1)

            @block.vector
            def _(v):
                def take(e):
                    for k in range(KD):
                        v.wait_ge(turned, 2 * e + k + 1)
                        if e >= 2:
                            v.wait_ge(hid_ready, 4 * (e - 1))
                        v.tensor_copy(XET[:, e % 2, k, :], TP[:, k, 0:CAP]).then_inc(turned_read, 1)

                take(0)
                for e in range(NE):
                    for q in (1, 3):
                        v.wait_ge(hid_ready, 4 * e + q + 1)
                        if e >= 2:
                            v.wait_ge(y_ready, e - 1)
                        out, hid = relu_out(e, q)
                        v.tensor_scalar(out, hid, 0.0, None, ALU.max).then_inc(relu_dve, 1)
                    if e + 1 < NE:
                        take(e + 1)


LH, LD = 16, 16
LPAD = 32
LC = LH * LPAD // P
LHC = LH // LC
PHI_EPS = 1e-3


def phi_out(v, out, product):
    return v.tensor_scalar(out, product, 0.0, PHI_EPS, ALU.max, ALU.add)


def mlp(nc, name, XT, ident, W1, W2, B1, HT, w1, b1, func, loads):
    loads = loads + [(W1[:], w1.rearrange("(k p) n -> p k n", p=P)), (B1[:], b1)]
    with Stage(nc, name) as st:
        ring = st.ps("ring", [P, 8, G4])
        loaded = st.sem("loaded")
        ready = st.sem("ready")
        read = st.sem("read")
        steps = [(g, c) for g in range(T // G4) for c in range(NHID)]
        with st.block() as block:
            @block.sync
            def _(sp):
                for dst, src in loads:
                    sp.dma_start(dst, src).then_inc(loaded, 16)

            @block.tensor
            def _(pe):
                pe.wait_ge(loaded, 16 * len(loads))
                for n, (g, c) in enumerate(steps):
                    if n >= 8:
                        pe.wait_ge(read, n - 7)
                    for k in range(KD):
                        ins = pe.matmul(ring[:, n % 8, :], W1[:, k, c * P:(c + 1) * P], XT[:, k, g * G4:(g + 1) * G4],
                                        start=(k == 0), stop=(k == KD - 1))
                    ins.then_inc(ready, 1)

            @block.scalar
            def _(act):
                act.wait_ge(loaded, 16 * len(loads))
                for n, (g, c) in enumerate(steps):
                    act.wait_ge(ready, n + 1)
                    act.activation(HT[:, c, g * G4:(g + 1) * G4], ring[:, n % 8, :], func, bias=B1[:, 0, c:c + 1]).then_inc(read, 1)


def mlp_product(HT, W2, B2, ident):
    def product(pe, t, out):
        for c in range(NHID):
            pe.matmul(out, HT[:, c, t * P:(t + 1) * P], W2[:, c, :], start=(c == 0), stop=False)
        return add_bias(pe, ident, out, B2[:])
    return product


def stage_performer(nc, io, X, XT, ident):
    with Stage(nc, "pf") as st:
        LN = st.sb("LN", [P, 4, KD])
        WO = st.sb("WO", [P, KD, D])
        X1 = st.sb("X1", [P, NT, D])
        W2 = st.sb("W2", [P, NHID, D])
        B2 = st.sb("B2", [1, D])
        finish_norm(nc, "pfln1", X, XT, ident, None, total=lambda t: X[:, t, :], base=lambda t: None,
                    out=lambda t: X1[:, t, :], eps=EPS6, scale=LN[:, 0, :], bias=LN[:, 1, :],
                    loads=[(LN[:], io["L1_attn_ln"])])
        with Stage(nc, "pg") as s1:
            QT = s1.sb("QT", [P, LC, T])
            KT = s1.sb("KT", [P, LC, T])
            VA = s1.sb("VA", [P, NT, LH, 2 * LD])
            WQ = s1.sb("WQ", [P, KD, LC * P])
            WK = s1.sb("WK", [P, KD, LC * P])
            WV = s1.sb("WV", [P, KD, D])
            MASK = s1.sb("MASK", [P, 2, P])
            loads = [(WQ[:], io["L1_attn_wq"].rearrange("(k p) n -> p k n", p=P)),
                     (WK[:], io["L1_attn_wk"].rearrange("(k p) n -> p k n", p=P)),
                     (WV[:], io["L1_attn_wv"].rearrange("(k p) n -> p k n", p=P)),
                     (WO[:], io["L1_attn_wo"].rearrange("(k p) n -> p k n", p=P)),
                     (MASK[:], io["tri"])]
            with s1.block() as block:
                @block.gpsimd
                def _(pool):
                    pool.memset(VA[:].rearrange("p t h d -> p (t h) d")[:, :, LD:2 * LD], 1.0)
            jobs = []
            for g in range(T // G4):
                tok = slice(g * G4, (g + 1) * G4)
                for W, OUT in ((WQ, QT), (WK, KT)):
                    for c in range(LC):
                        jobs.append((OUT[:, c, tok], [(W[:, k, c * P:(c + 1) * P], XT[:, k, tok]) for k in range(KD)], phi_out))

            def value_out(v, out, product):
                return v.tensor_copy(out, product.rearrange("p (h d) -> p h d", h=LH))

            for t in range(NT):
                jobs.append((VA[:, t, :, 0:LD], [(XT[:, k, t * P:(t + 1) * P], WV[:, k, :]) for k in range(KD)], value_out))
            products(nc, "pfproj", jobs, loads, dve_only=True)
            performer_core(nc, ident, QT, KT, VA, MASK, X1)
            turn_tiles(nc, "pfturn", X1, XT, ident)

        def out_product(pe, t, out):
            for k in range(KD):
                ins = pe.matmul(out, XT[:, k, t * P:(t + 1) * P], WO[:, k, :], start=(k == 0), stop=(k == KD - 1))
            return ins

        with Stage(nc, "ph") as s1:
            HT = s1.sb("HT", [P, NHID, T])
            with Stage(nc, "pi") as s2:
                YT = s2.sb("YT", [P, KD, T])
                W1 = s2.sb("W1", [P, KD, HID])
                B1 = s2.sb("B1", [P, 1, NHID])
                Z = s2.sb("Z", [P, 2, D])
                finish_norm(nc, "pfln2", X, YT, ident, out_product, total=lambda t: X1[:, t, :], also=lambda t: X[:, t, :],
                            out=lambda t: X1[:, t, :], eps=EPS6, scale=LN[:, 2, :], bias=LN[:, 3, :])
                mlp(nc, "pfmlp", YT, ident, W1, W2, B1, HT, io["L1_attn_w1"], io["L1_attn_b1"], ACT.Gelu_apprx_tanh,
                    [(W2[:], io["L1_attn_w2"].rearrange("(k p) n -> p k n", p=P)), (B2[:], io["L1_attn_b2"])])
            finish_norm(nc, "pfnorm", X, XT, ident, mlp_product(HT, W2, B2, ident))


def turn_tiles(nc, name, Y, YT, ident):
    with Stage(nc, name) as st:
        TP = st.ps("TP", [P, 4, 512])
        turned = st.sem("turned")
        read = st.sem("read")
        with st.block() as block:
            @block.tensor
            def _(pe):
                for t in range(NT):
                    if t >= 4:
                        pe.wait_ge(read, t - 3)
                    for k in range(KD):
                        ins = pe.transpose(TP[:, t % 4, k * P:(k + 1) * P], Y[:, t, k * P:(k + 1) * P], ident[:, 0:P])
                    ins.then_inc(turned, 1)

            @block.scalar
            def _(act):
                for t in range(NT):
                    act.wait_ge(turned, t + 1)
                    act.activation(YT[:, :, t * P:(t + 1) * P], TP[:, t % 4, 0:D].rearrange("p (k n) -> p k n", k=KD), ACT.Copy).then_inc(read, 1)


def performer_core(nc, ident, QT, KT, VA, MASK, AO):
    NU = B * LC
    with Stage(nc, "pfcore") as st:
        A = st.sb("A", [P, 2, LHC, 3, P])
        OS = st.sb("OS", [P, 2, S])
        RD = st.sb("RD", [P, 2, LHC])
        SC = st.ps("SC", [P, LHC, 512])
        OP = st.ps("OP", [P, 2, 512])
        TP = st.ps("TP", [P, 2, 512])
        scores_ready = st.sem("scores_ready")
        masked = st.sem("masked")
        out_ready = st.sem("out_ready")
        out_copied = st.sem("out_copied")
        turned = st.sem("turned")
        normed = st.sem("normed")
        dve_chain = st.sem("dve_chain")
        with st.block() as block:
            @block.tensor
            def _(pe):
                def turn(m):
                    pe.wait_ge(out_copied, m + 1)
                    if m >= 2:
                        pe.wait_ge(normed, m - 1)
                    for a in range(2):
                        ins = pe.transpose(TP[:, m % 2, a * P:(a + 1) * P], OS[:, m % 2, a * P:(a + 1) * P], ident[:, 0:P])
                    ins.then_inc(turned, 1)

                def outs(m):
                    b, c = m // LC, m % LC
                    pe.wait_ge(masked, m + 1)
                    if m >= 2:
                        pe.wait_ge(out_copied, m - 1)
                    for h in range(LHC):
                        hd = c * LHC + h
                        r = slice(h * LPAD, (h + 1) * LPAD)
                        pe.matmul(OP[r, m % 2, 0:S], VA[:, 2 * b, hd, :], A[:, m % 2, h, 0:2, :], start=True, stop=False)
                        ins = pe.matmul(OP[r, m % 2, P:S], VA[:, 2 * b + 1, hd, :], A[:, m % 2, h, 2, :], start=False, stop=True)
                    ins.then_inc(out_ready, 1)

                for m in range(NU):
                    b, c = m // LC, m % LC
                    if m:
                        pe.wait_ge(masked, m)
                    for h in range(LHC):
                        r = slice(h * LPAD, h * LPAD + LD)
                        pe.matmul(SC[:, h, 0:S], KT[r, c, b * S:b * S + P], QT[r, c, b * S:(b + 1) * S], start=True, stop=True,
                                  tile_position=(h * LPAD, 0))
                        ins = pe.matmul(SC[:, h, S:S + P], KT[r, c, b * S + P:(b + 1) * S], QT[r, c, b * S + P:(b + 1) * S], start=True, stop=True,
                                        tile_position=(h * LPAD, 0))
                    ins.then_inc(scores_ready, 1)
                    if m >= 1:
                        outs(m - 1)
                    if m >= 2:
                        turn(m - 2)
                outs(NU - 1)
                turn(NU - 2)
                turn(NU - 1)

            @block.scalar
            def _(act):
                for m in range(NU):
                    act.wait_ge(out_ready, m + 1)
                    if m >= 2:
                        act.wait_ge(turned, m - 1)
                    act.activation(OS[:, m % 2, :], OP[:, m % 2, 0:S], ACT.Copy).then_inc(out_copied, 1)

            @block.vector
            def _(v):
                ch = Chain(v, dve_chain)

                def norm(m):
                    b, c = m // LC, m % LC
                    v.wait_ge(turned, m + 1)
                    tp = TP[:, m % 2, 0:S].rearrange("p (a h d) -> p a h d", a=2, h=LHC)
                    ch.link(v.reciprocal(RD[:], tp[:, :, :, LD]))
                    for a in range(2):
                        ch.link(v.tensor_tensor(AO[:, 2 * b + a, c * LHC * LD:(c + 1) * LHC * LD].rearrange("p (h d) -> p h d", h=LHC),
                                                tp[:, a, :, 0:LD], RD[:, a, :].rearrange("p (h o) -> p h o", o=1).to_broadcast([P, LHC, LD]),
                                                ALU.mult))
                    v.sem_inc(normed, 1)

                for m in range(NU):
                    v.wait_ge(scores_ready, m + 1)
                    if m >= 2:
                        v.wait_ge(out_ready, m - 1)
                    sc = SC[:, :, 0:3 * P].rearrange("p h (a q) -> p h a q", a=3)
                    a = A[:, m % 2]
                    tri = MASK[:, 0:1, :].to_broadcast([P, LHC, P])
                    v.tensor_tensor(a[:, :, 0, :], sc[:, :, 0, :], tri, ALU.mult)
                    v.tensor_tensor(a[:, :, 2, :], sc[:, :, 2, :], tri, ALU.mult)
                    v.tensor_copy(a[:, :, 1, :], sc[:, :, 1, :]).then_inc(masked, 1)
                    if m >= 3:
                        norm(m - 3)
                for m in range(NU - 3, NU):
                    norm(m)


XH, XD = 4, 32
TOPK = 32
NST = 64
LO = 16
NF = 2 * 2
MASKED, TAKEN = -3e38, -3.4e38
MAGIC = 1.5 * 2 ** 23
TURN = 6.2831845


def stage_s4d(nc, io, X, XT, ident):
    with Stage(nc, "s4") as st:
        KF = st.sb("KF", [P, NF, D])
        s4d_kernel(nc, io, KF)
        Z = st.sb("Z", [P, NT, D])
        FO = st.sb("FO", [P, NT, 2 * D])
        with Stage(nc, "s5") as s1:
            CTT = s1.sb("CTT", [P, KD, T])
            topk_attention(nc, io, XT, ident, CTT)
            finish_norm(nc, "s4ln", X, None, ident, None, base=lambda t: None, out=lambda t: Z[:, t, :])
            film(nc, io, ident, CTT, Z, FO)
        s4d_convolve(nc, io, KF, X, Z, FO)
        with Stage(nc, "s6") as s1:
            HT = s1.sb("HT", [P, NHID, T])
            W2 = s1.sb("W2", [P, NHID, D])
            B2 = s1.sb("B2", [1, D])
            LN = s1.sb("LN", [P, 2, KD])
            finish_norm(nc, "s4ln2", X, XT, ident, None, total=lambda t: Z[:, t, :], base=lambda t: None,
                        out=lambda t: FO[:, t, 0:D], scale=LN[:, 0, :], bias=LN[:, 1, :], loads=[(LN[:], io["L1_xattn_ffn_ln"])])
            with Stage(nc, "s7") as s2:
                W1 = s2.sb("W1", [P, KD, HID])
                B1 = s2.sb("B1", [P, 1, NHID])
                mlp(nc, "s4mlp", XT, ident, W1, W2, B1, HT, io["L1_xattn_W1"], io["L1_xattn_b1"], ACT.Gelu,
                    [(W2[:], io["L1_xattn_W2"].rearrange("(k p) n -> p k n", p=P)), (B2[:], io["L1_xattn_b2"])])
            finish_norm(nc, "s4ln3", X, None, ident, mlp_product(HT, W2, B2, ident), total=lambda t: Z[:, t, :],
                        base=lambda t: Z[:, t, :], out=lambda t: Z[:, t, :])
        GB = st.sb("GB", [P, 2, D])
        with Stage(nc, "s8") as s1:
            loaded = s1.sem("loaded")
            scaled = s1.sem("scaled")
            with s1.block() as block:
                @block.sync
                def _(sp):
                    sp.dma_start(GB[:], io["L1_xattn_norm_out"]).then_inc(loaded, 16)

                @block.vector
                def _(v):
                    v.wait_ge(loaded, 16)
                    v.tensor_tensor(Z[:], Z[:], GB[:, 0:1, :].to_broadcast([P, NT, D]), ALU.mult).then_inc(scaled, 1)
                    v.wait_ge(scaled, 1)
                    v.tensor_tensor(Z[:], Z[:], GB[:, 1:2, :].to_broadcast([P, NT, D]), ALU.add)
        finish_norm(nc, "s4norm", X, XT, ident, None, base=lambda t: Z[:, t, :])


def s4d_kernel(nc, io, KF):
    HI = S // LO
    with Stage(nc, "s4k") as st, ExitStack() as closing:
        kp = closing.enter_context(Stage(nc, "s4p"))
        PAR = st.sb("PAR", [P, 5, D])
        COL = st.sb("COL", [P, 4])
        POW = st.sb("POW", [P, 2, LO])
        AR = st.sb("AR", [P, D])
        AI = st.sb("AI", [P, D])
        W_ = st.sb("W_", [P, 12, D])
        TT_ = st.sb("TT_", [P, D, LO])
        RR = st.sb("RR", [P, D, LO])
        EX = st.sb("EX", [P, D, LO])
        UU = st.sb("UU", [P, D, LO])
        U2 = st.sb("U2", [P, D, LO])
        VV = st.sb("VV", [P, D, LO])
        KA = st.sb("KA", [HI, D, LO])
        WK = st.sb("WK", [HI, LO, NF, P])
        KP = kp.ps("KP", [HI, D, LO])
        loaded = st.sem("loaded")
        for_act = st.sem("for_act")
        by_act = st.sem("by_act")
        tables_ready = st.sem("tables_ready")
        k_ready = st.sem("k_ready")
        dve_chain = st.sem("dve_chain")
        with st.block() as block:
            @block.sync
            def _(sp):
                sp.dma_start(PAR[:], io["L1_xattn_s4d"]).then_inc(loaded, 16)
                sp.dma_start(COL[:], io["phases"]).then_inc(loaded, 16)
                sp.dma_start(POW[:], io["powers"]).then_inc(loaded, 16)
                sp.dma_start(WK[:], io["dft_kernel"]).then_inc(loaded, 16)

            asked = [(PAR[:, 0, :], PAR[:, 0, :], ACT.Exp, 1.0), (W_[:, 0, :], AR[:], ACT.Tanh, 0.5),
                     (EX[:], TT_[:], ACT.Exp, 1.0), (UU[:], RR[:], ACT.Sin, TURN), (U2[:], RR[:], ACT.Sin, TURN),
                     (EX[:], TT_[:], ACT.Exp, 1.0), (VV[:], RR[:], ACT.Sin, TURN),
                     (W_[:, 1:4, :], W_[:, 1:4, :], ACT.Sin, TURN)]

            @block.scalar
            def _(act):
                for n, (out, in_, func, scale) in enumerate(asked):
                    act.wait_ge(for_act, n + 1)
                    act.activation(out, in_, func, scale=scale).then_inc(by_act, 1)

            @block.vector
            def _(v):
                ch = Chain(v, dve_chain)
                n = [0]

                def ask():
                    v.sem_inc(for_act, 1)
                    n[0] += 1

                def answered():
                    v.wait_ge(by_act, n[0])

                def fraction(out, turns, tmp):
                    ch.link(v.tensor_scalar(tmp, turns, MAGIC, None, ALU.add))
                    ch.link(v.tensor_scalar(tmp, tmp, MAGIC, None, ALU.subtract))
                    ch.link(v.tensor_tensor(out, turns, tmp, ALU.subtract))

                def wide(x):
                    return x.rearrange("p (d o) -> p d o", o=1).to_broadcast([P, D, LO])

                def power(i):
                    return POW[:, i:i + 1, :].to_broadcast([P, D, LO])

                v.wait_ge(loaded, 64)
                ask()
                answered()
                ch.link(v.tensor_tensor(AR[:], PAR[:, 1, :], PAR[:, 0, :], ALU.mult))
                ch.link(v.tensor_tensor(AI[:], PAR[:, 2, :], PAR[:, 0, :], ALU.mult))
                ch.link(v.tensor_scalar(AI[:], AI[:], 1.0 / (2 * np.pi), None, ALU.mult))
                ask()
                answered()
                for i, parts in ((0, ((0, UU), (1, U2))), (1, ((2, VV),))):
                    ch.link(v.tensor_tensor(TT_[:], wide(AR[:]), power(i), ALU.mult))
                    ask()
                    answered()
                    ch.link(v.tensor_tensor(TT_[:], wide(AI[:]), power(i), ALU.mult))
                    for col, out in parts:
                        ch.link(v.tensor_scalar(out[:], TT_[:], COL[:, col:col + 1], None, ALU.add))
                        fraction(RR[:], out[:], RR[:])
                        ask()
                        answered()
                        ch.link(v.tensor_tensor(out[:], out[:], EX[:], ALU.mult))
                th, s1, s2, s3 = (W_[:, i, :] for i in range(4))
                ch.link(v.tensor_scalar(s1, AI[:], 0.25, None, ALU.add))
                ch.link(v.tensor_copy(s2, AI[:]))
                ch.link(v.tensor_scalar(s3, AI[:], 0.5, None, ALU.mult))
                fraction(W_[:, 1:4, :], W_[:, 1:4, :], W_[:, 4:7, :])
                ask()
                answered()
                t4, t5, er, ei, nr, ni, a2, t11 = (W_[:, i, :] for i in range(4, 12))
                ch.link(v.tensor_scalar(t4, th, -1.0, 1.0, ALU.mult, ALU.add))
                ch.link(v.reciprocal(t4, t4))
                ch.link(v.scalar_tensor_tensor(t5, th, 2.0, t4, ALU.mult, ALU.mult))
                ch.link(v.tensor_tensor(er, t5, s1, ALU.mult))
                ch.link(v.tensor_tensor(s3, s3, s3, ALU.mult))
                ch.link(v.scalar_tensor_tensor(er, s3, -2.0, er, ALU.mult, ALU.add))
                ch.link(v.scalar_tensor_tensor(ei, t5, 1.0, s2, ALU.add, ALU.mult))
                Ar, Ai, Cr, Ci = (PAR[:, i, :] for i in range(1, 5))

                def combine(out, a, b, c, d, op):
                    ch.link(v.tensor_tensor(t11, a, b, ALU.mult))
                    ch.link(v.tensor_tensor(t4, c, d, ALU.mult))
                    ch.link(v.tensor_tensor(out, t11, t4, op))

                combine(nr, Cr, er, Ci, ei, ALU.subtract)
                combine(ni, Cr, ei, Ci, er, ALU.add)
                combine(a2, Ar, Ar, Ai, Ai, ALU.add)
                ch.link(v.reciprocal(a2, a2))
                combine(er, nr, Ar, ni, Ai, ALU.add)
                combine(ei, ni, Ar, nr, Ai, ALU.subtract)
                ch.link(v.tensor_tensor(er, er, a2, ALU.mult))
                ch.link(v.tensor_tensor(ei, ei, a2, ALU.mult))
                ch.link(v.tensor_tensor(UU[:], UU[:], wide(er), ALU.mult))
                ch.link(v.tensor_tensor(U2[:], U2[:], wide(ei), ALU.mult))
                v.tensor_tensor(UU[:], UU[:], U2[:], ALU.add).then_inc(tables_ready, 1)
                v.wait_ge(k_ready, 1)
                v.tensor_scalar(KA[:], KP[:], 2.0, None, ALU.mult)

            @block.tensor
            def _(pe):
                pe.wait_ge(tables_ready, 1)
                for d in range(D):
                    ins = pe.matmul(KP[:, d, :], UU[:, d, :], VV[:, d, :], start=True, stop=True)
                ins.then_inc(k_ready, 1)

        closing.close()
        products(nc, "s4kf", [(KF[:, q, :], [(WK[:, b, q, :], KA[:, :, b]) for b in range(LO)], copy_out) for q in range(NF)])


def topk_attention(nc, io, XT, ident, CTT):
    with Stage(nc, "tk") as st:
        QT = st.sb("QT", [P, T])
        KT = st.sb("KT", [P, T])
        V = st.sb("V", [P, NT, D])
        MB = st.sb("MB", [P, T])
        TM = st.sb("TM", [P, T])
        with Stage(nc, "tl") as s2:
            CT = s2.sb("CT", [P, 2, T])
            WQ = s2.sb("WQ", [P, KD, P])
            WK = s2.sb("WK", [P, 2, P])
            WV = s2.sb("WV", [P, 2, D])
            M8 = s2.sb("M8", [P, 2, T], U8)
            loads = load_context(io, CT) + load_split(WK, io["L1_xattn_Wk"]) + load_split(WV, io["L1_xattn_Wv"]) + [
                (WQ[:], io["L1_xattn_Wq"].rearrange("(k p) n -> p k n", p=P)), (M8[:, 0, :], io["text_mask"]), (M8[:, 1, :], io["vision_mask"])]
            jobs = []
            for g in range(T // G4):
                tok = slice(g * G4, (g + 1) * G4)
                jobs.append((QT[:, tok], [(WQ[:, k, :], XT[:, k, tok]) for k in range(KD)], copy_out))
                jobs.append((KT[:, tok], [(WK[0:KC[k], k, :], CT[0:KC[k], k, tok]) for k in range(2)], copy_out))
            for t in range(NT):
                jobs.append((V[:, t, :], [(CT[0:KC[k], k, t * P:(t + 1) * P], WV[0:KC[k], k, :]) for k in range(2)], copy_out))
            products(nc, "tkproj", jobs, loads)
            with s2.block() as block:
                @block.vector
                def _(v):
                    v.tensor_copy(TM[:], M8[:, 0, :])
                    v.tensor_scalar(MB[:], M8[:, 1, :], -MASKED, MASKED, ALU.mult, ALU.add)

        SS = st.sb("SS", [P, 2, XH, S])
        WW = st.sb("WW", [P, XH, S])
        EX = st.sb("EX", [P, 2, XH, S])
        PP = st.sb("PP", [P, XH, S])
        AM = st.sb("AM", [P, 2, S])
        AT = st.sb("AT", [P, 2, 2, P])
        MX = st.sb("MX", [P, XH, TOPK])
        NM = st.sb("NM", [P, 2, XH])
        SM = st.sb("SM", [P, XH])
        SC = st.ps("SC", [P, XH, 512])
        TP = st.ps("TP", [P, 2, 512])
        CP = st.ps("CP", [P, 2, 512])
        scores_ready = st.sem("scores_ready")
        scores_read = st.sem("scores_read")
        max_ready = st.sem("max_ready")
        exp_ready = st.sem("exp_ready")
        mean_ready = st.sem("mean_ready")
        turned = st.sem("turned")
        turned_read = st.sem("turned_read")
        pooled = st.sem("pooled")
        pooled_read = st.sem("pooled_read")
        dve_chain = st.sem("dve_chain")
        with st.block() as block:
            @block.tensor
            def _(pe):
                def scores(n):
                    if n:
                        pe.wait_ge(scores_read, n)
                    b = n // 2
                    for h in range(XH):
                        r = slice(h * XD, (h + 1) * XD)
                        ins = pe.matmul(SC[:, h, 0:S], QT[r, n * P:(n + 1) * P], KT[r, b * S:(b + 1) * S], start=True, stop=True,
                                        tile_position=(h * XD, 0))
                    ins.then_inc(scores_ready, 1)

                def pool_context(n):
                    pe.wait_ge(mean_ready, n + 1)
                    if n >= 2:
                        pe.wait_ge(turned_read, n - 1)
                    for k in range(2):
                        ins = pe.transpose(TP[:, n % 2, k * P:(k + 1) * P], AM[:, n % 2, k * P:(k + 1) * P], ident[:, 0:P])
                    ins.then_inc(turned, 1)
                    pe.wait_ge(turned_read, n + 1)
                    if n >= 2:
                        pe.wait_ge(pooled_read, n - 1)
                    for c in range(KD):
                        for k in range(2):
                            ins = pe.matmul(CP[:, n % 2, c * P:(c + 1) * P], V[:, (n // 2) * 2 + k, c * P:(c + 1) * P], AT[:, n % 2, k, :],
                                            start=(k == 0), stop=(k == 1))
                    ins.then_inc(pooled, 1)

                scores(0)
                for n in range(NT):
                    if n + 1 < NT:
                        scores(n + 1)
                    pool_context(n)

            @block.scalar
            def _(act):
                for n in range(NT):
                    act.wait_ge(max_ready, n + 1)
                    for h in range(XH):
                        ins = act.activation(EX[:, n % 2, h, :], SS[:, n % 2, h, :], ACT.Exp, bias=NM[:, n % 2, h:h + 1])
                    ins.then_inc(exp_ready, 1)
                    act.wait_ge(turned, n + 1)
                    act.activation(AT[:, n % 2], TP[:, n % 2, 0:2 * P].rearrange("p (k q) -> p k q", k=2), ACT.Copy).then_inc(turned_read, 1)

            @block.vector
            def _(v):
                ch = Chain(v, dve_chain)

                def pooled_out(n):
                    v.wait_ge(pooled, n + 1)
                    tok = slice(n * P, (n + 1) * P)
                    v.tensor_tensor(CTT[:, :, tok], CP[:, n % 2, 0:D].rearrange("p (c q) -> p c q", c=KD),
                                    TM[:, tok].rearrange("p (o q) -> p o q", o=1).to_broadcast([P, KD, P]), ALU.mult).then_inc(pooled_read, 1)

                for n in range(NT):
                    b = n // 2
                    v.wait_ge(scores_ready, n + 1)
                    ss = SS[:, n % 2]
                    v.scalar_tensor_tensor(ss, SC[:, :, 0:S], float(XD) ** -0.5,
                                           MB[:, b * S:(b + 1) * S].rearrange("p (o q) -> p o q", o=1).to_broadcast([P, XH, S]),
                                           ALU.mult, ALU.add).then_inc(scores_read, 1)
                    v.wait_ge(scores_read, n + 1)
                    for r in range(TOPK // 8):
                        src = ss if r == 0 else WW[:]
                        for h in range(XH):
                            ins = v.max(MX[:, h, 8 * r:8 * r + 8], src[:, h, :])
                        ch.link(ins)
                        if r == 0:
                            v.tensor_scalar(NM[:, n % 2, :], MX[:, :, 0], -1.0, None, ALU.mult).then_inc(max_ready, 1)
                        for h in range(XH):
                            ins = v.match_replace(WW[:, h, :], MX[:, h, 8 * r:8 * r + 8], src[:, h, :], TAKEN)
                        ch.link(ins)
                    v.wait_ge(exp_ready, n + 1)
                    for h in range(XH):
                        ins = v.scalar_tensor_tensor(PP[:, h, :], WW[:, h, :], 0.5 * (TAKEN + MASKED), EX[:, n % 2, h, :], ALU.is_le, ALU.mult,
                                                     accum_out=SM[:, h:h + 1])
                    ch.link(ins)
                    ch.link(v.reciprocal(SM[:], SM[:]))
                    ch.link(v.tensor_scalar(SM[:], SM[:], 1.0 / XH, None, ALU.mult))
                    if n >= 2:
                        v.wait_ge(turned, n - 1)
                    am = AM[:, n % 2, :]
                    ch.link(v.tensor_scalar(am, PP[:, 0, :], SM[:, 0:1], None, ALU.mult))
                    for h in range(1, XH):
                        ins = v.scalar_tensor_tensor(am, PP[:, h, :], SM[:, h:h + 1], am, ALU.mult, ALU.add)
                        ch.link(ins)
                    v.sem_inc(mean_ready, 1)
                    if n:
                        pooled_out(n - 1)
                pooled_out(NT - 1)


def film(nc, io, ident, CTT, Z, FO):
    with Stage(nc, "film") as st:
        WI = st.sb("WI", [P, 2, KD, 2 * D])
        BI = st.sb("BI", [1, 2, 2 * D])
        GB = st.sb("GB", [P, 2, D])
        GATE = st.sb("GATE", [P, 1])
        FI = st.sb("FI", [P, 2, 2 * D])
        FP = st.ps("FP", [P, 4, 512])
        loaded = st.sem("loaded")
        ready = st.sem("ready")
        in_read = st.sem("in_read")
        out_read = st.sem("out_read")
        affine = st.sem("affine")
        used = st.sem("used")
        pool_chain = st.sem("pool_chain")
        dve_chain = st.sem("dve_chain")
        with st.block() as block:
            @block.sync
            def _(sp):
                for n, name in enumerate(("in", "out")):
                    sp.dma_start(WI[:, n], io["L1_xattn_W_film_" + name].rearrange("(k p) n -> p k n", p=P)).then_inc(loaded, 16)
                    sp.dma_start(BI[:, n, :], io["L1_xattn_b_film_" + name]).then_inc(loaded, 16)
                sp.dma_start(GB[:], io["L1_xattn_norm_in"]).then_inc(loaded, 16)
                sp.dma_start(GATE[:], io["L1_xattn_gate"]).then_inc(loaded, 16)

            @block.tensor
            def _(pe):
                pe.wait_ge(loaded, 96)
                for t in range(NT):
                    if t >= 2:
                        pe.wait_ge(in_read, t - 1)
                        pe.wait_ge(out_read, t - 1)
                    for n in range(2):
                        bank = FP[:, 2 * (t % 2) + n, :]
                        for k in range(KD):
                            pe.matmul(bank, CTT[:, k, t * P:(t + 1) * P], WI[:, n, k, :], start=(k == 0), stop=False)
                        ins = add_bias(pe, ident, bank, BI[:, n, :])
                    ins.then_inc(ready, 1)

            @block.scalar
            def _(act):
                act.wait_ge(loaded, 96)
                for t in range(NT):
                    act.wait_ge(ready, t + 1)
                    if t >= 2:
                        act.wait_ge(used, t - 1)
                    act.activation(FI[:, t % 2, :], FP[:, 2 * (t % 2), :], ACT.Copy, scale=GATE[:]).then_inc(in_read, 1)
                    act.activation(FO[:, t, :], FP[:, 2 * (t % 2) + 1, :], ACT.Copy, scale=GATE[:]).then_inc(out_read, 1)

            @block.gpsimd
            def _(pool):
                ch = Chain(pool, pool_chain)
                pool.wait_ge(loaded, 96)
                for t in range(NT):
                    ch.link(pool.tensor_tensor(Z[:, t, :], Z[:, t, :], GB[:, 0, :], ALU.mult))
                    pool.tensor_tensor(Z[:, t, :], Z[:, t, :], GB[:, 1, :], ALU.add).then_inc(affine, 1)

            @block.vector
            def _(v):
                ch = Chain(v, dve_chain)
                for t in range(NT):
                    v.wait_ge(affine, t + 1)
                    v.wait_ge(in_read, t + 1)
                    ch.link(v.scalar_tensor_tensor(Z[:, t, :], FI[:, t % 2, 0:D], 1.0, Z[:, t, :], ALU.add, ALU.mult))
                    v.tensor_tensor(Z[:, t, :], Z[:, t, :], FI[:, t % 2, D:2 * D], ALU.add).then_inc(used, 1)


def s4d_convolve(nc, io, KF, X, Z, FO):
    NP = B // 2
    with Stage(nc, "cv") as st:
        DFT = st.sb("DFT", [P, 2, NF, P])
        INV = st.sb("INV", [P, NF, 2, P])
        SK = st.sb("SK", [P, D])
        MM = st.sb("MM", [P, 4, 2, D])
        YF = st.sb("YF", [P, 2, NF, 2, D])
        XD = st.sb("XD", [P, 4, D])
        XF = st.ps("XF", [P, NF, 2, D])
        YP = st.ps("YP", [P, 2, 2, D])
        loaded = st.sem("loaded")
        xf_ready = st.sem("xf_ready")
        xf_read = st.sem("xf_read")
        prod_ready = st.sem("prod_ready")
        prod_used = st.sem("prod_used")
        skip_ready = st.sem("skip_ready")
        y_ready = st.sem("y_ready")
        y_read = st.sem("y_read")
        done = st.sem("done")
        dve_chain = st.sem("dve_chain")
        pool_chain = st.sem("pool_chain")
        with st.block() as block:
            @block.sync
            def _(sp):
                sp.dma_start(DFT[:], io["dft"]).then_inc(loaded, 16)
                sp.dma_start(INV[:], io["dft_inverse"]).then_inc(loaded, 16)
                sp.dma_start(SK[:], io["L1_xattn_D_skip"]).then_inc(loaded, 16)

            def tiles(buf, pr):
                return buf[:, 4 * pr:4 * pr + 4, :].rearrange("p (b h) d -> p b h d", h=2)

            @block.tensor
            def _(pe):
                pe.wait_ge(loaded, 48)
                for pr in range(NP):
                    for ft in range(2):
                        for q in (2 * ft, 2 * ft + 1):
                            if pr:
                                pe.wait_ge(xf_read, 2 * (pr - 1) + ft + 1)
                            for h in range(2):
                                ins = pe.matmul(XF[:, q], DFT[:, h, q, :], tiles(Z, pr)[:, :, h, :], start=(h == 0), stop=(h == 1))
                        ins.then_inc(xf_ready, 1)
                    pe.wait_ge(prod_used, 2 * (pr + 1))
                    for h in range(2):
                        if pr:
                            pe.wait_ge(y_read, 2 * (pr - 1) + h + 1)
                        for q in range(NF):
                            ins = pe.matmul(YP[:, h], INV[:, q, h, :], YF[:, pr % 2, q], start=(q == 0), stop=(q == NF - 1))
                        ins.then_inc(y_ready, 1)

            @block.gpsimd
            def _(pool):
                ch = Chain(pool, pool_chain)
                pool.wait_ge(loaded, 48)
                for pr in range(NP):
                    if pr:
                        pool.wait_ge(y_read, 2 * pr)
                    pool.tensor_tensor(XD[:], Z[:, 4 * pr:4 * pr + 4, :], SK[:].rearrange("p (o d) -> p o d", o=1).to_broadcast([P, 4, D]),
                                       ALU.mult).then_inc(skip_ready, 1)
                    if pr >= 2:
                        pool.wait_ge(y_ready, 2 * (pr - 1))
                    for ft in range(2):
                        pool.wait_ge(prod_ready, 2 * pr + ft + 1)
                        ch.link(pool.tensor_tensor(YF[:, pr % 2, 2 * ft], MM[:, 0], MM[:, 1], ALU.subtract))
                        pool.tensor_tensor(YF[:, pr % 2, 2 * ft + 1], MM[:, 2], MM[:, 3], ALU.add).then_inc(prod_used, 1)

            @block.vector
            def _(v):
                ch = Chain(v, dve_chain)
                for pr in range(NP):
                    for ft in range(2):
                        n = 2 * pr + ft
                        v.wait_ge(xf_ready, n + 1)
                        if n:
                            v.wait_ge(prod_used, n)
                        for i, (x, k) in enumerate(((0, 0), (1, 1), (0, 1), (1, 0))):
                            ins = v.tensor_tensor(MM[:, i], XF[:, 2 * ft + x],
                                                  KF[:, 2 * ft + k:2 * ft + k + 1, :].to_broadcast([P, 2, D]), ALU.mult)
                            ch.link(ins)
                        v.sem_inc(prod_ready, 1)
                        v.sem_inc(xf_read, 1)
                    v.wait_ge(skip_ready, pr + 1)
                    for h in range(2):
                        v.wait_ge(y_ready, 2 * pr + h + 1)
                        z = tiles(Z, pr)[:, :, h, :]
                        fo = tiles(FO, pr)[:, :, h, :]
                        xd = XD[:].rearrange("p (b h) d -> p b h d", h=2)[:, :, h, :]
                        ch.link(v.tensor_tensor(z, YP[:, h], xd, ALU.add))
                        v.sem_inc(y_read, 1)
                        ch.link(v.scalar_tensor_tensor(z, fo[:, :, 0:D], 1.0, z, ALU.add, ALU.mult))
                        ch.link(v.tensor_tensor(z, z, fo[:, :, D:2 * D], ALU.add))
                        ch.link(v.tensor_tensor(z, z, tiles(X, pr)[:, :, h, :], ALU.add))


PH, PK, NK = 8, 8, 64
NC_ = 2 * PH
HK = PH * PK
J2 = NK // 2
BLK = 256
UNIT = 32
PSCALE = 2.0 ** 14
F16 = mybir.dt.float16


def stage_peer(nc, io, X, XT, ident):
    with Stage(nc, "pe") as st:
        IXT = st.sb("IXT", [P, T], F16)
        IYT = st.sb("IYT", [P, T], F16)
        PRT = st.sb("PRT", [P, T], F16)
        with Stage(nc, "pq") as s1:
            SV = s1.sb("SV", [P, NT, NC_, PK])
            IV = s1.sb("IV", [P, NT, NC_, PK], U32)
            peer_sides(nc, io, XT, ident, SV, IV)
            peer_select(nc, ident, SV, IV, IXT, IYT, PRT)
        peer_experts(nc, io, X, XT, IXT, IYT, PRT)
        finish_norm(nc, "pnorm", X, XT, ident, None, base=lambda t: None, last=True)


def peer_sides(nc, io, XT, ident, SV, IV):
    with Stage(nc, "sides") as st:
        WQ = st.sb("WQ", [P, KD, NC_ * P])
        KEYS = st.sb("KEYS", [P, NC_, NK])
        BN = st.sb("BN", [P, 2, NC_])
        QN = st.sb("QN", [P, 2, T])
        RAW = st.sb("RAW", [P, 4, 6])
        MV = st.sb("MV", [P, NC_, 2])
        SD = st.sb("SD", [P, NC_])
        SB_ = st.sb("SB_", [P, NC_, 2])
        QP = st.ps("QP", [P, 4, G4])
        SP_ = st.ps("SP_", [P, 2, NT, NK])
        loaded = st.sem("loaded")
        q_ready = st.sem("q_ready")
        var_ready = st.sem("var_ready")
        std_ready = st.sem("std_ready")
        affine_ready = st.sem("affine_ready")
        q_normed = st.sem("q_normed")
        sims_ready = st.sem("sims_ready")
        sims_read = st.sem("sims_read")
        dve_chain = st.sem("dve_chain")
        with st.block() as block:
            @block.sync
            def _(sp):
                sp.dma_start(WQ[:], io["L1_ffn_w_q"].rearrange("(k p) n -> p k n", p=P)).then_inc(loaded, 16)
                sp.dma_start(KEYS[:], io["L1_ffn_keysT"]).then_inc(loaded, 16)
                sp.dma_start(BN[:], io["L1_ffn_bn"]).then_inc(loaded, 16)

            @block.tensor
            def _(pe):
                def query(c):
                    if c:
                        pe.wait_ge(q_normed, c)
                    for g in range(4):
                        for k in range(KD):
                            ins = pe.matmul(QP[:, g, :], WQ[:, k, c * P:(c + 1) * P], XT[:, k, g * G4:(g + 1) * G4],
                                            start=(k == 0), stop=(k == KD - 1))
                    ins.then_inc(q_ready, 1)

                pe.wait_ge(loaded, 48)
                query(0)
                for c in range(NC_):
                    if c + 1 < NC_:
                        query(c + 1)
                    pe.wait_ge(q_normed, c + 1)
                    if c >= 2:
                        pe.wait_ge(sims_read, c - 1)
                    for t in range(NT):
                        ins = pe.matmul(SP_[:, c % 2, t, :], QN[:, c % 2, t * P:(t + 1) * P], KEYS[:, c, :], start=True, stop=True)
                    ins.then_inc(sims_ready, 1)

            @block.scalar
            def _(act):
                for c in range(NC_):
                    act.wait_ge(var_ready, c + 1)
                    act.activation(SD[:, c:c + 1], MV[:, c, 1:2], ACT.Sqrt, bias=ident[:, EPS5:EPS5 + 1]).then_inc(std_ready, 1)
                    act.wait_ge(affine_ready, c + 1)
                    if c >= 2:
                        act.wait_ge(sims_ready, c - 1)
                    act.activation(QN[:, c % 2, :], QP[:].rearrange("p g n -> p (g n)"), ACT.Identity, scale=SB_[:, c, 0:1],
                                   bias=SB_[:, c, 1:2]).then_inc(q_normed, 1)

            @block.vector
            def _(v):
                ch = Chain(v, dve_chain)

                def norm(c):
                    v.wait_ge(q_ready, c + 1)
                    for g in range(4):
                        ins = v.bn_stats(RAW[:, g, :], QP[:, g, :])
                    ch.link(ins)
                    v.bn_aggr(MV[:, c, :], RAW[:].rearrange("p g s -> p (g s)")).then_inc(var_ready, 1)
                    v.wait_ge(std_ready, c + 1)
                    ch.link(v.reciprocal(SD[:, c:c + 1], SD[:, c:c + 1]))
                    ch.link(v.tensor_tensor(SB_[:, c, 0:1], SD[:, c:c + 1], BN[:, 0, c:c + 1], ALU.mult))
                    ch.link(v.tensor_tensor(SB_[:, c, 1:2], SB_[:, c, 0:1], MV[:, c, 0:1], ALU.mult))
                    v.tensor_tensor(SB_[:, c, 1:2], BN[:, 1, c:c + 1], SB_[:, c, 1:2], ALU.subtract).then_inc(affine_ready, 1)

                v.wait_ge(loaded, 48)
                norm(0)
                for c in range(NC_):
                    if c + 1 < NC_:
                        norm(c + 1)
                    v.wait_ge(sims_ready, c + 1)
                    for t in range(NT):
                        ins = v.max(SV[:, t, c, :], SP_[:, c % 2, t, :])
                    ch.link(ins)
                    for t in range(NT):
                        ins = v.max_index(IV[:, t, c, :], SV[:, t, c, :], SP_[:, c % 2, t, :])
                    ins.then_inc(sims_read, 1)


def peer_select(nc, ident, SV, IV, IXT, IYT, PRT):
    N = NT * PH
    with Stage(nc, "select") as st:
        IF = st.sb("IF", [P, NT, NC_, PK])
        AS = st.sb("AS", [P, 2, PH, PK, PK])
        TV = st.sb("TV", [P, NT, PH, PK])
        AB = st.sb("AB", [P, 3, N, PK], U32)
        RF = st.sb("RF", [P, 2, N, PK])
        KX = st.sb("KX", [P, 2, N, PK])
        TMP = st.sb("TMP", [P, N, PK])
        PR = st.sb("PR", [P, N, PK])
        SM = st.sb("SM", [P, N])
        H16 = st.sb("H16", [P, N, PK], F16)
        DUP = st.sb("DUP", [P, 3, NT, 2, HK])
        TP = st.ps("TP", [P, 2, 4, P])
        summed = st.sem("summed")
        shifted = st.sem("shifted")
        exp_ready = st.sem("exp_ready")
        arranged = st.sem("arranged")
        turned = st.sem("turned")
        turned_read = st.sem("turned_read")
        picked = st.sem("picked")
        dve_chain = st.sem("dve_chain")
        with st.block() as block:
            @block.gpsimd
            def _(pool):
                for t in range(NT):
                    if t >= 2:
                        pool.wait_ge(picked, t - 1)
                    sx = SV[:, t, 0:PH, :].rearrange("p h (a o) -> p h a o", o=1).to_broadcast([P, PH, PK, PK])
                    sy = SV[:, t, PH:, :].rearrange("p h (o b) -> p h o b", o=1).to_broadcast([P, PH, PK, PK])
                    pool.tensor_tensor(AS[:, t % 2], sx, sy, ALU.add).then_inc(summed, 1)

            @block.scalar
            def _(act):
                act.wait_ge(shifted, 1)
                act.activation(PR[:], PR[:], ACT.Exp).then_inc(exp_ready, 1)
                for n in range(3 * NT // 4):
                    act.wait_ge(turned, n + 1)
                    q, t = n // (NT // 4), n % (NT // 4) * 4
                    out = (IXT, IYT, PRT)[q]
                    act.activation(out[:, t * P:(t + 4) * P], TP[:, n % 2].rearrange("p a q -> p (a q)"), ACT.Copy).then_inc(turned_read, 1)

            @block.tensor
            def _(pe):
                pe.wait_ge(arranged, 1)
                for n in range(3 * NT // 4):
                    if n >= 2:
                        pe.wait_ge(turned_read, n - 1)
                    for a in range(4):
                        q, t = n // (NT // 4), n % (NT // 4) * 4 + a
                        ins = pe.transpose(TP[:, n % 2, a, :], DUP[:, q, t].rearrange("p a k -> p (a k)"), ident[:, 0:P])
                    ins.then_inc(turned, 1)

            @block.vector
            def _(v):
                ch = Chain(v, dve_chain)
                ch.link(v.tensor_copy(IF[:], IV[:]))
                flat = AB[:, 0].rearrange("p (t h) k -> p t h k", t=NT)
                for t in range(NT):
                    v.wait_ge(summed, t + 1)
                    for h in range(PH):
                        ins = v.max(TV[:, t, h, :], AS[:, t % 2, h].rearrange("p a b -> p (a b)"))
                    ch.link(ins)
                    for h in range(PH):
                        ins = v.max_index(flat[:, t, h, :], TV[:, t, h, :], AS[:, t % 2, h].rearrange("p a b -> p (a b)"))
                    ch.link(ins)
                    v.sem_inc(picked, 1)
                tv = TV[:].rearrange("p t h k -> p (t h) k")
                ch.link(v.tensor_tensor(PR[:], tv, tv[:, :, 0:1].to_broadcast([P, N, PK]), ALU.subtract))
                v.sem_inc(shifted, 1)
                ch.link(v.tensor_scalar(AB[:, 1], AB[:, 0], 3, None, ALU.logical_shift_right))
                ch.link(v.tensor_scalar(AB[:, 2], AB[:, 0], PK - 1, None, ALU.bitwise_and))
                ch.link(v.tensor_copy(RF[:], AB[:, 1:3]))
                for side in range(2):
                    for r in range(PK):
                        idx = IF[:, :, side * PH:(side + 1) * PH, r:r + 1]
                        rf, tmp = (x.rearrange("p (t h) k -> p t h k", t=NT) for x in (RF[:, side], TMP[:]))
                        out = KX[:, side] if r == 0 else TMP[:]
                        ch.link(v.tensor_scalar(out, RF[:, side], float(r), None, ALU.is_equal))
                        o4 = out.rearrange("p (t h) k -> p t h k", t=NT)
                        ch.link(v.tensor_tensor(o4, o4, idx.to_broadcast([P, NT, PH, PK]), ALU.mult))
                        if r:
                            ch.link(v.tensor_tensor(KX[:, side], KX[:, side], TMP[:], ALU.add))
                v.wait_ge(exp_ready, 1)
                ch.link(v.tensor_reduce(SM[:], PR[:], AX_X, ALU.add))
                ch.link(v.reciprocal(SM[:], SM[:]))
                ch.link(v.tensor_scalar(SM[:], SM[:], PSCALE, None, ALU.mult))
                ch.link(v.tensor_tensor(PR[:], PR[:], SM[:].rearrange("p (n o) -> p n o", o=1).to_broadcast([P, N, PK]), ALU.mult))
                ch.link(v.tensor_copy(H16[:], PR[:]))
                dup = DUP[:].rearrange("p q t a (h k) -> p q a t h k", h=PH)
                kx = KX[:].rearrange("p q (t h) k -> p q t h k", t=NT)
                for a in range(2):
                    for q in range(2):
                        ch.link(v.tensor_copy(dup[:, q, a].rearrange("p t h k -> p t (h k)"), kx[:, q].rearrange("p t h k -> p t (h k)")))
                h16 = H16[:].rearrange("p (t h) k -> p t (h k)", t=NT)
                ch.link(v.tensor_copy(dup[:, 2, 0].rearrange("p t h k -> p t (h k)"), h16))
                v.tensor_tensor(dup[:, 2, 1].rearrange("p t h k -> p t (h k)"), PR[:].rearrange("p (t h) k -> p t (h k)", t=NT), h16,
                                ALU.subtract).then_inc(arranged, 1)


def peer_experts(nc, io, X, XT, IXT, IYT, PRT):
    NB = T // BLK
    UB = BLK // UNIT
    NU = NB * UB
    NP = J2 // 2
    PU = NP // UB
    TB = BLK // P
    with Stage(nc, "ex") as st:
        DOWN = st.sb("DOWN", [P, KD, J2, P])
        UP = st.sb("UP", [P, J2, D])
        GH = st.sb("GH", [P, 2, J2, BLK])
        IOTA = st.sb("IOTA", [P, NK, UNIT], F16)
        L = st.sb("L", [P, 2, NK, UNIT], F16)
        EQ = st.sb("EQ", [P, NK, UNIT], F16)
        R = st.sb("R", [P, 2, NK, UNIT], F16)
        HP = st.ps("HP", [P, 2, 2, BLK])
        GP = st.ps("GP", [P, 2, UNIT, J2])
        OP = st.ps("OP", [P, 2, 512])
        loaded = st.sem("loaded")
        hidden = st.sem("hidden")
        gelu_ready = st.sem("gelu_ready")
        left_ready = st.sem("left_ready")
        right_ready = st.sem("right_ready")
        gates_ready = st.sem("gates_ready")
        gated = st.sem("gated")
        out_ready = st.sem("out_ready")
        out_read = st.sem("out_read")
        dve_chain = st.sem("dve_chain")
        with st.block() as block:
            @block.sync
            def _(sp):
                sp.dma_start(IOTA[:], io["key_numbers"]).then_inc(loaded, 16)
                sp.dma_start(DOWN[:], io["L1_ffn_down"]).then_inc(loaded, 16)
                sp.dma_start(UP[:], io["L1_ffn_up"]).then_inc(loaded, 16)

            @block.tensor
            def _(pe):
                def hid(b, q):
                    n = b * NP + q
                    if n >= 2:
                        pe.wait_ge(gelu_ready, n - 1)
                    for a in range(2):
                        for k in range(KD):
                            ins = pe.matmul(HP[:, n % 2, a, :], DOWN[:, k, 2 * q + a, :], XT[:, k, b * BLK:(b + 1) * BLK],
                                            start=(k == 0), stop=(k == KD - 1))
                    ins.then_inc(hidden, 1)

                def gates(n):
                    pe.wait_ge(left_ready, n + 1)
                    pe.wait_ge(right_ready, n + 1)
                    if n >= 2:
                        pe.wait_ge(gated, n - 1)
                    for t in range(UNIT):
                        for jp in range(2):
                            ins = pe.matmul(GP[jp * NK:(jp + 1) * NK, n % 2, t, :], L[:, n % 2, :, t], R[:, n % 2, jp * J2:(jp + 1) * J2, t],
                                            start=True, stop=True, tile_position=(0, jp * NK))
                    ins.then_inc(gates_ready, 1)

                def answer(m):
                    b, a = m // TB, m % TB
                    pe.wait_ge(gated, (m + 1) * P // UNIT)
                    if m >= 2:
                        pe.wait_ge(out_read, m - 1)
                    for j in range(J2):
                        ins = pe.matmul(OP[:, m % 2, 0:D], GH[:, b % 2, j, a * P:(a + 1) * P], UP[:, j, :], start=(j == 0), stop=(j == J2 - 1))
                    ins.then_inc(out_ready, 1)

                pe.wait_ge(loaded, 48)
                for q in range(NP):
                    hid(0, q)
                for n in range(NU):
                    b, u = n // UB, n % UB
                    gates(n)
                    if n % (P // UNIT) == 1 and n > P // UNIT:
                        answer(n // (P // UNIT) - 1)
                    if b + 1 < NB:
                        for q in range(PU):
                            hid(b + 1, u * PU + q)
                answer(NT - 1)

            @block.scalar
            def _(act):
                for b in range(NB):
                    for q in range(NP):
                        n = b * NP + q
                        act.wait_ge(hidden, n + 1)
                        if b >= 2:
                            act.wait_ge(out_ready, (b - 1) * TB)
                        act.activation(GH[:, b % 2, 2 * q:2 * q + 2, :], HP[:, n % 2], ACT.Gelu_apprx_tanh).then_inc(gelu_ready, 1)

            @block.vector
            def _(v):
                ch = Chain(v, dve_chain)

                def answer_out(v, m):
                    v.wait_ge(out_ready, m + 1)
                    v.tensor_tensor(X[:, m, :], X[:, m, :], OP[:, m % 2, 0:D], ALU.add).then_inc(out_read, 1)

                def sides(n):
                    tok = slice(n * UNIT, (n + 1) * UNIT)

                    def along(x):
                        return x[:, tok].rearrange("p (o t) -> p o t", o=1).to_broadcast([P, NK, UNIT])

                    if n >= 2:
                        v.wait_ge(gates_ready, n - 1)
                    v.tensor_tensor(L[:, n % 2], IOTA[:], along(IXT), ALU.is_equal).then_inc(left_ready, 1)
                    ch.link(v.tensor_tensor(EQ[:], IOTA[:], along(IYT), ALU.is_equal))
                    v.tensor_tensor(R[:, n % 2], EQ[:], along(PRT), ALU.mult).then_inc(right_ready, 1)
                    v.wait_ge(right_ready, n + 1)

                v.wait_ge(loaded, 48)
                sides(0)
                for n in range(NU):
                    b, u = n // UB, n % UB
                    if n + 1 < NU:
                        sides(n + 1)
                    v.wait_ge(gates_ready, n + 1)
                    v.wait_ge(gelu_ready, (b + 1) * NP)
                    gh = GH[:, b % 2, :, u * UNIT:(u + 1) * UNIT]
                    v.scalar_tensor_tensor(gh, GP[:, n % 2].rearrange("p t j -> p j t"), 1.0 / PSCALE, gh, ALU.mult, ALU.mult).then_inc(gated, 1)
                    if n % (P // UNIT) == 2 and n > P // UNIT:
                        answer_out(v, n // (P // UNIT) - 1)
                answer_out(v, NT - 1)


STAGES = [stage_mamba, stage_xattn, stage_moe, stage_performer, stage_s4d, stage_peer]


def build(nc, io, out, stages=None):
    with nc.sbuf_tensor("X", [P, NT, D], F32) as X, nc.sbuf_tensor("XT", [P, KD, T], F32) as XT, \
            nc.sbuf_tensor("ident", [P, NI], F32) as ident:
        stored = nc.alloc_semaphore("stored")
        stage_load(nc, io, X, XT, ident)
        for stage in (STAGES if stages is None else stages):
            stage(nc, io, X, XT, ident)
            nc.clear_and_free_semaphores(list(Stage.semaphores))
            Stage.semaphores.clear()
            nc.all_engine_barrier()
        stage_store(nc, out, X, stored)


def columns(*vectors):
    return np.stack([v.reshape(-1, P).T for v in vectors], axis=1)


def rows(*vectors):
    return np.tile(np.stack(vectors), (P, 1, 1))


def layouts(inputs):
    a = {k: np.asarray(v) for k, v in inputs.items()}
    io = {}
    io["x"] = a["x"]
    io["xT"] = a["x"].reshape(T, D).T
    io["ident"] = np.concatenate([np.eye(P), np.full((P, 1), 1e-5), np.full((P, 1), 1e-6), np.ones((P, P))], axis=1).astype(np.float32)
    io["L0_attn_in_projT"] = a["L0_attn_in_proj_w"].T
    io["L0_attn_out_projT"] = a["L0_attn_out_proj_w"].T
    xp = a["L0_attn_x_proj_w"]
    io["L0_attn_x_delta"] = np.repeat(xp[0:1].T, P, axis=1)
    io["L0_attn_x_bc"] = np.concatenate([xp[1:].T] * 3, axis=1)
    sel = np.zeros((96, 32, P), np.uint16)
    for r in range(96):
        sel[r, r % 32, :] = BF16_ONE
    io["sel_bc"] = sel
    io["L0_attn_conv_w"] = a["L0_attn_conv_w"]
    io["L0_attn_vec"] = columns(a["L0_attn_conv_b"], a["L0_attn_dt_proj_w"][:, 0], a["L0_attn_dt_proj_b"], a["L0_attn_D"])
    io["L0_attn_A_log"] = a["L0_attn_A_log"]
    io["ctxT"] = a["ctx_768"].reshape(T, DCTX).T
    for n in ("Wq", "Wk", "Wv", "Wo"):
        io["L0_xattn_" + n] = a["L0_xattn_" + n]
    io["L0_xattn_bo"] = a["L0_xattn_bo"][None]
    io["L0_ffn_gateT"] = a["L0_ffn_gate_w"].T
    io["L0_ffn_w1"] = a["L0_ffn_w1"]
    io["L0_ffn_w2"] = a["L0_ffn_w2"]
    io["tri"] = np.stack([np.triu(np.ones((P, P))), np.ones((P, P))], axis=1).astype(np.float32)
    io["expert_numbers"] = np.tile(np.arange(NE, dtype=np.float32), (P, 1))
    io["spill_rows"] = (SLOTS + np.arange(T).reshape(NT, P).T).astype(np.float32)
    io["L1_attn_ln"] = columns(a["L1_attn_ln1_scale"], a["L1_attn_ln1_bias"], a["L1_attn_ln2_scale"], a["L1_attn_ln2_bias"])
    for n in ("wq", "wk"):
        io["L1_attn_" + n] = np.pad(a["L1_attn_" + n], ((0, 0), (0, 0), (0, LPAD - LD))).reshape(D, LH * LPAD)
    io["L1_attn_wv"] = a["L1_attn_wv"].reshape(D, D)
    io["L1_attn_wo"] = a["L1_attn_wo"].reshape(D, D)
    io["L1_attn_w1"] = a["L1_attn_w1"]
    io["L1_attn_w2"] = a["L1_attn_w2"]
    io["L1_attn_b1"] = columns(a["L1_attn_b1"])
    io["L1_attn_b2"] = a["L1_attn_b2"][None]
    for n in ("Wq", "Wk", "Wv", "W_film_in", "W_film_out", "W1", "W2"):
        io["L1_xattn_" + n] = a["L1_xattn_" + n]
    for n in ("b_film_in", "b_film_out", "b2"):
        io["L1_xattn_" + n] = a["L1_xattn_" + n][None]
    io["L1_xattn_b1"] = columns(a["L1_xattn_b1"])
    io["L1_xattn_ffn_ln"] = columns(a["L1_xattn_g_ffn"], a["L1_xattn_b_ffn"])
    io["L1_xattn_norm_in"] = rows(a["L1_xattn_g_norm_in"], a["L1_xattn_b_norm_in"])
    io["L1_xattn_norm_out"] = rows(a["L1_xattn_g_norm_out"], a["L1_xattn_b_norm_out"])
    io["L1_xattn_D_skip"] = np.tile(a["L1_xattn_D_skip"], (P, 1))
    io["L1_xattn_gate"] = np.tile(a["L1_xattn_mod_gate"].reshape(1, 1), (P, 1))
    for n, m in (("text_mask", "mask_BxS_bf1"), ("vision_mask", "mask_BxS2_bf1")):
        io[n] = np.tile(a[m].reshape(1, T).view(np.uint8), (P, 1))
    io["L1_xattn_s4d"] = np.stack([np.tile(a["L1_xattn_log_dt"], (P, 1))] +
                                  [np.concatenate([a["L1_xattn_" + n].T] * 2) for n in ("A_re", "A_im", "C_re", "C_im")], axis=1)
    low = (np.arange(P) < NST)[:, None]
    io["phases"] = np.concatenate([np.where(low, x, y) for x, y in ((0.25, 0.0), (0.5, 0.25), (0.25, 0.5), (0, 0))], axis=1).astype(np.float32)
    io["powers"] = np.tile(np.stack([LO * np.arange(LO), np.arange(LO)]).astype(np.float32), (P, 1, 1))
    angle = 2 * np.pi * np.outer(np.arange(S), np.arange(S) + 0.5) / (2 * S)
    forward = np.stack([np.cos(angle).reshape(S, 2, P), -np.sin(angle).reshape(S, 2, P)], axis=2).reshape(S, NF, P)
    io["dft_kernel"] = forward.reshape(S // LO, LO, NF, P).astype(np.float32)
    io["dft"] = forward.reshape(2, P, NF, P).transpose(1, 0, 2, 3).astype(np.float32)
    io["dft_inverse"] = (forward.reshape(2, P, NF, P).transpose(3, 2, 0, 1) / S).astype(np.float32)
    io["L1_ffn_w_q"] = a["L1_ffn_w_q"]
    io["L1_ffn_bn"] = columns(a["L1_ffn_bn_gamma"], a["L1_ffn_bn_beta"])
    io["L1_ffn_keysT"] = a["L1_ffn_keys"].transpose(3, 2, 0, 1).reshape(P, NC_, NK)
    tiles = (NK, 2, J2, D)
    io["L1_ffn_down"] = a["L1_ffn_down_embed"].reshape(tiles).transpose(3, 2, 1, 0).reshape(KD, P, J2, P).transpose(1, 0, 2, 3)
    io["L1_ffn_up"] = a["L1_ffn_up_embed"].reshape(tiles).transpose(1, 0, 2, 3).reshape(P, J2, D)
    io["key_numbers"] = np.tile(np.arange(NK, dtype=np.float16)[None, :, None], (P, 1, UNIT))
    return {k: np.ascontiguousarray(v) for k, v in io.items()}


def kernel(**inputs):
    import concourse.bacc as bacc
    from concourse.bass_utils import run_bass_kernel_spmd

    nc = bacc.Bacc("TRN2", target_bir_lowering=False, num_devices=1)
    arrays = layouts(inputs)
    io = {name: nc.dram_tensor(f"in_{name}", a.shape, mybir.dt.from_np(a.dtype), kind="ExternalInput").ap()
          for name, a in arrays.items()}
    out = nc.dram_tensor("out_0", (B, S, D), F32, kind="ExternalOutput").ap()
    build(nc, io, out)
    r = run_bass_kernel_spmd(nc, [{f"in_{k}": a for k, a in arrays.items()}], core_ids=[0])
    return r.results[0]["out_0"]
```

```python
from contextlib import ExitStack, contextmanager

import numpy as np

import concourse.bass as bass
from concourse import mybir

P = 128
B, S, D = 8, 256, 256
T = B * S
NT = T // P
KD = D // P
G4 = 512

F32 = mybir.dt.float32
BF16 = mybir.dt.bfloat16
I32 = mybir.dt.int32
U32 = mybir.dt.uint32
U8 = mybir.dt.uint8
ALU = mybir.AluOpType
ACT = mybir.ActivationFunctionType
AX_X = mybir.AxisListType.X
LN_EPS = 1e-5


class Chain:

    def __init__(self, eng, sem):
        self.eng, self.sem, self.n, self.base = eng, sem, 0, 0

    def link(self, ins):
        self.n += 1
        ins.then_inc(self.sem, 1)
        self.eng.wait_ge(self.sem, self.base + self.n)

    @contextmanager
    def loop(self, count, per):
        n0 = self.n
        with self.eng.Fori(0, count) as i:
            self.base, self.n = i * per + n0, 0
            yield i
            assert self.n == per, f"{self.n} links in a turn"
        self.base, self.n = 0, n0 + count * per


class Stage:

    semaphores = []

    def __init__(self, nc, name):
        self.nc, self.name, self.ctx, self.dmas = nc, name, ExitStack(), 0

    def __enter__(self):
        self.ctx.__enter__()
        return self

    def __exit__(self, *e):
        return self.ctx.__exit__(*e)

    def sb(self, name, shape, dt=F32):
        return self.ctx.enter_context(self.nc.sbuf_tensor(f"{self.name}_{name}", shape, dt))

    def ps(self, name, shape, dt=F32):
        return self.ctx.enter_context(self.nc.psum_tensor(f"{self.name}_{name}", shape, dt))

    def sem(self, name):
        self.semaphores.append(self.nc.alloc_semaphore(f"{self.name}_{name}"))
        return self.semaphores[-1]

    def block(self):
        return self.nc.Block(f"{self.name}_block")


def norm_stats(v, chain, x, raw, mean_var):
    chain.link(v.bn_stats(raw, x))
    return v.bn_aggr(mean_var, raw)


EPS5, EPS6 = P, P + 1
ONES = P + 2
NI = ONES + P


def stage_load(nc, io, X, XT, ident):
    with Stage(nc, "load") as st:
        loaded = st.sem("loaded")
        with st.block() as block:
            @block.sync
            def _(sp):
                sp.dma_start(X[:], io["x"].rearrange("b (h p) d -> p (b h) d", p=P)).then_inc(loaded, 16)
                sp.dma_start(XT[:], io["xT"].rearrange("(k p) t -> p k t", p=P)).then_inc(loaded, 16)
                sp.dma_start(ident[:], io["ident"]).then_inc(loaded, 16)
                sp.wait_ge(loaded, 48)


def stage_store(nc, out, X, stored):
    with Stage(nc, "store") as st:
        with st.block() as block:
            @block.sync
            def _(sp):
                sp.dma_start(out.rearrange("b (h p) d -> p (b h) d", p=P), X[:]).then_inc(stored, 16)
                sp.wait_ge(stored, 16)


def add_bias(pe, ident, out, row):
    return pe.matmul(out, ident[0:1, ONES:ONES + P], row, start=False, stop=True)


def products(nc, name, jobs, loads=(), dve_only=False):
    with Stage(nc, name) as st:
        BANKS = 8
        ring = st.ps("ring", [P, BANKS, 512])
        loaded = st.sem("loaded")
        product_ready = st.sem("product_ready")
        even_read = st.sem("even_read")
        odd_read = st.sem("odd_read")

        def bank(n, out):
            size = 1
            for d in out.shape[1:]:
                size *= d
            return ring[0:out.shape[0], n % BANKS, 0:size]

        def by_vector(n):
            return dve_only or n % 2 == 1

        with st.block() as block:
            @block.sync
            def _(sp):
                for dst, src in loads:
                    sp.dma_start(dst, src).then_inc(loaded, 16)

            @block.tensor
            def _(pe):
                if loads:
                    pe.wait_ge(loaded, 16 * len(loads))
                for n, (out, pairs, _) in enumerate(jobs):
                    m = n - BANKS
                    if m >= 0:
                        if dve_only:
                            pe.wait_ge(odd_read, m + 1)
                        else:
                            pe.wait_ge(odd_read if by_vector(m) else even_read, m // 2 + 1)
                    for i, (lhsT, rhs) in enumerate(pairs):
                        ins = pe.matmul(bank(n, out), lhsT, rhs, start=(i == 0), stop=(i == len(pairs) - 1))
                    ins.then_inc(product_ready, 1)

            @block.scalar
            def _(act):
                if loads:
                    act.wait_ge(loaded, 16 * len(loads))
                for n, (out, _, evacuate) in enumerate(jobs):
                    if not by_vector(n):
                        act.wait_ge(product_ready, n + 1)
                        evacuate(act, out, bank(n, out)).then_inc(even_read, 1)

            @block.vector
            def _(v):
                if loads:
                    v.wait_ge(loaded, 16 * len(loads))
                for n, (out, _, evacuate) in enumerate(jobs):
                    if by_vector(n):
                        v.wait_ge(product_ready, n + 1)
                        evacuate(v, out, bank(n, out)).then_inc(odd_read, 1)


def copy_out(eng, out, product):
    if len(out.shape) == 3:
        product = product.rearrange("p (a b) -> p a b", a=out.shape[1])
    if eng.engine == mybir.EngineType.Activation:
        return eng.activation(out, product, ACT.Copy)
    return eng.tensor_copy(out, product)


def finish_norm(nc, name, X, XT, ident, residual, total=None, base=None, out=None, also=None, eps=EPS5,
                scale=None, bias=None, loads=(), last=False):
    XT = None if last else XT
    total = total or (lambda t: X[:, t, :])
    base = base or (lambda t: X[:, t, :])
    out = out or (lambda t: X[:, t, :])
    RB, LAG = 4, 3
    with Stage(nc, name) as st:
        R = st.ps("R", [P, RB, 512])
        TP = st.ps("TP", [P, 2, 512])
        raw = st.sb("raw", [P, 6])
        MV = st.sb("MV", [P, NT, 2])
        RS = st.sb("RS", [P, NT])
        loaded = st.sem("loaded")
        stats_ready = st.sem("stats_ready")
        std_ready = st.sem("std_ready")
        residual_ready = st.sem("residual_ready")
        residual_read = st.sem("residual_read")
        normed = st.sem("normed")
        turned = st.sem("turned")
        turned_read = st.sem("turned_read")
        dve_chain = st.sem("dve_chain")
        with st.block() as block:
            @block.sync
            def _(sp):
                for dst, src in loads:
                    sp.dma_start(dst, src).then_inc(loaded, 16)

            @block.tensor
            def _(pe):
                if loads:
                    pe.wait_ge(loaded, 16 * len(loads))
                for t in range(NT + LAG):
                    if t < NT and residual:
                        if t >= RB:
                            pe.wait_ge(residual_read, t - RB + 1)
                        residual(pe, t, R[:, t % RB, 0:D]).then_inc(residual_ready, 1)
                    if t >= LAG and XT is not None:
                        u = t - LAG
                        pe.wait_ge(normed, u + 1)
                        if u >= 2:
                            pe.wait_ge(turned_read, u - 1)
                        for k in range(KD):
                            ins = pe.transpose(TP[:, u % 2, k * P:(k + 1) * P], out(u)[:, k * P:(k + 1) * P], ident[:, 0:P])
                        ins.then_inc(turned, 1)

            @block.vector
            def _(v):
                ch = Chain(v, dve_chain)
                for t in range(NT + 1):
                    if t < NT:
                        if residual:
                            v.wait_ge(residual_ready, t + 1)
                            v.tensor_tensor(total(t), R[:, t % RB, 0:D], base(t), ALU.add).then_inc(residual_read, 1)
                            v.wait_ge(residual_read, t + 1)
                        elif base(t) is not None:
                            ch.link(v.tensor_tensor(total(t), X[:, t, :], base(t), ALU.add))
                        if also:
                            ch.link(v.tensor_tensor(also(t), also(t), total(t), ALU.add))
                        norm_stats(v, ch, total(t), raw[:], MV[:, t, :]).then_inc(stats_ready, 1)
                        v.wait_ge(stats_ready, t + 1)
                    if t >= 1:
                        u = t - 1
                        v.wait_ge(std_ready, u + 1)
                        ch.link(v.reciprocal(RS[:, u:u + 1], RS[:, u:u + 1]))
                        v.tensor_scalar(out(u), total(u), MV[:, u, 0:1], RS[:, u:u + 1], ALU.subtract, ALU.mult).then_inc(normed, 1)

            @block.scalar
            def _(act):
                if loads:
                    act.wait_ge(loaded, 16 * len(loads))
                for t in range(NT + 2):
                    if t < NT:
                        act.wait_ge(stats_ready, t + 1)
                        act.activation(RS[:, t:t + 1], MV[:, t, 1:2], ACT.Sqrt, bias=ident[:, eps:eps + 1]).then_inc(std_ready, 1)
                    if t >= 2 and XT is not None:
                        u = t - 2
                        act.wait_ge(turned, u + 1)
                        if scale is None:
                            act.activation(XT[:, :, u * P:(u + 1) * P], TP[:, u % 2, 0:D].rearrange("p (k n) -> p k n", k=KD),
                                           ACT.Copy).then_inc(turned_read, 1)
                        else:
                            for k in range(KD):
                                ins = act.activation(XT[:, k, u * P:(u + 1) * P], TP[:, u % 2, k * P:(k + 1) * P],
                                                     ACT.Identity, scale=scale[:, k:k + 1], bias=bias[:, k:k + 1])
                            ins.then_inc(turned_read, 1)


DI, DS, DC = 512, 16, 4
NCH = DI // P
HALF = T // 2
NPASS = NCH * 2
BF16_ONE = 0x3F80


def stage_mamba(nc, io, X, XT, ident, KF):
    with ExitStack() as outer:
        U = outer.enter_context(nc.sbuf_tensor("mamba_U", [P, NPASS, HALF], F32))
        WO = outer.enter_context(nc.sbuf_tensor("mamba_WO", [P, NCH, D], F32))
        with Stage(nc, "mamba") as st:
            DU = st.sb("DU", [P, NPASS, HALF])
            E = st.sb("E", [P, NPASS, HALF])
            BC = st.sb("BC", [96, T], BF16)
            WD = st.sb("WD", [P, NCH, P])
            WBC = st.sb("WBC", [P, NCH, 96])
            SEL = st.sb("SEL", [96, 2 * DS, P], BF16)
            CW = st.sb("CW", [P, NCH, DC])
            VEC = st.sb("VEC", [P, 4, NCH])
            AA = st.sb("AA", [P, NPASS, DS])
            DV = st.sb("DV", [P, NPASS])
            with Stage(nc, "mamba_in") as s2:
                W = s2.sb("W", [P, KD, 2 * DI])
                SIL = s2.sb("SIL", [P, 2, G4])
                CV = s2.sb("CV", [P, 2, G4])
                R1 = s2.sb("R1", [96, 2, G4])
                MID = s2.sb("MID", [96, G4], BF16)
                UP = s2.ps("UP", [P, 2, G4])
                ZP = s2.ps("ZP", [P, 2, G4])
                PP = s2.ps("PP", [P, G4])
                DP = s2.ps("DP", [P, G4])
                loaded = s2.sem("loaded")
                uz_ready = s2.sem("uz_ready")
                u_read = s2.sem("u_read")
                silu_ready = s2.sem("silu_ready")
                gated = s2.sem("gated")
                proj_ready = s2.sem("proj_ready")
                bc_read = s2.sem("bc_read")
                exp_ready = s2.sem("exp_ready")
                a_exp = s2.sem("a_exp")
                dve_chain = s2.sem("dve_chain")
                NG = T // G4

                def group(buf, c, g):
                    return buf[:, 2 * c + g // 2, (g % 2) * G4:(g % 2 + 1) * G4]

                with s2.block() as block:
                    @block.sync
                    def _(sp):
                        sp.dma_start(W[:], io["L0_attn_in_projT"].rearrange("(k p) n -> p k n", p=P)).then_inc(loaded, 16)
                        sp.dma_start(WO[:], io["L0_attn_out_projT"].rearrange("(k p) n -> p k n", p=P)).then_inc(loaded, 16)
                        sp.dma_start(WD[:], io["L0_attn_x_delta"].rearrange("(k p) n -> p k n", p=P)).then_inc(loaded, 16)
                        sp.dma_start(WBC[:], io["L0_attn_x_bc"].rearrange("(k p) n -> p k n", p=P)).then_inc(loaded, 16)
                        sp.dma_start(SEL[:].bitcast(mybir.dt.uint16), io["sel_bc"]).then_inc(loaded, 16)
                        sp.dma_start(CW[:], io["L0_attn_conv_w"].rearrange("(k p) o n -> p k (o n)", p=P)).then_inc(loaded, 16)
                        sp.dma_start(VEC[:], io["L0_attn_vec"]).then_inc(loaded, 16)
                        for h in range(2):
                            sp.dma_start(AA[:].rearrange("p (c h) s -> p h c s", h=2)[:, h],
                                         io["L0_attn_A_log"].rearrange("(k p) s -> p k s", p=P)).then_inc(loaded, 16)

                    NLOAD = 9 * 16

                    @block.tensor
                    def _(pe):
                        pe.wait_ge(loaded, NLOAD)
                        for g in range(NG):
                            for c in range(NCH):
                                n = g * NCH + c
                                if n >= 2:
                                    pe.wait_ge(u_read, n - 1)
                                    pe.wait_ge(silu_ready, n - 1)
                                for dst, col in ((UP, c * P), (ZP, DI + c * P)):
                                    for k in range(KD):
                                        ins = pe.matmul(dst[:, n % 2, :], W[:, k, col:col + P], XT[:, k, g * G4:(g + 1) * G4],
                                                        start=(k == 0), stop=(k == KD - 1))
                                ins.then_inc(uz_ready, 1)
                            pe.wait_ge(gated, (g + 1) * NCH)
                            if g:
                                pe.wait_ge(bc_read, g)
                                pe.wait_ge(exp_ready, g * NCH)
                            for dst, w, m in ((PP, WBC, 96), (DP, WD, P)):
                                for c in range(NCH):
                                    ins = pe.matmul(dst[0:m, :], w[:, c, :], group(U, c, g), start=(c == 0), stop=(c == NCH - 1))
                            ins.then_inc(proj_ready, 1)

                    @block.scalar
                    def _(act):
                        act.wait_ge(loaded, NLOAD)
                        act.activation(AA[:], AA[:], ACT.Exp).then_inc(a_exp, 1)
                        for g in range(NG):
                            for c in range(NCH):
                                n = g * NCH + c
                                act.wait_ge(uz_ready, n + 1)
                                if n >= 2:
                                    act.wait_ge(gated, n - 1)
                                act.activation(SIL[:, n % 2, :], ZP[:, n % 2, :], ACT.Silu).then_inc(silu_ready, 1)
                            act.wait_ge(proj_ready, g + 1)
                            for c in range(NCH):
                                act.activation(group(E, c, g), DP[:], ACT.Exp, scale=VEC[:, 1, c:c + 1],
                                               bias=VEC[:, 2, c:c + 1]).then_inc(exp_ready, 1)

                    @block.vector
                    def _(v):
                        ch = Chain(v, dve_chain)
                        v.wait_ge(loaded, NLOAD)
                        v.wait_ge(a_exp, 1)
                        ch.link(v.tensor_scalar(AA[:], AA[:], -1.0, -3e38, ALU.mult, ALU.max))
                        for h in range(2):
                            ch.link(v.tensor_copy(DV[:].rearrange("p (c h) -> p h c", h=2)[:, h], VEC[:, 3, :]))
                        for g in range(NG):
                            for c in range(NCH):
                                n = g * NCH + c
                                v.wait_ge(uz_ready, n + 1)
                                cv = CV[:, n % 2, :]
                                ch.link(v.tensor_scalar(cv, UP[:, n % 2, :], CW[:, c, DC - 1:DC], VEC[:, 0, c:c + 1], ALU.mult, ALU.add))
                                for s in range(1, DC):
                                    o = cv.rearrange("p (b t) -> p b t", t=S)[:, :, s:]
                                    i = UP[:, n % 2, :].rearrange("p (b t) -> p b t", t=S)[:, :, 0:S - s]
                                    ch.link(v.scalar_tensor_tensor(o, i, CW[:, c, DC - 1 - s:DC - s], o, ALU.mult, ALU.add))
                                v.sem_inc(u_read, 1)
                                v.wait_ge(silu_ready, n + 1)
                                v.tensor_tensor(group(U, c, g), cv, SIL[:, n % 2, :], ALU.mult).then_inc(gated, 1)
                            v.wait_ge(gated, (g + 1) * NCH)
                            v.wait_ge(proj_ready, g + 1)
                            bc = BC[:, g * G4:(g + 1) * G4]
                            ch.link(v.tensor_copy(bc, PP[0:96, :]))
                            ch.link(v.tensor_tensor(R1[:, 0, :], PP[0:96, :], bc, ALU.subtract))
                            v.sem_inc(bc_read, 1)
                            ch.link(v.tensor_copy(MID[:], R1[:, 0, :]))
                            ch.link(v.tensor_tensor(R1[:, 1, :], R1[:, 0, :], MID[:], ALU.subtract))
                            ch.link(v.tensor_copy(bc[32:64], MID[32:64, :]))
                            ch.link(v.tensor_copy(bc[64:96], R1[64:96, 1, :]))
                            for c in range(NCH):
                                v.wait_ge(exp_ready, g * NCH + c + 1)
                                ch.link(v.scalar_tensor_tensor(group(DU, c, g), group(E, c, g), 1.0, group(U, c, g), ALU.add, ALU.mult))

            with Stage(nc, "scan") as s3:
                AB = s3.sb("AB", [P, 2, HALF])
                BU = s3.sb("BU", [P, 2, HALF])
                H = s3.sb("H", [P, 3, HALF])
                CS = s3.sb("CS", [P, 3, HALF])
                HC = s3.sb("HC", [P, 2, HALF])
                YP = s3.ps("YP", [P, HALF])
                BP = s3.ps("BP", [P, 2, HALF])
                CP = s3.ps("CP", [P, HALF])
                zeroed = s3.sem("zeroed")
                b_ready = s3.sem("b_ready")
                c_ready = s3.sem("c_ready")
                decay_ready = s3.sem("decay_ready")
                c_copied = s3.sem("c_copied")
                bu_ready = s3.sem("bu_ready")
                h_ready = s3.sem("h_ready")
                hc_ready = s3.sem("hc_ready")
                y_added = s3.sem("y_added")
                y_read = s3.sem("y_read")
                NH = HALF // G4
                with s3.block() as block:
                    @block.gpsimd
                    def _(pool):
                        pool.memset(AB[:], 0.0).then_inc(zeroed, 1)
                        for i in range(NPASS):
                            for s in range(DS):
                                n = i * DS + s
                                pool.wait_ge(h_ready, n + 1)
                                pool.wait_ge(c_copied, n + 1)
                                if n >= 2:
                                    pool.wait_ge(y_added, n - 1)
                                pool.tensor_tensor(HC[:, n % 2, :], H[:, n % 3, :], CS[:, n % 3, :], ALU.mult).then_inc(hc_ready, 1)

                    @block.tensor
                    def _(pe):
                        def spread(n):
                            i, s = n // DS, n % DS
                            tok = (i % 2) * HALF
                            if n >= 2:
                                pe.wait_ge(bu_ready, n - 1)
                            for q in range(NH):
                                ins = pe.matmul(BP[:, n % 2, q * G4:(q + 1) * G4], SEL[:, s, :], BC[:, tok + q * G4:tok + (q + 1) * G4],
                                                start=True, stop=True)
                            ins.then_inc(b_ready, 1)
                            if n >= 1:
                                pe.wait_ge(c_copied, n)
                            for q in range(NH):
                                ins = pe.matmul(CP[:, q * G4:(q + 1) * G4], SEL[:, DS + s, :], BC[:, tok + q * G4:tok + (q + 1) * G4],
                                                start=True, stop=True)
                            ins.then_inc(c_ready, 1)

                        N = NPASS * DS
                        spread(0)
                        spread(1)
                        for n in range(N):
                            i, s = n // DS, n % DS
                            if n + 2 < N:
                                spread(n + 2)
                            pe.wait_ge(hc_ready, n + 1)
                            if i and s == 0:
                                pe.wait_ge(y_read, i)
                            for q in range(NH):
                                ins = pe.matmul(YP[:, q * G4:(q + 1) * G4], ident[:, 0:P], HC[:, n % 2, q * G4:(q + 1) * G4],
                                                start=(s == 0), stop=(s == DS - 1))
                            ins.then_inc(y_added, 1)

                    @block.scalar
                    def _(act):
                        act.wait_ge(zeroed, 1)
                        for i in range(NPASS):
                            for s in range(DS):
                                n = i * DS + s
                                if n >= 2:
                                    act.wait_ge(h_ready, n - 1)
                                ab = AB[:, n % 2, :].rearrange("p (b t) -> p b t", t=S)[:, :, 1:]
                                e = E[:, i, :].rearrange("p (b t) -> p b t", t=S)[:, :, 1:]
                                act.activation(ab, e, ACT.Exp, scale=AA[:, i, s:s + 1], bias=AA[:, i, s:s + 1]).then_inc(decay_ready, 1)
                                act.wait_ge(c_ready, n + 1)
                                if n >= 3:
                                    act.wait_ge(hc_ready, n - 2)
                                act.activation(CS[:, n % 3, :], CP[:], ACT.Copy).then_inc(c_copied, 1)

                    @block.vector
                    def _(v):
                        for i in range(NPASS):
                            for s in range(DS):
                                n = i * DS + s
                                v.wait_ge(b_ready, n + 1)
                                if n >= 2:
                                    v.wait_ge(h_ready, n - 1)
                                v.tensor_tensor(BU[:, n % 2, :], DU[:, i, :], BP[:, n % 2, :], ALU.mult).then_inc(bu_ready, 1)
                                v.wait_ge(bu_ready, n + 1)
                                v.wait_ge(decay_ready, n + 1)
                                if n >= 3:
                                    v.wait_ge(hc_ready, n - 2)
                                v.tensor_tensor_scan(H[:, n % 3, :], AB[:, n % 2, :], BU[:, n % 2, :], 0.0, ALU.mult, ALU.add).then_inc(h_ready, 1)
                            v.wait_ge(y_added, (i + 1) * DS)
                            v.scalar_tensor_tensor(U[:, i, :], U[:, i, :], DV[:, i:i + 1], YP[:], ALU.mult, ALU.add).then_inc(y_read, 1)

        def out_product(pe, t, out):
            h, col = t // (NT // 2), (t % (NT // 2)) * P
            for c in range(NCH):
                ins = pe.matmul(out, U[:, 2 * c + h, col:col + P], WO[:, c, :], start=(c == 0), stop=(c == NCH - 1))
            return ins

        finish_norm(nc, "mamba_norm", X, XT, ident, out_product)


NHEAD, DH = 8, 64
INNER = NHEAD * DH
NIN = INNER // P
DCTX = 192
KC = [P, DCTX - P]


def load_context(io, CT):
    return [(CT[0:KC[k], k, :], io["ctxT"][k * P:k * P + KC[k], :]) for k in range(2)]


def load_split(W, src):
    return [(W[0:KC[k], k, :], src[k * P:k * P + KC[k], :]) for k in range(2)]


def stage_xattn(nc, io, X, XT, ident, KF):
    with Stage(nc, "xa") as st:
        QT = st.sb("QT", [P, NIN, T])
        WO = st.sb("WO", [P, NIN, D])
        BO = st.sb("BO", [1, D])
        with Stage(nc, "xb") as s1:
            KT = s1.sb("KT", [P, NIN, T])
            V = s1.sb("V", [P, NT, INNER])
            with Stage(nc, "xc") as s2:
                CT = s2.sb("CT", [P, 2, T])
                WQ = s2.sb("WQ", [P, KD, INNER])
                WK = s2.sb("WK", [P, 2, INNER])
                WV = s2.sb("WV", [P, 2, INNER])
                loads = load_context(io, CT) + load_split(WK, io["L0_xattn_Wk"]) + load_split(WV, io["L0_xattn_Wv"]) + [
                    (WQ[:], io["L0_xattn_Wq"].rearrange("(k p) n -> p k n", p=P)),
                    (WO[:], io["L0_xattn_Wo"].rearrange("(k p) n -> p k n", p=P)), (BO[:], io["L0_xattn_bo"])]
                jobs = []
                for g in range(T // G4):
                    tok = slice(g * G4, (g + 1) * G4)
                    for c in range(NIN):
                        col = slice(c * P, (c + 1) * P)
                        jobs.append((QT[:, c, tok], [(WQ[:, k, col], XT[:, k, tok]) for k in range(KD)], copy_out))
                        jobs.append((KT[:, c, tok], [(WK[0:KC[k], k, col], CT[0:KC[k], k, tok]) for k in range(2)], copy_out))
                for t in range(NT):
                    jobs.append((V[:, t, :], [(CT[0:KC[k], k, t * P:(t + 1) * P], WV[0:KC[k], k, :]) for k in range(2)], copy_out))
                products(nc, "xproj", jobs, loads)

            attention(nc, ident, QT, KT, V)

        def out_product(pe, t, out):
            for c in range(NIN):
                pe.matmul(out, QT[:, c, t * P:(t + 1) * P], WO[:, c, :], start=(c == 0), stop=False)
            return add_bias(pe, ident, out, BO[:])

        finish_norm(nc, "xnorm", X, XT, ident, out_product)


def attention(nc, ident, QT, KT, V):
    NU = B * NIN
    SCALE = float(DH) ** -0.5
    with Stage(nc, "attn") as st:
        PR = st.sb("PR", [P, 2, 4, S])
        PN = st.sb("PN", [P, 2, 4, S])
        PT = st.sb("PT", [P, 2, 2, 2, S])
        MX = st.sb("MX", [P, NU, 4])
        SM = st.sb("SM", [P, NU, 4])
        SC = st.ps("SC", [P, 2, 4, S])
        TP = st.ps("TP", [P, 2, 2, S])
        OT = st.ps("OT", [P, 2, 512])
        scores_ready = st.sem("scores_ready")
        max_ready = st.sem("max_ready")
        exp_ready = st.sem("exp_ready")
        sum_ready = st.sem("sum_ready")
        probs_ready = st.sem("probs_ready")
        turned = st.sem("turned")
        turned_act = st.sem("turned_act")
        turned_dve = st.sem("turned_dve")
        out_ready = st.sem("out_ready")
        out_copied = st.sem("out_copied")
        dve_chain = st.sem("dve_chain")
        with st.block() as block:
            @block.tensor
            def _(pe):
                def scores(m):
                    b, c = m // NIN, m % NIN
                    if m >= 2:
                        pe.wait_ge(exp_ready, m - 1)
                    for t in range(2):
                        for h in range(2):
                            r = slice(h * DH, (h + 1) * DH)
                            ins = pe.matmul(SC[:, m % 2, 2 * h + t, :], QT[r, c, b * S + t * P:b * S + (t + 1) * P],
                                            KT[r, c, b * S:(b + 1) * S], start=True, stop=True)
                    ins.then_inc(scores_ready, 1)

                def values(m):
                    b, c = m // NIN, m % NIN
                    pe.wait_ge(turned_act, m + 1)
                    pe.wait_ge(turned_dve, m + 1)
                    if m >= 2:
                        pe.wait_ge(out_copied, m - 1)
                    for h in range(2):
                        for k in range(2):
                            ins = pe.matmul(OT[h * DH:(h + 1) * DH, m % 2, 0:S], V[:, 2 * b + k, c * P + h * DH:c * P + (h + 1) * DH],
                                            PT[:, m % 2, h, k, :], start=(k == 0), stop=(k == 1))
                    ins.then_inc(out_ready, 1)

                scores(0)
                scores(1)
                for m in range(NU):
                    if m + 2 < NU:
                        scores(m + 2)
                    pe.wait_ge(probs_ready, m + 1)
                    if m:
                        pe.wait_ge(turned_act, m)
                        pe.wait_ge(turned_dve, m)
                    for h in range(2):
                        for k in range(2):
                            for t in range(2):
                                ins = pe.transpose(TP[:, h, k, t * P:(t + 1) * P], PN[:, m % 2, 2 * h + t, k * P:(k + 1) * P], ident[:, 0:P])
                        ins.then_inc(turned, 1)
                    if m:
                        values(m - 1)
                values(NU - 1)

            @block.scalar
            def _(act):
                def exps(m):
                    act.wait_ge(max_ready, m + 1)
                    if m >= 2:
                        act.wait_ge(probs_ready, m - 1)
                    for j in range(4):
                        ins = act.activation(PR[:, m % 2, j, :], SC[:, m % 2, j, :], ACT.Exp, scale=SCALE,
                                             bias=MX[:, m, j:j + 1], accum_out=SM[:, m, j:j + 1])
                    ins.then_inc(exp_ready, 1)

                def out_copy(m):
                    act.wait_ge(out_ready, m + 1)
                    b, c = m // NIN, m % NIN
                    act.activation(QT[:, c, b * S:(b + 1) * S], OT[:, m % 2, 0:S], ACT.Copy).then_inc(out_copied, 1)

                exps(0)
                for m in range(NU):
                    if m + 1 < NU:
                        exps(m + 1)
                    act.wait_ge(turned, 2 * m + 1)
                    if m >= 2:
                        act.wait_ge(out_ready, m - 1)
                    act.activation(PT[:, m % 2, 0], TP[:, 0], ACT.Copy).then_inc(turned_act, 1)
                    if m:
                        out_copy(m - 1)
                out_copy(NU - 1)


            @block.gpsimd
            def _(pool):
                for m in range(NU):
                    pool.wait_ge(sum_ready, m + 1)
                    if m >= 2:
                        pool.wait_ge(turned, 2 * (m - 1))
                    pool.tensor_tensor(PN[:, m % 2], PR[:, m % 2], SM[:, m, :].rearrange("p (j o) -> p j o", o=1).to_broadcast([P, 4, S]),
                                       ALU.mult).then_inc(probs_ready, 1)

            @block.vector
            def _(v):
                ch = Chain(v, dve_chain)

                def maxima(m):
                    v.wait_ge(scores_ready, m + 1)
                    ch.link(v.tensor_reduce(MX[:, m, :], SC[:, m % 2], AX_X, ALU.max))
                    v.tensor_scalar(MX[:, m, :], MX[:, m, :], -SCALE, None, ALU.mult).then_inc(max_ready, 1)

                def sums(m):
                    v.wait_ge(exp_ready, m + 1)
                    v.reciprocal(SM[:, m, :], SM[:, m, :]).then_inc(sum_ready, 1)

                maxima(0)
                maxima(1)
                sums(0)
                for m in range(NU):
                    if m + 2 < NU:
                        maxima(m + 2)
                    if m + 1 < NU:
                        sums(m + 1)
                    v.wait_ge(turned, 2 * m + 2)
                    if m >= 2:
                        v.wait_ge(out_ready, m - 1)
                    v.tensor_copy(PT[:, m % 2, 1], TP[:, 1]).then_inc(turned_dve, 1)


NE, HID = 16, 1024
CAP = int(1.25 * T / NE)
SLOTS = NE * CAP
HC_ = CAP // 2
NHID = HID // P


NST = 64
LO = 16
NF = 2 * 2
MAGIC = 1.5 * 2 ** 23
TURN = 6.2831845
HI = S // LO
LB = P // HI


class S4dTables:

    def __init__(self, keep, st, io):
        self.io = io
        self.UU = keep.sb("UU", [P, D, LO])
        self.VV = keep.sb("VV", [P, D, LO])
        self.U2 = st.sb("U2", [P, D, LO])
        self.TT = st.sb("TT", [P, D, LO])
        self.HIGH = st.sb("HIGH", [P, D, LO])
        self.LOW = st.sb("LOW", [P, D, LO])
        self.PAR = st.sb("PAR", [P, 5, D])
        self.COL = st.sb("COL", [P, 4])
        self.AR = st.sb("AR", [P, D])
        self.AI = st.sb("AI", [P, D])
        self.W = st.sb("W", [P, 12, D])
        self.loaded = st.sem("tables_loaded")
        self.dt_ready = st.sem("dt_ready")
        self.exponents_ready = st.sem("exponents_ready")
        self.tanh_ready = st.sem("tanh_ready")
        self.phases_ready = st.sem("phases_ready")
        self.small_sines = st.sem("small_sines")
        self.moduli_ready = st.sem("moduli_ready")
        self.fraction_ready = st.sem("fraction_ready")
        self.sine_ready = st.sem("sine_ready")
        self.factor_ready = st.sem("factor_ready")
        self.pool_chain = st.sem("tables_pool_chain")
        self.small_chain = st.sem("tables_small_chain")

    def load(self, sp):
        sp.dma_start(self.PAR[:], self.io["L1_xattn_s4d"]).then_inc(self.loaded, 16)
        sp.dma_start(self.COL[:], self.io["phases"]).then_inc(self.loaded, 16)

    def powers(self, act, out, x, func, step, bias=0.0):
        for l in range(LO):
            ins = act.activation(out[:, :, l], x[:], func, scale=float(step * l), bias=bias)
        return ins

    def scalar_step(self, act, n):
        if n == 0:
            act.wait_ge(self.loaded, 32)
            act.activation(self.PAR[:, 0, :], self.PAR[:, 0, :], ACT.Exp).then_inc(self.dt_ready, 1)
            act.wait_ge(self.exponents_ready, 1)
            act.activation(self.W[:, 0, :], self.AR[:], ACT.Tanh, scale=0.5).then_inc(self.tanh_ready, 1)
            self.powers(act, self.UU, self.AI, ACT.Identity, LO, self.COL[:, 0:1]).then_inc(self.phases_ready, 1)
        elif n == 1:
            self.powers(act, self.U2, self.AI, ACT.Identity, LO, self.COL[:, 1:2]).then_inc(self.phases_ready, 1)
        elif n == 2:
            self.powers(act, self.VV, self.AI, ACT.Identity, 1, self.COL[:, 2:3]).then_inc(self.phases_ready, 1)
        elif n == 3:
            act.wait_ge(self.exponents_ready, 2)
            act.activation(self.W[:, 1:4, :], self.W[:, 1:4, :], ACT.Sin, scale=TURN).then_inc(self.small_sines, 1)
        elif n == 4:
            self.powers(act, self.HIGH, self.AR, ACT.Exp, LO).then_inc(self.moduli_ready, 1)
        elif n == 5:
            self.powers(act, self.LOW, self.AR, ACT.Exp, 1).then_inc(self.moduli_ready, 1)
        elif n in (7, 8, 9):
            act.wait_ge(self.fraction_ready, n - 6)
            x = (self.UU, self.U2, self.VV)[n - 7]
            act.activation(x[:], x[:], ACT.Sin, scale=TURN).then_inc(self.sine_ready, 1)

    def exponents(self, v):
        ch = self.small = Chain(v, self.small_chain)
        v.wait_ge(self.loaded, 32)
        v.wait_ge(self.dt_ready, 1)
        ch.link(v.tensor_tensor(self.AR[:], self.PAR[:, 1, :], self.PAR[:, 0, :], ALU.mult))
        ch.link(v.tensor_tensor(self.AI[:], self.PAR[:, 2, :], self.PAR[:, 0, :], ALU.mult))
        v.tensor_scalar(self.AI[:], self.AI[:], 1.0 / (2 * np.pi), None, ALU.mult).then_inc(self.exponents_ready, 1)
        v.wait_ge(self.exponents_ready, 1)
        W = self.W
        v.tensor_scalar(W[:, 1, :], self.AI[:], 0.25, None, ALU.add)
        v.tensor_copy(W[:, 2, :], self.AI[:])
        ch.link(v.tensor_scalar(W[:, 3, :], self.AI[:], 0.5, None, ALU.mult))
        ch.link(v.tensor_scalar(W[:, 4:7, :], W[:, 1:4, :], MAGIC, None, ALU.add))
        ch.link(v.tensor_scalar(W[:, 4:7, :], W[:, 4:7, :], MAGIC, None, ALU.subtract))
        v.tensor_tensor(W[:, 1:4, :], W[:, 1:4, :], W[:, 4:7, :], ALU.subtract).then_inc(self.exponents_ready, 1)

    def combine(self, v, out, a, b, c, d, op):
        t11, t4 = self.W[:, 11, :], self.W[:, 4, :]
        v.tensor_tensor(t11, a, b, ALU.mult)
        self.small.link(v.tensor_tensor(t4, c, d, ALU.mult))
        self.small.link(v.tensor_tensor(out, t11, t4, op))

    def factor_step(self, v, n):
        ch = self.small
        th, s1, s2, s3, t4, t5, er, ei, nr, ni, a2, t11 = (self.W[:, i, :] for i in range(12))
        Ar, Ai, Cr, Ci = (self.PAR[:, i, :] for i in range(1, 5))
        if n == 0:
            v.wait_ge(self.tanh_ready, 1)
            v.wait_ge(self.small_sines, 1)
            ch.link(v.tensor_scalar(t4, th, -1.0, 1.0, ALU.mult, ALU.add))
            ch.link(v.reciprocal(t4, t4))
            v.tensor_tensor(s3, s3, s3, ALU.mult)
            ch.link(v.scalar_tensor_tensor(t5, th, 2.0, t4, ALU.mult, ALU.mult))
            ch.link(v.tensor_tensor(er, t5, s1, ALU.mult))
            v.scalar_tensor_tensor(ei, t5, 1.0, s2, ALU.add, ALU.mult)
            ch.link(v.scalar_tensor_tensor(er, s3, -2.0, er, ALU.mult, ALU.add))
        elif n == 1:
            self.combine(v, nr, Cr, er, Ci, ei, ALU.subtract)
            self.combine(v, ni, Cr, ei, Ci, er, ALU.add)
            self.combine(v, a2, Ar, Ar, Ai, Ai, ALU.add)
        elif n == 2:
            ch.link(v.reciprocal(a2, a2))
            self.combine(v, er, nr, Ar, ni, Ai, ALU.add)
            self.combine(v, ei, ni, Ar, nr, Ai, ALU.subtract)
            ch.link(v.tensor_tensor(er, er, a2, ALU.mult))
            v.tensor_tensor(ei, ei, a2, ALU.mult).then_inc(self.factor_ready, 1)

    def gpsimd_program(self, pool):
        ch = Chain(pool, self.pool_chain)

        def wide(x):
            return x.rearrange("p (d o) -> p d o", o=1).to_broadcast([P, D, LO])

        for n, x in enumerate((self.UU, self.U2, self.VV)):
            pool.wait_ge(self.phases_ready, n + 1)
            ch.link(pool.tensor_scalar(self.TT[:], x[:], MAGIC, None, ALU.add))
            ch.link(pool.tensor_scalar(self.TT[:], self.TT[:], MAGIC, None, ALU.subtract))
            pool.tensor_tensor(x[:], x[:], self.TT[:], ALU.subtract).then_inc(self.fraction_ready, 1)
            pool.wait_ge(self.fraction_ready, n + 1)
        pool.wait_ge(self.moduli_ready, 2)
        for n, (x, modulus) in enumerate(((self.UU, self.HIGH), (self.U2, self.HIGH), (self.VV, self.LOW))):
            pool.wait_ge(self.sine_ready, n + 1)
            ch.link(pool.tensor_tensor(x[:], x[:], modulus[:], ALU.mult))
        pool.wait_ge(self.factor_ready, 1)
        er, ei = self.W[:, 6, :], self.W[:, 7, :]
        pool.tensor_tensor(self.UU[:], self.UU[:], wide(er), ALU.mult)
        ch.link(pool.tensor_tensor(self.U2[:], self.U2[:], wide(ei), ALU.mult))
        pool.tensor_tensor(self.UU[:], self.UU[:], self.U2[:], ALU.add)


def combine(nc, io, tables, answers, FROM, WT, GA, KF):
    with Stage(nc, "combine") as st:
        WK = st.sb("WK", [P, LO // LB, NF, P])
        KA = st.sb("KA", [HI, LO, D])
        KB = st.sb("KB", [P, LO // LB, D])
        KP = st.ps("KP", [P, 8, 512])
        gathered = st.sem("gathered")
        loaded = st.sem("loaded")
        k_ready = st.sem("k_ready")
        k_copied = st.sem("k_copied")
        k_moved = st.sem("k_moved")
        kf_ready = st.sem("kf_ready")
        DB = 512 // LO
        with st.block() as block:
            @block.gpsimd
            def _(pool):
                for t in range(NT):
                    pool.indirect_dma_start(out=GA[:, t, :], out_offset=None, in_=answers,
                                            in_offset=bass.IndirectOffsetOnAxis(ap=FROM[:, t:t + 1], axis=0)).then_inc(gathered, 16)
                pool.wait_ge(gathered, 16 * NT)

            @block.sync
            def _(sp):
                sp.dma_start(WK[:], io["dft_kernel"]).then_inc(loaded, 16)
                sp.wait_ge(k_copied, 8)
                for l in range(LO):
                    sp.dma_start(KB[l % LB * HI:(l % LB + 1) * HI, l // LB, :], KA[:, l, :]).then_inc(k_moved, 16)

            @block.tensor
            def _(pe):
                for d in range(D):
                    ins = pe.matmul(KP[0:HI, d // DB, d % DB * LO:(d % DB + 1) * LO], tables.UU[:, d, :], tables.VV[:, d, :], start=True, stop=True)
                    if d % DB == DB - 1:
                        ins.then_inc(k_ready, 1)
                pe.wait_ge(k_copied, 8)
                pe.wait_ge(loaded, 16)
                pe.wait_ge(k_moved, 16 * LO)
                for q in range(NF):
                    for i in range(LO // LB):
                        ins = pe.matmul(KP[:, q, 0:D], WK[:, i, q, :], KB[:, i, :], start=(i == 0), stop=(i == LO // LB - 1))
                    ins.then_inc(kf_ready, 1)

            @block.vector
            def _(v):
                for n in range(8):
                    v.wait_ge(k_ready, n + 1)
                    v.tensor_scalar(KA[:, :, n * DB:(n + 1) * DB].rearrange("p l d -> p d l"),
                                    KP[0:HI, n, :].rearrange("p (d l) -> p d l", l=LO), 2.0, None, ALU.mult).then_inc(k_copied, 1)
                for q in range(NF):
                    v.wait_ge(kf_ready, q + 1)
                    v.tensor_copy(KF[:, q, :], KP[:, q, 0:D])

            @block.scalar
            def _(act):
                act.wait_ge(gathered, 16 * NT)
                for t in range(NT):
                    act.activation(GA[:, t, :], GA[:, t, :], ACT.Copy, scale=WT[:, t:t + 1])


def stage_moe(nc, io, X, XT, ident, KF):
    dispatch = nc.dram_tensor("moe_dispatch", (SLOTS + T, D), F32).ap()
    answers = nc.dram_tensor("moe_answers", (SLOTS, D), F32).ap()
    with Stage(nc, "moe") as st:
        TO = st.sb("TO", [P, NT], I32)
        FROM = st.sb("FROM", [P, NT], I32)
        WT = st.sb("WT", [P, NT])
        moe_route(nc, io, X, XT, ident, TO, FROM, WT, dispatch)
        with Stage(nc, "s4") as keep:
            with Stage(nc, "s4t") as s1:
                tables = S4dTables(keep, s1, io)
                moe_experts(nc, io, ident, dispatch, answers, tables)
            GA = keep.sb("GA", [P, NT, D])
            combine(nc, io, tables, answers, FROM, WT, GA, KF)
            finish_norm(nc, "moenorm", X, XT, ident, None, base=lambda t: GA[:, t, :])


def moe_route(nc, io, X, XT, ident, TO, FROM, WT, dispatch):
    with Stage(nc, "route") as st:
        GW = st.sb("GW", [P, KD, NE])
        TRI = st.sb("TRI", [P, 2, P])
        EI = st.sb("EI", [P, NE])
        TI = st.sb("TI", [P, NT])
        ZERO = st.sb("ZERO", [P, SLOTS // P * D])
        MX = st.sb("MX", [P, NT, 8])
        MI = st.sb("MI", [P, NT, 8], U32)
        NM = st.sb("NM", [P, NT])
        EX = st.sb("EX", [P, NT, NE])
        SM = st.sb("SM", [P, NT])
        OH = st.sb("OH", [P, NT, NE])
        RUN = st.sb("RUN", [P, NT, NE])
        TMP = st.sb("TMP", [P, NE])
        FI = st.sb("FI", [P, NT])
        LOC = st.sb("LOC", [P, NT])
        KEEP = st.sb("KEEP", [P, NT])
        FT = st.sb("FT", [P, NT])
        LG = st.ps("LG", [P, NT, NE])
        CS = st.ps("CS", [P, NT, NE])
        loaded = st.sem("loaded")
        zero_ready = st.sem("zero_ready")
        zeroed = st.sem("zeroed")
        logits_ready = st.sem("logits_ready")
        max_ready = st.sem("max_ready")
        exp_ready = st.sem("exp_ready")
        onehot_ready = st.sem("onehot_ready")
        counted = st.sem("counted")
        routed = st.sem("routed")
        sent = st.sem("sent")
        dve_chain = st.sem("dve_chain")
        with st.block() as block:
            @block.sync
            def _(sp):
                sp.dma_start(GW[:], io["L0_ffn_gateT"].rearrange("(k p) n -> p k n", p=P)).then_inc(loaded, 16)
                sp.dma_start(TRI[:], io["tri"]).then_inc(loaded, 16)
                sp.dma_start(EI[:], io["expert_numbers"]).then_inc(loaded, 16)
                sp.dma_start(TI[:], io["spill_rows"]).then_inc(loaded, 16)
                sp.wait_ge(zero_ready, 1)
                sp.dma_start(dispatch[0:SLOTS, :].rearrange("(p r) d -> p (r d)", p=P), ZERO[:]).then_inc(zeroed, 16)

            @block.tensor
            def _(pe):
                pe.wait_ge(loaded, 64)
                for t in range(NT):
                    for k in range(KD):
                        ins = pe.matmul(LG[:, t, :], XT[:, k, t * P:(t + 1) * P], GW[:, k, :], start=(k == 0), stop=(k == KD - 1))
                ins.then_inc(logits_ready, 1)
                pe.wait_ge(onehot_ready, 1)
                for t in range(NT):
                    if t:
                        pe.matmul(CS[:, t, :], TRI[:, 1, :], RUN[:, t, :], start=True, stop=False)
                    ins = pe.matmul(CS[:, t, :], TRI[:, 0, :], OH[:, t, :], start=(t == 0), stop=True)
                ins.then_inc(counted, 1)

            @block.scalar
            def _(act):
                act.wait_ge(max_ready, 1)
                for t in range(NT):
                    ins = act.activation(EX[:, t, :], LG[:, t, :], ACT.Exp, bias=NM[:, t:t + 1], accum_out=SM[:, t:t + 1])
                ins.then_inc(exp_ready, 1)

            @block.vector
            def _(v):
                ch = Chain(v, dve_chain)
                v.memset(ZERO[:], 0.0).then_inc(zero_ready, 1)
                v.wait_ge(loaded, 64)
                v.wait_ge(logits_ready, 1)
                for t in range(NT):
                    ch.link(v.max(MX[:, t, :], LG[:, t, :]))
                    ch.link(v.max_index(MI[:, t, :], MX[:, t, :], LG[:, t, :]))
                v.tensor_scalar(NM[:], MX[:, :, 0], -1.0, None, ALU.mult).then_inc(max_ready, 1)
                ch.link(v.tensor_copy(FI[:], MI[:, :, 0]))
                for t in range(NT):
                    ch.link(v.tensor_scalar(OH[:, t, :], EI[:], FI[:, t:t + 1], None, ALU.is_equal))
                ch.link(v.memset(RUN[:, 0, :], 0.0))
                for t in range(1, NT):
                    ins = v.tensor_tensor(RUN[:, t, :], RUN[:, t - 1, :], OH[:, t - 1, :], ALU.add)
                    ch.link(ins)
                v.sem_inc(onehot_ready, 1)
                v.wait_ge(counted, 1)
                for t in range(NT):
                    ch.link(v.tensor_tensor(TMP[:], OH[:, t, :], CS[:, t, :], ALU.mult))
                    ch.link(v.tensor_reduce(LOC[:, t:t + 1], TMP[:], AX_X, ALU.add))
                ch.link(v.tensor_scalar(LOC[:], LOC[:], 1.0, None, ALU.subtract))
                ch.link(v.tensor_scalar(KEEP[:], LOC[:], float(CAP), None, ALU.is_lt))
                ch.link(v.scalar_tensor_tensor(FI[:], FI[:], float(CAP), LOC[:], ALU.mult, ALU.add))
                ch.link(v.tensor_tensor(FT[:], FI[:], KEEP[:], ALU.mult))
                ch.link(v.tensor_copy(FROM[:], FT[:]))
                ch.link(v.tensor_tensor(FI[:], FI[:], TI[:], ALU.subtract))
                ch.link(v.tensor_tensor(FI[:], FI[:], KEEP[:], ALU.mult))
                ch.link(v.tensor_tensor(FI[:], FI[:], TI[:], ALU.add))
                v.tensor_copy(TO[:], FI[:]).then_inc(routed, 1)
                v.wait_ge(exp_ready, 1)
                ch.link(v.reciprocal(SM[:], SM[:]))
                ch.link(v.tensor_tensor(WT[:], SM[:], KEEP[:], ALU.mult))

            @block.gpsimd
            def _(pool):
                pool.wait_ge(routed, 1)
                pool.wait_ge(zeroed, 16)
                for t in range(NT):
                    pool.indirect_dma_start(out=dispatch, out_offset=bass.IndirectOffsetOnAxis(ap=TO[:, t:t + 1], axis=0),
                                            in_=X[:, t, :], in_offset=None).then_inc(sent, 16)
                pool.wait_ge(sent, 16 * NT)


def moe_experts(nc, io, ident, dispatch, answers, tables):
    with Stage(nc, "experts") as st:
        W1 = st.sb("W1", [P, 2, KD, HID])
        W2 = st.sb("W2", [P, 2, NHID, D])
        XE = st.sb("XE", [HC_, 2, 2, D])
        XET = st.sb("XET", [P, 2, KD, CAP])
        HT = st.sb("HT", [P, 2, NHID, CAP])
        YE = st.sb("YE", [HC_, 2, 2, D])
        TP = st.ps("TP", [P, 2, 512])
        HP = st.ps("HP", [P, 4, 512])
        YP = st.ps("YP", [HC_, 2, 2, D])
        w_loaded = [st.sem(f"w_loaded{i}") for i in range(2)]
        x_loaded = [st.sem(f"x_loaded{i}") for i in range(2)]
        stored = [st.sem(f"stored{i}") for i in range(2)]
        turned = st.sem("turned")
        turned_read = st.sem("turned_read")
        hid_ready = st.sem("hid_ready")
        relu_act = st.sem("relu_act")
        relu_dve = st.sem("relu_dve")
        y_ready = st.sem("y_ready")
        y_copied = st.sem("y_copied")
        with st.block() as block:
            @block.sync
            def _(sp):
                def store(e):
                    sp.wait_ge(y_copied, e + 1)
                    sp.dma_start(answers[e * CAP:(e + 1) * CAP, :].rearrange("(a p) d -> p a d", p=HC_), YE[:, e % 2]).then_inc(stored[e % 2], 16)

                tables.load(sp)
                for e in range(NE):
                    if e >= 2:
                        sp.wait_ge(y_ready, e - 1)
                    sp.dma_start(XE[:, e % 2], dispatch[e * CAP:(e + 1) * CAP, :].rearrange("(a p) d -> p a d", p=HC_)).then_inc(x_loaded[e % 2], 16)
                    sp.dma_start(W1[:, e % 2], io["L0_ffn_w1"][e].rearrange("(k p) n -> p k n", p=P)).then_inc(w_loaded[e % 2], 16)
                    sp.dma_start(W2[:, e % 2], io["L0_ffn_w2"][e].rearrange("(k p) n -> p k n", p=P)).then_inc(w_loaded[e % 2], 16)
                    if e >= 2:
                        store(e - 2)
                store(NE - 2)
                store(NE - 1)
                for i in range(2):
                    sp.wait_ge(stored[i], 16 * (NE // 2))

            @block.tensor
            def _(pe):
                def turn(e):
                    pe.wait_ge(x_loaded[e % 2], 16 * (e // 2 + 1))
                    for k in range(KD):
                        if 2 * e + k >= 2:
                            pe.wait_ge(turned_read, 2 * e + k - 1)
                        for a in range(2):
                            ins = pe.transpose(TP[:, k, a * HC_:(a + 1) * HC_], XE[:, e % 2, a, k * P:(k + 1) * P], ident[0:HC_, 0:HC_])
                        ins.then_inc(turned, 1)

                turn(0)
                for e in range(NE):
                    pe.wait_ge(w_loaded[e % 2], 32 * (e // 2 + 1))
                    pe.wait_ge(turned_read, 2 * (e + 1))
                    for q in range(NHID // 2):
                        n = e * 4 + q
                        if n >= 4:
                            pe.wait_ge(relu_dve if q % 2 else relu_act, (n - 4) // 2 + 1)
                        for a in range(2):
                            c = 2 * q + a
                            for k in range(KD):
                                ins = pe.matmul(HP[:, q, a * CAP:(a + 1) * CAP], W1[:, e % 2, k, c * P:(c + 1) * P], XET[:, e % 2, k, :],
                                                start=(k == 0), stop=(k == KD - 1))
                        ins.then_inc(hid_ready, 1)
                    if e + 1 < NE:
                        turn(e + 1)
                    pe.wait_ge(relu_act, 2 * (e + 1))
                    pe.wait_ge(relu_dve, 2 * (e + 1))
                    if e >= 2:
                        pe.wait_ge(y_copied, e - 1)
                    for a in range(2):
                        for c in range(NHID):
                            ins = pe.matmul(YP[:, e % 2, a, :], HT[:, e % 2, c, a * HC_:(a + 1) * HC_], W2[:, e % 2, c, :],
                                            start=(c == 0), stop=(c == NHID - 1))
                    ins.then_inc(y_ready, 1)

            def relu_out(e, q):
                return HT[:, e % 2, 2 * q:2 * q + 2, :], HP[:, q, 0:2 * CAP].rearrange("p (a n) -> p a n", a=2)

            @block.scalar
            def _(act):
                tables.scalar_step(act, 0)
                for e in range(NE):
                    for q in (0, 2):
                        act.wait_ge(hid_ready, 4 * e + q + 1)
                        if e >= 2:
                            act.wait_ge(y_ready, e - 1)
                        out, hid = relu_out(e, q)
                        act.activation(out, hid, ACT.Relu).then_inc(relu_act, 1)
                    act.wait_ge(y_ready, e + 1)
                    if e >= 2:
                        act.wait_ge(stored[e % 2], 16 * (e // 2))
                    act.activation(YE[:, e % 2], YP[:, e % 2], ACT.Copy).then_inc(y_copied, 1)
                    tables.scalar_step(act, e + 1)

            @block.vector
            def _(v):
                def take(e):
                    for k in range(KD):
                        v.wait_ge(turned, 2 * e + k + 1)
                        if e >= 2:
                            v.wait_ge(hid_ready, 4 * (e - 1))
                        v.tensor_copy(XET[:, e % 2, k, :], TP[:, k, 0:CAP]).then_inc(turned_read, 1)

                tables.exponents(v)
                take(0)
                for e in range(NE):
                    for q in (1, 3):
                        v.wait_ge(hid_ready, 4 * e + q + 1)
                        if e >= 2:
                            v.wait_ge(y_ready, e - 1)
                        out, hid = relu_out(e, q)
                        v.tensor_scalar(out, hid, 0.0, None, ALU.max).then_inc(relu_dve, 1)
                    if e + 1 < NE:
                        take(e + 1)
                    if 4 <= e < 7:
                        tables.factor_step(v, e - 4)

            @block.gpsimd
            def _(pool):
                tables.gpsimd_program(pool)


LH, LD = 16, 16
LPAD = 32
LC = LH * LPAD // P
LHC = LH // LC
PHI_EPS = 1e-3


def phi_out(v, out, product):
    return v.tensor_scalar(out, product, 0.0, PHI_EPS, ALU.max, ALU.add)


def mlp(nc, name, XT, ident, W1, W2, B1, HT, w1, b1, func, loads):
    loads = loads + [(W1[:], w1.rearrange("(k p) n -> p k n", p=P)), (B1[:], b1)]
    with Stage(nc, name) as st:
        ring = st.ps("ring", [P, 8, G4])
        loaded = st.sem("loaded")
        ready = st.sem("ready")
        read = st.sem("read")
        steps = [(g, c) for g in range(T // G4) for c in range(NHID)]
        with st.block() as block:
            @block.sync
            def _(sp):
                for dst, src in loads:
                    sp.dma_start(dst, src).then_inc(loaded, 16)

            @block.tensor
            def _(pe):
                pe.wait_ge(loaded, 16 * len(loads))
                for n, (g, c) in enumerate(steps):
                    if n >= 8:
                        pe.wait_ge(read, n - 7)
                    for k in range(KD):
                        ins = pe.matmul(ring[:, n % 8, :], W1[:, k, c * P:(c + 1) * P], XT[:, k, g * G4:(g + 1) * G4],
                                        start=(k == 0), stop=(k == KD - 1))
                    ins.then_inc(ready, 1)

            @block.scalar
            def _(act):
                act.wait_ge(loaded, 16 * len(loads))
                for n, (g, c) in enumerate(steps):
                    act.wait_ge(ready, n + 1)
                    act.activation(HT[:, c, g * G4:(g + 1) * G4], ring[:, n % 8, :], func, bias=B1[:, 0, c:c + 1]).then_inc(read, 1)


def mlp_product(HT, W2, B2, ident):
    def product(pe, t, out):
        for c in range(NHID):
            pe.matmul(out, HT[:, c, t * P:(t + 1) * P], W2[:, c, :], start=(c == 0), stop=False)
        return add_bias(pe, ident, out, B2[:])
    return product


def stage_performer(nc, io, X, XT, ident, KF):
    with Stage(nc, "pf") as st:
        LN = st.sb("LN", [P, 4, KD])
        WO = st.sb("WO", [P, KD, D])
        X1 = st.sb("X1", [P, NT, D])
        W2 = st.sb("W2", [P, NHID, D])
        B2 = st.sb("B2", [1, D])
        finish_norm(nc, "pfln1", X, XT, ident, None, total=lambda t: X[:, t, :], base=lambda t: None,
                    out=lambda t: X1[:, t, :], eps=EPS6, scale=LN[:, 0, :], bias=LN[:, 1, :],
                    loads=[(LN[:], io["L1_attn_ln"])])
        with Stage(nc, "pg") as s1:
            QT = s1.sb("QT", [P, LC, T])
            KT = s1.sb("KT", [P, LC, T])
            VA = s1.sb("VA", [P, NT, LH, 2 * LD])
            WQ = s1.sb("WQ", [P, KD, LC * P])
            WK = s1.sb("WK", [P, KD, LC * P])
            WV = s1.sb("WV", [P, KD, D])
            MASK = s1.sb("MASK", [P, 2, P])
            loads = [(WQ[:], io["L1_attn_wq"].rearrange("(k p) n -> p k n", p=P)),
                     (WK[:], io["L1_attn_wk"].rearrange("(k p) n -> p k n", p=P)),
                     (WV[:], io["L1_attn_wv"].rearrange("(k p) n -> p k n", p=P)),
                     (WO[:], io["L1_attn_wo"].rearrange("(k p) n -> p k n", p=P)),
                     (MASK[:], io["tri"])]
            with s1.block() as block:
                @block.gpsimd
                def _(pool):
                    pool.memset(VA[:].rearrange("p t h d -> p (t h) d")[:, :, LD:2 * LD], 1.0)
            jobs = []
            for g in range(T // G4):
                tok = slice(g * G4, (g + 1) * G4)
                for W, OUT in ((WQ, QT), (WK, KT)):
                    for c in range(LC):
                        jobs.append((OUT[:, c, tok], [(W[:, k, c * P:(c + 1) * P], XT[:, k, tok]) for k in range(KD)], phi_out))

            def value_out(v, out, product):
                return v.tensor_copy(out, product.rearrange("p (h d) -> p h d", h=LH))

            for t in range(NT):
                jobs.append((VA[:, t, :, 0:LD], [(XT[:, k, t * P:(t + 1) * P], WV[:, k, :]) for k in range(KD)], value_out))
            products(nc, "pfproj", jobs, loads, dve_only=True)
            performer_core(nc, ident, QT, KT, VA, MASK, X1)
            turn_tiles(nc, "pfturn", X1, XT, ident)

        def out_product(pe, t, out):
            for k in range(KD):
                ins = pe.matmul(out, XT[:, k, t * P:(t + 1) * P], WO[:, k, :], start=(k == 0), stop=(k == KD - 1))
            return ins

        with Stage(nc, "ph") as s1:
            HT = s1.sb("HT", [P, NHID, T])
            with Stage(nc, "pi") as s2:
                YT = s2.sb("YT", [P, KD, T])
                W1 = s2.sb("W1", [P, KD, HID])
                B1 = s2.sb("B1", [P, 1, NHID])
                Z = s2.sb("Z", [P, 2, D])
                finish_norm(nc, "pfln2", X, YT, ident, out_product, total=lambda t: X1[:, t, :], also=lambda t: X[:, t, :],
                            out=lambda t: X1[:, t, :], eps=EPS6, scale=LN[:, 2, :], bias=LN[:, 3, :])
                mlp(nc, "pfmlp", YT, ident, W1, W2, B1, HT, io["L1_attn_w1"], io["L1_attn_b1"], ACT.Gelu_apprx_tanh,
                    [(W2[:], io["L1_attn_w2"].rearrange("(k p) n -> p k n", p=P)), (B2[:], io["L1_attn_b2"])])
            finish_norm(nc, "pfnorm", X, XT, ident, mlp_product(HT, W2, B2, ident))


def turn_tiles(nc, name, Y, YT, ident):
    with Stage(nc, name) as st:
        TP = st.ps("TP", [P, 4, 512])
        turned = st.sem("turned")
        read = st.sem("read")
        with st.block() as block:
            @block.tensor
            def _(pe):
                for t in range(NT):
                    if t >= 4:
                        pe.wait_ge(read, t - 3)
                    for k in range(KD):
                        ins = pe.transpose(TP[:, t % 4, k * P:(k + 1) * P], Y[:, t, k * P:(k + 1) * P], ident[:, 0:P])
                    ins.then_inc(turned, 1)

            @block.scalar
            def _(act):
                for t in range(NT):
                    act.wait_ge(turned, t + 1)
                    act.activation(YT[:, :, t * P:(t + 1) * P], TP[:, t % 4, 0:D].rearrange("p (k n) -> p k n", k=KD), ACT.Copy).then_inc(read, 1)


def performer_core(nc, ident, QT, KT, VA, MASK, AO):
    NU = B * LC
    with Stage(nc, "pfcore") as st:
        A = st.sb("A", [P, 2, LHC, 3, P])
        OS = st.sb("OS", [P, 2, S])
        RD = st.sb("RD", [P, 2, LHC])
        SC = st.ps("SC", [P, LHC, 512])
        OP = st.ps("OP", [P, 2, 512])
        TP = st.ps("TP", [P, 2, 512])
        scores_ready = st.sem("scores_ready")
        masked = st.sem("masked")
        out_ready = st.sem("out_ready")
        out_copied = st.sem("out_copied")
        turned = st.sem("turned")
        normed = st.sem("normed")
        dve_chain = st.sem("dve_chain")
        with st.block() as block:
            @block.tensor
            def _(pe):
                def turn(m):
                    pe.wait_ge(out_copied, m + 1)
                    if m >= 2:
                        pe.wait_ge(normed, m - 1)
                    for a in range(2):
                        ins = pe.transpose(TP[:, m % 2, a * P:(a + 1) * P], OS[:, m % 2, a * P:(a + 1) * P], ident[:, 0:P])
                    ins.then_inc(turned, 1)

                def outs(m):
                    b, c = m // LC, m % LC
                    pe.wait_ge(masked, m + 1)
                    if m >= 2:
                        pe.wait_ge(out_copied, m - 1)
                    for h in range(LHC):
                        hd = c * LHC + h
                        r = slice(h * LPAD, (h + 1) * LPAD)
                        pe.matmul(OP[r, m % 2, 0:S], VA[:, 2 * b, hd, :], A[:, m % 2, h, 0:2, :], start=True, stop=False)
                        ins = pe.matmul(OP[r, m % 2, P:S], VA[:, 2 * b + 1, hd, :], A[:, m % 2, h, 2, :], start=False, stop=True)
                    ins.then_inc(out_ready, 1)

                for m in range(NU):
                    b, c = m // LC, m % LC
                    if m:
                        pe.wait_ge(masked, m)
                    for h in range(LHC):
                        r = slice(h * LPAD, h * LPAD + LD)
                        pe.matmul(SC[:, h, 0:S], KT[r, c, b * S:b * S + P], QT[r, c, b * S:(b + 1) * S], start=True, stop=True,
                                  tile_position=(h * LPAD, 0))
                        ins = pe.matmul(SC[:, h, S:S + P], KT[r, c, b * S + P:(b + 1) * S], QT[r, c, b * S + P:(b + 1) * S], start=True, stop=True,
                                        tile_position=(h * LPAD, 0))
                    ins.then_inc(scores_ready, 1)
                    if m >= 1:
                        outs(m - 1)
                    if m >= 2:
                        turn(m - 2)
                outs(NU - 1)
                turn(NU - 2)
                turn(NU - 1)

            @block.scalar
            def _(act):
                for m in range(NU):
                    act.wait_ge(out_ready, m + 1)
                    if m >= 2:
                        act.wait_ge(turned, m - 1)
                    act.activation(OS[:, m % 2, :], OP[:, m % 2, 0:S], ACT.Copy).then_inc(out_copied, 1)

            @block.vector
            def _(v):
                ch = Chain(v, dve_chain)

                def norm(m):
                    b, c = m // LC, m % LC
                    v.wait_ge(turned, m + 1)
                    tp = TP[:, m % 2, 0:S].rearrange("p (a h d) -> p a h d", a=2, h=LHC)
                    ch.link(v.reciprocal(RD[:], tp[:, :, :, LD]))
                    for a in range(2):
                        ch.link(v.tensor_tensor(AO[:, 2 * b + a, c * LHC * LD:(c + 1) * LHC * LD].rearrange("p (h d) -> p h d", h=LHC),
                                                tp[:, a, :, 0:LD], RD[:, a, :].rearrange("p (h o) -> p h o", o=1).to_broadcast([P, LHC, LD]),
                                                ALU.mult))
                    v.sem_inc(normed, 1)

                for m in range(NU):
                    v.wait_ge(scores_ready, m + 1)
                    if m >= 2:
                        v.wait_ge(out_ready, m - 1)
                    sc = SC[:, :, 0:3 * P].rearrange("p h (a q) -> p h a q", a=3)
                    a = A[:, m % 2]
                    tri = MASK[:, 0:1, :].to_broadcast([P, LHC, P])
                    v.tensor_tensor(a[:, :, 0, :], sc[:, :, 0, :], tri, ALU.mult)
                    v.tensor_tensor(a[:, :, 2, :], sc[:, :, 2, :], tri, ALU.mult)
                    v.tensor_copy(a[:, :, 1, :], sc[:, :, 1, :]).then_inc(masked, 1)
                    if m >= 3:
                        norm(m - 3)
                for m in range(NU - 3, NU):
                    norm(m)


XH, XD = 4, 32
TOPK = 32
MASKED, TAKEN = -3e38, -3.4e38


def stage_s4d(nc, io, X, XT, ident, KF):
    with Stage(nc, "s4") as st:
        Z = st.sb("Z", [P, NT, D])
        FO = st.sb("FO", [P, NT, 2 * D])
        with Stage(nc, "s5") as s1:
            CTT = s1.sb("CTT", [P, KD, T])
            finish_norm(nc, "s4ln", X, None, ident, None, base=lambda t: None, out=lambda t: Z[:, t, :])
            topk_attention(nc, io, XT, ident, CTT, Z, FO)
        s4d_convolve(nc, io, KF, X, Z, FO)
        with Stage(nc, "s6") as s1:
            HT = s1.sb("HT", [P, NHID, T])
            W2 = s1.sb("W2", [P, NHID, D])
            B2 = s1.sb("B2", [1, D])
            LN = s1.sb("LN", [P, 2, KD])
            finish_norm(nc, "s4ln2", X, XT, ident, None, total=lambda t: Z[:, t, :], base=lambda t: None,
                        out=lambda t: FO[:, t, 0:D], scale=LN[:, 0, :], bias=LN[:, 1, :], loads=[(LN[:], io["L1_xattn_ffn_ln"])])
            with Stage(nc, "s7") as s2:
                W1 = s2.sb("W1", [P, KD, HID])
                B1 = s2.sb("B1", [P, 1, NHID])
                mlp(nc, "s4mlp", XT, ident, W1, W2, B1, HT, io["L1_xattn_W1"], io["L1_xattn_b1"], ACT.Gelu,
                    [(W2[:], io["L1_xattn_W2"].rearrange("(k p) n -> p k n", p=P)), (B2[:], io["L1_xattn_b2"])])
            finish_norm(nc, "s4ln3", X, None, ident, mlp_product(HT, W2, B2, ident), total=lambda t: Z[:, t, :],
                        base=lambda t: Z[:, t, :], out=lambda t: Z[:, t, :])
        GB = st.sb("GB", [P, 2, D])
        with Stage(nc, "s8") as s1:
            loaded = s1.sem("loaded")
            scaled = s1.sem("scaled")
            with s1.block() as block:
                @block.sync
                def _(sp):
                    sp.dma_start(GB[:], io["L1_xattn_norm_out"]).then_inc(loaded, 16)

                @block.vector
                def _(v):
                    v.wait_ge(loaded, 16)
                    v.tensor_tensor(Z[:], Z[:], GB[:, 0:1, :].to_broadcast([P, NT, D]), ALU.mult).then_inc(scaled, 1)
                    v.wait_ge(scaled, 1)
                    v.tensor_tensor(Z[:], Z[:], GB[:, 1:2, :].to_broadcast([P, NT, D]), ALU.add)
        finish_norm(nc, "s4norm", X, XT, ident, None, base=lambda t: Z[:, t, :])


def topk_attention(nc, io, XT, ident, CTT, Z, FO):
    with Stage(nc, "tk") as st:
        QT = st.sb("QT", [P, T])
        KT = st.sb("KT", [P, T])
        V = st.sb("V", [P, NT, D])
        MB = st.sb("MB", [P, T])
        TM = st.sb("TM", [P, T])
        WI = st.sb("WI", [P, 2, KD, 2 * D])
        BI = st.sb("BI", [1, 2, 2 * D])
        GB = st.sb("GB", [P, 2, D])
        GATE = st.sb("GATE", [P, 1])
        film_loads = [(GB[:], io["L1_xattn_norm_in"]), (GATE[:], io["L1_xattn_gate"])]
        for n, name in enumerate(("in", "out")):
            film_loads += [(WI[:, n], io["L1_xattn_W_film_" + name].rearrange("(k p) n -> p k n", p=P)),
                           (BI[:, n, :], io["L1_xattn_b_film_" + name])]
        with Stage(nc, "tl") as s2:
            CT = s2.sb("CT", [P, 2, T])
            WQ = s2.sb("WQ", [P, KD, P])
            WK = s2.sb("WK", [P, 2, P])
            WV = s2.sb("WV", [P, 2, D])
            M8 = s2.sb("M8", [P, 2, T], U8)
            loads = load_context(io, CT) + load_split(WK, io["L1_xattn_Wk"]) + load_split(WV, io["L1_xattn_Wv"]) + [
                (WQ[:], io["L1_xattn_Wq"].rearrange("(k p) n -> p k n", p=P)), (M8[:, 0, :], io["text_mask"]), (M8[:, 1, :], io["vision_mask"])]
            jobs = []
            for g in range(T // G4):
                tok = slice(g * G4, (g + 1) * G4)
                jobs.append((QT[:, tok], [(WQ[:, k, :], XT[:, k, tok]) for k in range(KD)], copy_out))
                jobs.append((KT[:, tok], [(WK[0:KC[k], k, :], CT[0:KC[k], k, tok]) for k in range(2)], copy_out))
            for t in range(NT):
                jobs.append((V[:, t, :], [(CT[0:KC[k], k, t * P:(t + 1) * P], WV[0:KC[k], k, :]) for k in range(2)], copy_out))
            products(nc, "tkproj", jobs, loads)
            with s2.block() as block:
                @block.vector
                def _(v):
                    v.tensor_scalar(TM[:], M8[:, 0, :], 1.0 / XH, None, ALU.mult)
                    v.tensor_scalar(MB[:], M8[:, 1, :], -MASKED, MASKED, ALU.mult, ALU.add)

        SS = st.sb("SS", [P, 2, XH, S])
        WW = st.sb("WW", [P, XH, S])
        EX = st.sb("EX", [P, 2, XH, S])
        PP = st.sb("PP", [P, 2, XH, S])
        DG = st.sb("DG", [P, XH, P])
        AT = st.sb("AT", [P, 2, 2, P])
        MX = st.sb("MX", [P, XH, TOPK])
        NM = st.sb("NM", [P, 2, XH])
        SM = st.sb("SM", [P, 2, XH])
        SC = st.ps("SC", [P, XH, 512])
        TP = st.ps("TP", [P, 2, 2, D])
        FP = st.ps("FP", [P, 2, 2 * D])
        FI = st.sb("FI", [P, 2, 2 * D])
        film_loaded = st.sem("film_loaded")
        film_ready = st.sem("film_ready")
        film_read = st.sem("film_read")
        updated = st.sem("updated")
        pool_chain = st.sem("pool_chain")
        scores_ready = st.sem("scores_ready")
        scores_read = st.sem("scores_read")
        max_ready = st.sem("max_ready")
        exp_ready = st.sem("exp_ready")
        sums_ready = st.sem("sums_ready")
        scale_ready = st.sem("scale_ready")
        turned = st.sem("turned")
        turned_read = st.sem("turned_read")
        pooled = st.sem("pooled")
        pooled_read = st.sem("pooled_read")
        dve_chain = st.sem("dve_chain")
        with st.block() as block:
            @block.tensor
            def _(pe):
                def scores(n):
                    if n:
                        pe.wait_ge(scores_read, n)
                    b = n // 2
                    for h in range(XH):
                        r = slice(h * XD, (h + 1) * XD)
                        ins = pe.matmul(SC[:, h, 0:S], QT[r, n * P:(n + 1) * P], KT[r, b * S:(b + 1) * S], start=True, stop=True,
                                        tile_position=(h * XD, 0))
                    ins.then_inc(scores_ready, 1)

                def turn(n):
                    pe.wait_ge(scale_ready, n + 1)
                    if n >= 2:
                        pe.wait_ge(pooled_read, n - 1)
                    for k in range(2):
                        for h in range(XH):
                            ins = pe.matmul(TP[:, n % 2, 0, k * P:(k + 1) * P], PP[:, n % 2, h, k * P:(k + 1) * P], DG[:, h, :],
                                            start=(h == 0), stop=(h == XH - 1))
                    ins.then_inc(turned, 1)

                def pool_context(n):
                    pe.wait_ge(turned_read, n + 1)
                    for c in range(KD):
                        for k in range(2):
                            ins = pe.matmul(TP[:, n % 2, 1, c * P:(c + 1) * P], V[:, (n // 2) * 2 + k, c * P:(c + 1) * P], AT[:, n % 2, k, :],
                                            start=(k == 0), stop=(k == 1))
                    ins.then_inc(pooled, 1)

                def film(n):
                    pe.wait_ge(pooled_read, n + 1)
                    if n:
                        pe.wait_ge(film_read, n)
                    for i in range(2):
                        for k in range(KD):
                            pe.matmul(FP[:, i, :], CTT[:, k, n * P:(n + 1) * P], WI[:, i, k, :], start=(k == 0), stop=False)
                        ins = add_bias(pe, ident, FP[:, i, :], BI[:, i, :])
                    ins.then_inc(film_ready, 1)

                scores(0)
                pe.wait_ge(film_loaded, 16 * len(film_loads))
                for n in range(NT):
                    if n + 1 < NT:
                        scores(n + 1)
                    turn(n)
                    pool_context(n)
                    if n:
                        film(n - 1)
                film(NT - 1)

            @block.sync
            def _(sp):
                for dst, src in film_loads:
                    sp.dma_start(dst, src).then_inc(film_loaded, 16)

            @block.gpsimd
            def _(pool):
                ch = Chain(pool, pool_chain)
                pool.wait_ge(film_loaded, 16 * len(film_loads))
                for n in range(NT):
                    ch.link(pool.tensor_tensor(Z[:, n, :], Z[:, n, :], GB[:, 0, :], ALU.mult))
                    ch.link(pool.tensor_tensor(Z[:, n, :], Z[:, n, :], GB[:, 1, :], ALU.add))
                    pool.wait_ge(film_read, n + 1)
                    ch.link(pool.tensor_tensor(Z[:, n, :], Z[:, n, :], FI[:, n % 2, 0:D], ALU.mult))
                    pool.tensor_tensor(Z[:, n, :], Z[:, n, :], FI[:, n % 2, D:2 * D], ALU.add).then_inc(updated, 1)

            @block.scalar
            def _(act):
                def film(n):
                    act.wait_ge(film_ready, n + 1)
                    if n >= 2:
                        act.wait_ge(updated, n - 1)
                    act.activation(FI[:, n % 2, 0:D], FP[:, 0, 0:D], ACT.Identity, scale=GATE[:], bias=ident[:, ONES:ONES + 1])
                    act.activation(FI[:, n % 2, D:2 * D], FP[:, 0, D:2 * D], ACT.Copy, scale=GATE[:])
                    act.activation(FO[:, n, :], FP[:, 1, :], ACT.Copy, scale=GATE[:]).then_inc(film_read, 1)

                act.wait_ge(film_loaded, 16 * len(film_loads))
                for n in range(NT):
                    act.wait_ge(max_ready, n + 1)
                    for h in range(XH):
                        ins = act.activation(EX[:, n % 2, h, :], SS[:, n % 2, h, :], ACT.Exp, bias=NM[:, n % 2, h:h + 1])
                    ins.then_inc(exp_ready, 1)
                    if n >= 2:
                        film(n - 2)
                    act.wait_ge(sums_ready, n + 1)
                    for h in range(XH):
                        ins = act.activation(DG[:, h, :], ident[:, 0:P], ACT.Copy, scale=SM[:, n % 2, h:h + 1])
                    ins.then_inc(scale_ready, 1)
                    act.wait_ge(turned, n + 1)
                    act.activation(AT[:, n % 2], TP[:, n % 2, 0, :].rearrange("p (k q) -> p k q", k=2), ACT.Copy).then_inc(turned_read, 1)
                film(NT - 2)
                film(NT - 1)

            @block.vector
            def _(v):
                ch = Chain(v, dve_chain)

                def pooled_out(n):
                    v.wait_ge(pooled, n + 1)
                    tok = slice(n * P, (n + 1) * P)
                    v.tensor_tensor(CTT[:, :, tok], TP[:, n % 2, 1, :].rearrange("p (c q) -> p c q", c=KD),
                                    TM[:, tok].rearrange("p (o q) -> p o q", o=1).to_broadcast([P, KD, P]), ALU.mult).then_inc(pooled_read, 1)

                for n in range(NT):
                    b = n // 2
                    v.wait_ge(scores_ready, n + 1)
                    ss = SS[:, n % 2]
                    v.scalar_tensor_tensor(ss, SC[:, :, 0:S], float(XD) ** -0.5,
                                           MB[:, b * S:(b + 1) * S].rearrange("p (o q) -> p o q", o=1).to_broadcast([P, XH, S]),
                                           ALU.mult, ALU.add).then_inc(scores_read, 1)
                    v.wait_ge(scores_read, n + 1)
                    for r in range(TOPK // 8):
                        src = ss if r == 0 else WW[:]
                        for h in range(XH):
                            ins = v.max(MX[:, h, 8 * r:8 * r + 8], src[:, h, :])
                        ch.link(ins)
                        if r == 0:
                            v.tensor_scalar(NM[:, n % 2, :], MX[:, :, 0], -1.0, None, ALU.mult).then_inc(max_ready, 1)
                        for h in range(XH):
                            ins = v.match_replace(WW[:, h, :], MX[:, h, 8 * r:8 * r + 8], src[:, h, :], TAKEN)
                        ch.link(ins)
                    v.wait_ge(exp_ready, n + 1)
                    if n >= 2:
                        v.wait_ge(turned, n - 1)
                    for h in range(XH):
                        ins = v.scalar_tensor_tensor(PP[:, n % 2, h, :], WW[:, h, :], 0.5 * (TAKEN + MASKED), EX[:, n % 2, h, :], ALU.is_le, ALU.mult,
                                                     accum_out=SM[:, n % 2, h:h + 1])
                    ch.link(ins)
                    v.reciprocal(SM[:, n % 2, :], SM[:, n % 2, :]).then_inc(sums_ready, 1)
                    if n:
                        pooled_out(n - 1)
                pooled_out(NT - 1)


def s4d_convolve(nc, io, KF, X, Z, FO):
    NP = B // 2
    with Stage(nc, "cv") as st:
        DFT = st.sb("DFT", [P, 2, NF, P])
        INV = st.sb("INV", [P, NF, 2, P])
        SK = st.sb("SK", [P, D])
        MM = st.sb("MM", [P, 4, 2, D])
        YF = st.sb("YF", [P, 2, NF, 2, D])
        XD = st.sb("XD", [P, 4, D])
        XF = st.ps("XF", [P, NF, 2, D])
        YP = st.ps("YP", [P, 2, 2, D])
        loaded = st.sem("loaded")
        xf_ready = st.sem("xf_ready")
        xf_read = st.sem("xf_read")
        prod_ready = st.sem("prod_ready")
        prod_used = st.sem("prod_used")
        skip_ready = st.sem("skip_ready")
        y_ready = st.sem("y_ready")
        y_read = st.sem("y_read")
        done = st.sem("done")
        dve_chain = st.sem("dve_chain")
        pool_chain = st.sem("pool_chain")
        with st.block() as block:
            @block.sync
            def _(sp):
                sp.dma_start(DFT[:], io["dft"]).then_inc(loaded, 16)
                sp.dma_start(INV[:], io["dft_inverse"]).then_inc(loaded, 16)
                sp.dma_start(SK[:], io["L1_xattn_D_skip"]).then_inc(loaded, 16)

            def tiles(buf, pr):
                return buf[:, 4 * pr:4 * pr + 4, :].rearrange("p (b h) d -> p b h d", h=2)

            @block.tensor
            def _(pe):
                pe.wait_ge(loaded, 48)
                for pr in range(NP):
                    for ft in range(2):
                        for q in (2 * ft, 2 * ft + 1):
                            if pr:
                                pe.wait_ge(xf_read, 2 * (pr - 1) + ft + 1)
                            for h in range(2):
                                ins = pe.matmul(XF[:, q], DFT[:, h, q, :], tiles(Z, pr)[:, :, h, :], start=(h == 0), stop=(h == 1))
                        ins.then_inc(xf_ready, 1)
                    pe.wait_ge(prod_used, 2 * (pr + 1))
                    for h in range(2):
                        if pr:
                            pe.wait_ge(y_read, 2 * (pr - 1) + h + 1)
                        for q in range(NF):
                            ins = pe.matmul(YP[:, h], INV[:, q, h, :], YF[:, pr % 2, q], start=(q == 0), stop=(q == NF - 1))
                        ins.then_inc(y_ready, 1)

            @block.gpsimd
            def _(pool):
                ch = Chain(pool, pool_chain)
                pool.wait_ge(loaded, 48)
                for pr in range(NP):
                    if pr:
                        pool.wait_ge(y_read, 2 * pr)
                    pool.tensor_tensor(XD[:], Z[:, 4 * pr:4 * pr + 4, :], SK[:].rearrange("p (o d) -> p o d", o=1).to_broadcast([P, 4, D]),
                                       ALU.mult).then_inc(skip_ready, 1)
                    if pr >= 2:
                        pool.wait_ge(y_ready, 2 * (pr - 1))
                    for ft in range(2):
                        pool.wait_ge(prod_ready, 2 * pr + ft + 1)
                        ch.link(pool.tensor_tensor(YF[:, pr % 2, 2 * ft], MM[:, 0], MM[:, 1], ALU.subtract))
                        pool.tensor_tensor(YF[:, pr % 2, 2 * ft + 1], MM[:, 2], MM[:, 3], ALU.add).then_inc(prod_used, 1)

            @block.vector
            def _(v):
                ch = Chain(v, dve_chain)
                for pr in range(NP):
                    for ft in range(2):
                        n = 2 * pr + ft
                        v.wait_ge(xf_ready, n + 1)
                        if n:
                            v.wait_ge(prod_used, n)
                        for i, (x, k) in enumerate(((0, 0), (1, 1), (0, 1), (1, 0))):
                            ins = v.tensor_tensor(MM[:, i], XF[:, 2 * ft + x],
                                                  KF[:, 2 * ft + k:2 * ft + k + 1, :].to_broadcast([P, 2, D]), ALU.mult)
                            ch.link(ins)
                        v.sem_inc(prod_ready, 1)
                        v.sem_inc(xf_read, 1)
                    v.wait_ge(skip_ready, pr + 1)
                    for h in range(2):
                        v.wait_ge(y_ready, 2 * pr + h + 1)
                        z = tiles(Z, pr)[:, :, h, :]
                        fo = tiles(FO, pr)[:, :, h, :]
                        xd = XD[:].rearrange("p (b h) d -> p b h d", h=2)[:, :, h, :]
                        ch.link(v.tensor_tensor(z, YP[:, h], xd, ALU.add))
                        v.sem_inc(y_read, 1)
                        ch.link(v.scalar_tensor_tensor(z, fo[:, :, 0:D], 1.0, z, ALU.add, ALU.mult))
                        ch.link(v.tensor_tensor(z, z, fo[:, :, D:2 * D], ALU.add))
                        ch.link(v.tensor_tensor(z, z, tiles(X, pr)[:, :, h, :], ALU.add))


PH, PK, NK = 8, 8, 64
NC_ = 2 * PH
HK = PH * PK
J2 = NK // 2
BLK = 256
UNIT = 32
PSCALE = 2.0 ** 14
F16 = mybir.dt.float16


def stage_peer(nc, io, X, XT, ident, KF):
    with Stage(nc, "pe") as st:
        IXT = st.sb("IXT", [P, T], F16)
        IYT = st.sb("IYT", [P, T], F16)
        PRT = st.sb("PRT", [P, T], F16)
        with Stage(nc, "pq") as s1:
            SV = s1.sb("SV", [P, NT, NC_, PK])
            IV = s1.sb("IV", [P, NT, NC_, PK], U32)
            peer_sides(nc, io, XT, ident, SV, IV)
            peer_select(nc, ident, SV, IV, IXT, IYT, PRT)
        peer_experts(nc, io, X, XT, IXT, IYT, PRT)
        finish_norm(nc, "pnorm", X, XT, ident, None, base=lambda t: None, last=True)


def peer_sides(nc, io, XT, ident, SV, IV):
    with Stage(nc, "sides") as st:
        WQ = st.sb("WQ", [P, KD, NC_ * P])
        KEYS = st.sb("KEYS", [P, NC_, NK])
        BN = st.sb("BN", [P, 2, NC_])
        QN = st.sb("QN", [P, 2, T])
        RAW = st.sb("RAW", [P, 4, 6])
        MV = st.sb("MV", [P, NC_, 2])
        SD = st.sb("SD", [P, NC_])
        SB_ = st.sb("SB_", [P, NC_, 2])
        QP = st.ps("QP", [P, 4, G4])
        SP_ = st.ps("SP_", [P, 2, NT, NK])
        loaded = st.sem("loaded")
        q_ready = st.sem("q_ready")
        var_ready = st.sem("var_ready")
        std_ready = st.sem("std_ready")
        affine_ready = st.sem("affine_ready")
        q_normed = st.sem("q_normed")
        sims_ready = st.sem("sims_ready")
        sims_read = st.sem("sims_read")
        dve_chain = st.sem("dve_chain")
        with st.block() as block:
            @block.sync
            def _(sp):
                sp.dma_start(WQ[:], io["L1_ffn_w_q"].rearrange("(k p) n -> p k n", p=P)).then_inc(loaded, 16)
                sp.dma_start(KEYS[:], io["L1_ffn_keysT"]).then_inc(loaded, 16)
                sp.dma_start(BN[:], io["L1_ffn_bn"]).then_inc(loaded, 16)

            @block.tensor
            def _(pe):
                def query(c):
                    for g in range(4):
                        if c:
                            pe.wait_ge(q_normed, 4 * (c - 1) + g + 1)
                        for k in range(KD):
                            ins = pe.matmul(QP[:, g, :], WQ[:, k, c * P:(c + 1) * P], XT[:, k, g * G4:(g + 1) * G4],
                                            start=(k == 0), stop=(k == KD - 1))
                        ins.then_inc(q_ready, 1)

                pe.wait_ge(loaded, 48)
                query(0)
                for c in range(NC_):
                    if c + 1 < NC_:
                        query(c + 1)
                    pe.wait_ge(q_normed, 4 * (c + 1))
                    if c >= 2:
                        pe.wait_ge(sims_read, c - 1)
                    for t in range(NT):
                        ins = pe.matmul(SP_[:, c % 2, t, :], QN[:, c % 2, t * P:(t + 1) * P], KEYS[:, c, :], start=True, stop=True)
                    ins.then_inc(sims_ready, 1)

            @block.scalar
            def _(act):
                for c in range(NC_):
                    act.wait_ge(var_ready, c + 1)
                    act.activation(SD[:, c:c + 1], MV[:, c, 1:2], ACT.Sqrt, bias=ident[:, EPS5:EPS5 + 1]).then_inc(std_ready, 1)
                    act.wait_ge(affine_ready, c + 1)
                    if c >= 2:
                        act.wait_ge(sims_ready, c - 1)
                    for g in range(4):
                        act.activation(QN[:, c % 2, g * G4:(g + 1) * G4], QP[:, g, :], ACT.Identity, scale=SB_[:, c, 0:1],
                                       bias=SB_[:, c, 1:2]).then_inc(q_normed, 1)

            @block.vector
            def _(v):
                ch = Chain(v, dve_chain)

                def norm(c):
                    for g in range(4):
                        v.wait_ge(q_ready, 4 * c + g + 1)
                        ins = v.bn_stats(RAW[:, g, :], QP[:, g, :])
                    ch.link(ins)
                    v.bn_aggr(MV[:, c, :], RAW[:].rearrange("p g s -> p (g s)")).then_inc(var_ready, 1)
                    v.wait_ge(std_ready, c + 1)
                    ch.link(v.reciprocal(SD[:, c:c + 1], SD[:, c:c + 1]))
                    ch.link(v.tensor_tensor(SB_[:, c, 0:1], SD[:, c:c + 1], BN[:, 0, c:c + 1], ALU.mult))
                    ch.link(v.tensor_tensor(SB_[:, c, 1:2], SB_[:, c, 0:1], MV[:, c, 0:1], ALU.mult))
                    v.tensor_tensor(SB_[:, c, 1:2], BN[:, 1, c:c + 1], SB_[:, c, 1:2], ALU.subtract).then_inc(affine_ready, 1)

                v.wait_ge(loaded, 48)
                norm(0)
                for c in range(NC_):
                    if c + 1 < NC_:
                        norm(c + 1)
                    v.wait_ge(sims_ready, c + 1)
                    for t in range(NT):
                        ins = v.max(SV[:, t, c, :], SP_[:, c % 2, t, :])
                    ch.link(ins)
                    for t in range(NT):
                        ins = v.max_index(IV[:, t, c, :], SV[:, t, c, :], SP_[:, c % 2, t, :])
                    ins.then_inc(sims_read, 1)


def peer_select(nc, ident, SV, IV, IXT, IYT, PRT):
    N = NT * PH
    with Stage(nc, "select") as st:
        IF = st.sb("IF", [P, NT, NC_, PK])
        AS = st.sb("AS", [P, 2, PH, PK, PK])
        TV = st.sb("TV", [P, NT, PH, PK])
        AB = st.sb("AB", [P, 3, N, PK], U32)
        RF = st.sb("RF", [P, 2, N, PK])
        KX = st.sb("KX", [P, 2, N, PK])
        TMP = st.sb("TMP", [P, N, PK])
        PR = st.sb("PR", [P, N, PK])
        SM = st.sb("SM", [P, N])
        H16 = st.sb("H16", [P, N, PK], F16)
        DUP = st.sb("DUP", [P, 3, NT, 2, HK])
        TP = st.ps("TP", [P, 2, 4, P])
        summed = st.sem("summed")
        shifted = st.sem("shifted")
        exp_ready = st.sem("exp_ready")
        arranged = st.sem("arranged")
        turned = st.sem("turned")
        turned_read = st.sem("turned_read")
        picked = st.sem("picked")
        dve_chain = st.sem("dve_chain")
        with st.block() as block:
            @block.gpsimd
            def _(pool):
                for t in range(NT):
                    if t >= 2:
                        pool.wait_ge(picked, t - 1)
                    sx = SV[:, t, 0:PH, :].rearrange("p h (a o) -> p h a o", o=1).to_broadcast([P, PH, PK, PK])
                    sy = SV[:, t, PH:, :].rearrange("p h (o b) -> p h o b", o=1).to_broadcast([P, PH, PK, PK])
                    pool.tensor_tensor(AS[:, t % 2], sx, sy, ALU.add).then_inc(summed, 1)

            @block.scalar
            def _(act):
                act.wait_ge(shifted, 1)
                act.activation(PR[:], PR[:], ACT.Exp).then_inc(exp_ready, 1)
                for n in range(3 * NT // 4):
                    act.wait_ge(turned, n + 1)
                    q, t = n // (NT // 4), n % (NT // 4) * 4
                    out = (IXT, IYT, PRT)[q]
                    act.activation(out[:, t * P:(t + 4) * P], TP[:, n % 2].rearrange("p a q -> p (a q)"), ACT.Copy).then_inc(turned_read, 1)

            @block.tensor
            def _(pe):
                pe.wait_ge(arranged, 1)
                for n in range(3 * NT // 4):
                    if n >= 2:
                        pe.wait_ge(turned_read, n - 1)
                    for a in range(4):
                        q, t = n // (NT // 4), n % (NT // 4) * 4 + a
                        ins = pe.transpose(TP[:, n % 2, a, :], DUP[:, q, t].rearrange("p a k -> p (a k)"), ident[:, 0:P])
                    ins.then_inc(turned, 1)

            @block.vector
            def _(v):
                ch = Chain(v, dve_chain)
                ch.link(v.tensor_copy(IF[:], IV[:]))
                flat = AB[:, 0].rearrange("p (t h) k -> p t h k", t=NT)
                for t in range(NT):
                    v.wait_ge(summed, t + 1)
                    for h in range(PH):
                        ins = v.max(TV[:, t, h, :], AS[:, t % 2, h].rearrange("p a b -> p (a b)"))
                    ch.link(ins)
                    for h in range(PH):
                        ins = v.max_index(flat[:, t, h, :], TV[:, t, h, :], AS[:, t % 2, h].rearrange("p a b -> p (a b)"))
                    ch.link(ins)
                    v.sem_inc(picked, 1)
                tv = TV[:].rearrange("p t h k -> p (t h) k")
                ch.link(v.tensor_tensor(PR[:], tv, tv[:, :, 0:1].to_broadcast([P, N, PK]), ALU.subtract))
                v.sem_inc(shifted, 1)
                ch.link(v.tensor_scalar(AB[:, 1], AB[:, 0], 3, None, ALU.logical_shift_right))
                ch.link(v.tensor_scalar(AB[:, 2], AB[:, 0], PK - 1, None, ALU.bitwise_and))
                ch.link(v.tensor_copy(RF[:], AB[:, 1:3]))
                for side in range(2):
                    for r in range(PK):
                        idx = IF[:, :, side * PH:(side + 1) * PH, r:r + 1]
                        rf, tmp = (x.rearrange("p (t h) k -> p t h k", t=NT) for x in (RF[:, side], TMP[:]))
                        out = KX[:, side] if r == 0 else TMP[:]
                        ch.link(v.tensor_scalar(out, RF[:, side], float(r), None, ALU.is_equal))
                        o4 = out.rearrange("p (t h) k -> p t h k", t=NT)
                        ch.link(v.tensor_tensor(o4, o4, idx.to_broadcast([P, NT, PH, PK]), ALU.mult))
                        if r:
                            ch.link(v.tensor_tensor(KX[:, side], KX[:, side], TMP[:], ALU.add))
                v.wait_ge(exp_ready, 1)
                ch.link(v.tensor_reduce(SM[:], PR[:], AX_X, ALU.add))
                ch.link(v.reciprocal(SM[:], SM[:]))
                ch.link(v.tensor_scalar(SM[:], SM[:], PSCALE, None, ALU.mult))
                ch.link(v.tensor_tensor(PR[:], PR[:], SM[:].rearrange("p (n o) -> p n o", o=1).to_broadcast([P, N, PK]), ALU.mult))
                ch.link(v.tensor_copy(H16[:], PR[:]))
                dup = DUP[:].rearrange("p q t a (h k) -> p q a t h k", h=PH)
                kx = KX[:].rearrange("p q (t h) k -> p q t h k", t=NT)
                for a in range(2):
                    for q in range(2):
                        ch.link(v.tensor_copy(dup[:, q, a].rearrange("p t h k -> p t (h k)"), kx[:, q].rearrange("p t h k -> p t (h k)")))
                h16 = H16[:].rearrange("p (t h) k -> p t (h k)", t=NT)
                ch.link(v.tensor_copy(dup[:, 2, 0].rearrange("p t h k -> p t (h k)"), h16))
                v.tensor_tensor(dup[:, 2, 1].rearrange("p t h k -> p t (h k)"), PR[:].rearrange("p (t h) k -> p t (h k)", t=NT), h16,
                                ALU.subtract).then_inc(arranged, 1)


def peer_experts(nc, io, X, XT, IXT, IYT, PRT):
    NB = T // BLK
    UB = BLK // UNIT
    NU = NB * UB
    NP = J2 // 2
    PU = NP // UB
    TB = BLK // P
    with Stage(nc, "ex") as st:
        DOWN = st.sb("DOWN", [P, KD, J2, P])
        UP = st.sb("UP", [P, J2, D])
        GH = st.sb("GH", [P, 2, J2, BLK])
        IOTA = st.sb("IOTA", [P, NK, UNIT], F16)
        L = st.sb("L", [P, 2, NK, UNIT], F16)
        EQ = st.sb("EQ", [P, NK, UNIT], F16)
        R = st.sb("R", [P, 2, NK, UNIT], F16)
        HP = st.ps("HP", [P, 2, 2, BLK])
        GP = st.ps("GP", [P, 2, UNIT, J2])
        OP = st.ps("OP", [P, 2, 512])
        loaded = st.sem("loaded")
        hidden = st.sem("hidden")
        gelu_ready = st.sem("gelu_ready")
        left_ready = st.sem("left_ready")
        right_ready = st.sem("right_ready")
        gates_ready = st.sem("gates_ready")
        gated = st.sem("gated")
        out_ready = st.sem("out_ready")
        out_read = st.sem("out_read")
        dve_chain = st.sem("dve_chain")
        with st.block() as block:
            @block.sync
            def _(sp):
                sp.dma_start(IOTA[:], io["key_numbers"]).then_inc(loaded, 16)
                sp.dma_start(DOWN[:], io["L1_ffn_down"]).then_inc(loaded, 16)
                sp.dma_start(UP[:], io["L1_ffn_up"]).then_inc(loaded, 16)

            @block.tensor
            def _(pe):
                def hid(b, q):
                    n = b * NP + q
                    if n >= 2:
                        pe.wait_ge(gelu_ready, n - 1)
                    for a in range(2):
                        for k in range(KD):
                            ins = pe.matmul(HP[:, n % 2, a, :], DOWN[:, k, 2 * q + a, :], XT[:, k, b * BLK:(b + 1) * BLK],
                                            start=(k == 0), stop=(k == KD - 1))
                    ins.then_inc(hidden, 1)

                def gates(n):
                    pe.wait_ge(left_ready, n + 1)
                    pe.wait_ge(right_ready, n + 1)
                    if n >= 2:
                        pe.wait_ge(gated, n - 1)
                    for t in range(UNIT):
                        for jp in range(2):
                            ins = pe.matmul(GP[jp * NK:(jp + 1) * NK, n % 2, t, :], L[:, n % 2, :, t], R[:, n % 2, jp * J2:(jp + 1) * J2, t],
                                            start=True, stop=True, tile_position=(0, jp * NK))
                    ins.then_inc(gates_ready, 1)

                def answer(m):
                    b, a = m // TB, m % TB
                    pe.wait_ge(gated, (m + 1) * P // UNIT)
                    if m >= 2:
                        pe.wait_ge(out_read, m - 1)
                    for j in range(J2):
                        ins = pe.matmul(OP[:, m % 2, 0:D], GH[:, b % 2, j, a * P:(a + 1) * P], UP[:, j, :], start=(j == 0), stop=(j == J2 - 1))
                    ins.then_inc(out_ready, 1)

                pe.wait_ge(loaded, 48)
                for q in range(NP):
                    hid(0, q)
                for n in range(NU):
                    b, u = n // UB, n % UB
                    gates(n)
                    if n % (P // UNIT) == 1 and n > P // UNIT:
                        answer(n // (P // UNIT) - 1)
                    if b + 1 < NB:
                        for q in range(PU):
                            hid(b + 1, u * PU + q)
                answer(NT - 1)

            @block.scalar
            def _(act):
                for b in range(NB):
                    for q in range(NP):
                        n = b * NP + q
                        act.wait_ge(hidden, n + 1)
                        if b >= 2:
                            act.wait_ge(out_ready, (b - 1) * TB)
                        act.activation(GH[:, b % 2, 2 * q:2 * q + 2, :], HP[:, n % 2], ACT.Gelu_apprx_tanh).then_inc(gelu_ready, 1)

            @block.vector
            def _(v):
                ch = Chain(v, dve_chain)

                def answer_out(v, m):
                    v.wait_ge(out_ready, m + 1)
                    v.tensor_tensor(X[:, m, :], X[:, m, :], OP[:, m % 2, 0:D], ALU.add).then_inc(out_read, 1)

                def sides(n):
                    tok = slice(n * UNIT, (n + 1) * UNIT)

                    def along(x):
                        return x[:, tok].rearrange("p (o t) -> p o t", o=1).to_broadcast([P, NK, UNIT])

                    if n >= 2:
                        v.wait_ge(gates_ready, n - 1)
                    v.tensor_tensor(L[:, n % 2], IOTA[:], along(IXT), ALU.is_equal).then_inc(left_ready, 1)
                    ch.link(v.tensor_tensor(EQ[:], IOTA[:], along(IYT), ALU.is_equal))
                    v.tensor_tensor(R[:, n % 2], EQ[:], along(PRT), ALU.mult).then_inc(right_ready, 1)
                    v.wait_ge(right_ready, n + 1)

                v.wait_ge(loaded, 48)
                sides(0)
                for n in range(NU):
                    b, u = n // UB, n % UB
                    if n + 1 < NU:
                        sides(n + 1)
                    v.wait_ge(gates_ready, n + 1)
                    v.wait_ge(gelu_ready, (b + 1) * NP)
                    gh = GH[:, b % 2, :, u * UNIT:(u + 1) * UNIT]
                    v.scalar_tensor_tensor(gh, GP[:, n % 2].rearrange("p t j -> p j t"), 1.0 / PSCALE, gh, ALU.mult, ALU.mult).then_inc(gated, 1)
                    if n % (P // UNIT) == 2 and n > P // UNIT:
                        answer_out(v, n // (P // UNIT) - 1)
                answer_out(v, NT - 1)


STAGES = [stage_mamba, stage_xattn, stage_moe, stage_performer, stage_s4d, stage_peer]


def build(nc, io, out, stages=None):
    with nc.sbuf_tensor("X", [P, NT, D], F32) as X, nc.sbuf_tensor("XT", [P, KD, T], F32) as XT, \
            nc.sbuf_tensor("ident", [P, NI], F32) as ident, \
            nc.sbuf_tensor("KF", [P, NF, D], F32) as KF:
        stored = nc.alloc_semaphore("stored")
        stage_load(nc, io, X, XT, ident)
        for stage in (STAGES if stages is None else stages):
            stage(nc, io, X, XT, ident, KF)
            nc.clear_and_free_semaphores(list(Stage.semaphores))
            Stage.semaphores.clear()
            nc.all_engine_barrier()
        stage_store(nc, out, X, stored)


def columns(*vectors):
    return np.stack([v.reshape(-1, P).T for v in vectors], axis=1)


def rows(*vectors):
    return np.tile(np.stack(vectors), (P, 1, 1))


def layouts(inputs):
    a = {k: np.asarray(v) for k, v in inputs.items()}
    io = {}
    io["x"] = a["x"]
    io["xT"] = a["x"].reshape(T, D).T
    io["ident"] = np.concatenate([np.eye(P), np.full((P, 1), 1e-5), np.full((P, 1), 1e-6), np.ones((P, P))], axis=1).astype(np.float32)
    io["L0_attn_in_projT"] = a["L0_attn_in_proj_w"].T
    io["L0_attn_out_projT"] = a["L0_attn_out_proj_w"].T
    xp = a["L0_attn_x_proj_w"]
    io["L0_attn_x_delta"] = np.repeat(xp[0:1].T, P, axis=1)
    io["L0_attn_x_bc"] = np.concatenate([xp[1:].T] * 3, axis=1)
    sel = np.zeros((96, 32, P), np.uint16)
    for r in range(96):
        sel[r, r % 32, :] = BF16_ONE
    io["sel_bc"] = sel
    io["L0_attn_conv_w"] = a["L0_attn_conv_w"]
    io["L0_attn_vec"] = columns(a["L0_attn_conv_b"], a["L0_attn_dt_proj_w"][:, 0], a["L0_attn_dt_proj_b"], a["L0_attn_D"])
    io["L0_attn_A_log"] = a["L0_attn_A_log"]
    io["ctxT"] = a["ctx_768"].reshape(T, DCTX).T
    for n in ("Wq", "Wk", "Wv", "Wo"):
        io["L0_xattn_" + n] = a["L0_xattn_" + n]
    io["L0_xattn_bo"] = a["L0_xattn_bo"][None]
    io["L0_ffn_gateT"] = a["L0_ffn_gate_w"].T
    io["L0_ffn_w1"] = a["L0_ffn_w1"]
    io["L0_ffn_w2"] = a["L0_ffn_w2"]
    io["tri"] = np.stack([np.triu(np.ones((P, P))), np.ones((P, P))], axis=1).astype(np.float32)
    io["expert_numbers"] = np.tile(np.arange(NE, dtype=np.float32), (P, 1))
    io["spill_rows"] = (SLOTS + np.arange(T).reshape(NT, P).T).astype(np.float32)
    io["L1_attn_ln"] = columns(a["L1_attn_ln1_scale"], a["L1_attn_ln1_bias"], a["L1_attn_ln2_scale"], a["L1_attn_ln2_bias"])
    for n in ("wq", "wk"):
        io["L1_attn_" + n] = np.pad(a["L1_attn_" + n], ((0, 0), (0, 0), (0, LPAD - LD))).reshape(D, LH * LPAD)
    io["L1_attn_wv"] = a["L1_attn_wv"].reshape(D, D)
    io["L1_attn_wo"] = a["L1_attn_wo"].reshape(D, D)
    io["L1_attn_w1"] = a["L1_attn_w1"]
    io["L1_attn_w2"] = a["L1_attn_w2"]
    io["L1_attn_b1"] = columns(a["L1_attn_b1"])
    io["L1_attn_b2"] = a["L1_attn_b2"][None]
    for n in ("Wq", "Wk", "Wv", "W_film_in", "W_film_out", "W1", "W2"):
        io["L1_xattn_" + n] = a["L1_xattn_" + n]
    for n in ("b_film_in", "b_film_out", "b2"):
        io["L1_xattn_" + n] = a["L1_xattn_" + n][None]
    io["L1_xattn_b1"] = columns(a["L1_xattn_b1"])
    io["L1_xattn_ffn_ln"] = columns(a["L1_xattn_g_ffn"], a["L1_xattn_b_ffn"])
    io["L1_xattn_norm_in"] = rows(a["L1_xattn_g_norm_in"], a["L1_xattn_b_norm_in"])
    io["L1_xattn_norm_out"] = rows(a["L1_xattn_g_norm_out"], a["L1_xattn_b_norm_out"])
    io["L1_xattn_D_skip"] = np.tile(a["L1_xattn_D_skip"], (P, 1))
    io["L1_xattn_gate"] = np.tile(a["L1_xattn_mod_gate"].reshape(1, 1), (P, 1))
    for n, m in (("text_mask", "mask_BxS_bf1"), ("vision_mask", "mask_BxS2_bf1")):
        io[n] = np.tile(a[m].reshape(1, T).view(np.uint8), (P, 1))
    io["L1_xattn_s4d"] = np.stack([np.tile(a["L1_xattn_log_dt"], (P, 1))] +
                                  [np.concatenate([a["L1_xattn_" + n].T] * 2) for n in ("A_re", "A_im", "C_re", "C_im")], axis=1)
    low = (np.arange(P) < NST)[:, None]
    io["phases"] = np.concatenate([np.where(low, x, y) for x, y in ((0.25, 0.0), (0.5, 0.25), (0.25, 0.5), (0, 0))], axis=1).astype(np.float32)
    angle = 2 * np.pi * np.outer(np.arange(S), np.arange(S) + 0.5) / (2 * S)
    forward = np.stack([np.cos(angle).reshape(S, 2, P), -np.sin(angle).reshape(S, 2, P)], axis=2).reshape(S, NF, P)
    io["dft_kernel"] = forward.reshape(HI, LO // LB, LB, NF, P).transpose(2, 0, 1, 3, 4).reshape(P, LO // LB, NF, P).astype(np.float32)
    io["dft"] = forward.reshape(2, P, NF, P).transpose(1, 0, 2, 3).astype(np.float32)
    io["dft_inverse"] = (forward.reshape(2, P, NF, P).transpose(3, 2, 0, 1) / S).astype(np.float32)
    io["L1_ffn_w_q"] = a["L1_ffn_w_q"]
    io["L1_ffn_bn"] = columns(a["L1_ffn_bn_gamma"], a["L1_ffn_bn_beta"])
    io["L1_ffn_keysT"] = a["L1_ffn_keys"].transpose(3, 2, 0, 1).reshape(P, NC_, NK)
    tiles = (NK, 2, J2, D)
    io["L1_ffn_down"] = a["L1_ffn_down_embed"].reshape(tiles).transpose(3, 2, 1, 0).reshape(KD, P, J2, P).transpose(1, 0, 2, 3)
    io["L1_ffn_up"] = a["L1_ffn_up_embed"].reshape(tiles).transpose(1, 0, 2, 3).reshape(P, J2, D)
    io["key_numbers"] = np.tile(np.arange(NK, dtype=np.float16)[None, :, None], (P, 1, UNIT))
    return {k: np.ascontiguousarray(v) for k, v in io.items()}


def kernel(**inputs):
    import concourse.bacc as bacc
    from concourse.bass_utils import run_bass_kernel_spmd

    nc = bacc.Bacc("TRN2", target_bir_lowering=False, num_devices=1)
    arrays = layouts(inputs)
    io = {name: nc.dram_tensor(f"in_{name}", a.shape, mybir.dt.from_np(a.dtype), kind="ExternalInput").ap()
          for name, a in arrays.items()}
    out = nc.dram_tensor("out_0", (B, S, D), F32, kind="ExternalOutput").ap()
    build(nc, io, out)
    r = run_bass_kernel_spmd(nc, [{f"in_{k}": a for k, a in arrays.items()}], core_ids=[0])
    return r.results[0]["out_0"]
```

```python
from contextlib import ExitStack

import numpy as np

import concourse.bass as bass
from concourse import mybir

P = 128
B, S, D = 8, 256, 256
T = B * S
NT = T // P
KD = D // P
G4 = 512

F32 = mybir.dt.float32
BF16 = mybir.dt.bfloat16
I32 = mybir.dt.int32
U32 = mybir.dt.uint32
U8 = mybir.dt.uint8
ALU = mybir.AluOpType
ACT = mybir.ActivationFunctionType
AX_X = mybir.AxisListType.X


class Chain:

    def __init__(self, eng, sem):
        self.eng, self.sem, self.n = eng, sem, 0

    def link(self, ins):
        self.n += 1
        ins.then_inc(self.sem, 1)
        self.eng.wait_ge(self.sem, self.n)

    def mark(self, ins):
        self.n += 1
        ins.then_inc(self.sem, 1)
        return self.n

    def need(self, number):
        self.eng.wait_ge(self.sem, number)


class Stage:

    semaphores = []

    def __init__(self, nc, name):
        self.nc, self.name, self.ctx, self.dmas = nc, name, ExitStack(), 0

    def __enter__(self):
        self.ctx.__enter__()
        return self

    def __exit__(self, *e):
        return self.ctx.__exit__(*e)

    def sb(self, name, shape, dt=F32):
        return self.ctx.enter_context(self.nc.sbuf_tensor(f"{self.name}_{name}", shape, dt))

    def ps(self, name, shape, dt=F32):
        return self.ctx.enter_context(self.nc.psum_tensor(f"{self.name}_{name}", shape, dt))

    def sem(self, name):
        self.semaphores.append(self.nc.alloc_semaphore(f"{self.name}_{name}"))
        return self.semaphores[-1]

    def block(self):
        return self.nc.Block(f"{self.name}_block")


class Loads:

    def __init__(self, nc, name, pairs):
        self.pairs = list(pairs)
        self.loaded = nc.alloc_semaphore(f"{name}_in_place")

    def issue(self, sp):
        for dst, src in self.pairs:
            sp.dma_start(dst, src).then_inc(self.loaded, 16)

    def wait(self, eng):
        eng.wait_ge(self.loaded, 16 * len(self.pairs))


class Inputs:

    def __init__(self, nc, name):
        self.nc, self.name, self.buffers, self.pairs = nc, name, ExitStack(), []

    def sb(self, name, shape, dt=F32):
        return self.buffers.enter_context(self.nc.sbuf_tensor(f"{self.name}_{name}", shape, dt, side="right"))

    def ready(self):
        self.loads = Loads(self.nc, f"{self.name}_inputs", self.pairs)
        return self

    def free(self):
        self.buffers.close()


EPS5, EPS6 = P, P + 1
ONES = P + 2
NI = ONES + P


def load_tokens(io, X):
    return X[:], io["x"].rearrange("b (h p) d -> p (b h) d", p=P)


def stage_load(nc, io, X, XT, ident, with_x):
    loads = [(XT[:], io["xT"].rearrange("(k p) t -> p k t", p=P)), (ident[:], io["ident"])]
    loads = Loads(nc, "first", loads + ([load_tokens(io, X)] if with_x else []))
    with Stage(nc, "load") as st:
        with st.block() as block:
            @block.sync
            def _(sp):
                loads.issue(sp)
                loads.wait(sp)


def stage_store(nc, out, X, stored):
    with Stage(nc, "store") as st:
        with st.block() as block:
            @block.sync
            def _(sp):
                sp.dma_start(out.rearrange("b (h p) d -> p (b h) d", p=P), X[:]).then_inc(stored, 16)
                sp.wait_ge(stored, 16)


def add_bias(pe, ident, out, row):
    return pe.matmul(out, ident[0:1, ONES:ONES + P], row, start=False, stop=True)


def add_row(pool, x, row):
    return pool.tensor_tensor(x[:], x[:], row[:].rearrange("p (o d) -> p o d", o=1).to_broadcast([P, NT, D]), ALU.add)


def products(nc, name, jobs, loads, dve_only=False, ahead=(), beside=None):
    with Stage(nc, name) as st:
        BANKS = 8
        ring = st.ps("ring", [P, BANKS, 512])
        product_ready = st.sem("product_ready")
        even_read = st.sem("even_read")
        odd_read = st.sem("odd_read")

        def bank(n, out):
            size = 1
            for d in out.shape[1:]:
                size *= d
            return ring[0:out.shape[0], n % BANKS, 0:size]

        def by_vector(n):
            return dve_only or n % 2 == 1

        with st.block() as block:
            @block.sync
            def _(sp):
                for x in ahead:
                    x.issue(sp)

            @block.tensor
            def _(pe):
                loads.wait(pe)
                for n, (out, pairs, _) in enumerate(jobs):
                    m = n - BANKS
                    if m >= 0:
                        if dve_only:
                            pe.wait_ge(odd_read, m + 1)
                        else:
                            pe.wait_ge(odd_read if by_vector(m) else even_read, m // 2 + 1)
                    for i, (lhsT, rhs) in enumerate(pairs):
                        ins = pe.matmul(bank(n, out), lhsT, rhs, start=(i == 0), stop=(i == len(pairs) - 1))
                    ins.then_inc(product_ready, 1)

            if beside:
                @block.gpsimd
                def _(pool):
                    beside.gpsimd(pool)

            @block.scalar
            def _(act):
                if beside:
                    beside.scalar(act)
                for n, (out, _, evacuate) in enumerate(jobs):
                    if not by_vector(n):
                        act.wait_ge(product_ready, n + 1)
                        evacuate(act, out, bank(n, out)).then_inc(even_read, 1)

            @block.vector
            def _(v):
                if beside:
                    beside.vector(v)
                for n, (out, _, evacuate) in enumerate(jobs):
                    if by_vector(n):
                        v.wait_ge(product_ready, n + 1)
                        evacuate(v, out, bank(n, out)).then_inc(odd_read, 1)


def copy_out(eng, out, product):
    if len(out.shape) == 3:
        product = product.rearrange("p (a b) -> p a b", a=out.shape[1])
    if eng.engine == mybir.EngineType.Activation:
        return eng.activation(out, product, ACT.Copy)
    return eng.tensor_copy(out, product)


def finish_norm(nc, name, X, XT, ident, residual, total=None, base=None, out=None, also=None, eps=EPS5,
                scale=None, bias=None, needs=(), affine=None):
    total = total or (lambda t: X[:, t, :])
    base = base or (lambda t: X[:, t, :])
    out = out or (lambda t: X[:, t, :])
    RB, LAG = 4, 3
    with Stage(nc, name) as st:
        R = st.ps("R", [P, RB, 512])
        TP = st.ps("TP", [P, 2, 512])
        raw = st.sb("raw", [P, 2, 6])
        MV = st.sb("MV", [P, NT, 2])
        RS = st.sb("RS", [P, NT])
        stats_ready = st.sem("stats_ready")
        std_ready = st.sem("std_ready")
        residual_ready = st.sem("residual_ready")
        residual_read = st.sem("residual_read")
        normed = st.sem("normed")
        turned = st.sem("turned")
        turned_read = st.sem("turned_read")
        dve_chain = st.sem("dve_chain")
        pool_chain = st.sem("pool_chain")
        with st.block() as block:
            @block.tensor
            def _(pe):
                for x in needs:
                    x.wait(pe)
                for t in range(NT + LAG):
                    if t < NT:
                        if t >= RB:
                            pe.wait_ge(residual_read, t - RB + 1)
                        residual(pe, t, R[:, t % RB, 0:D]).then_inc(residual_ready, 1)
                    if t >= LAG and XT is not None:
                        u = t - LAG
                        pe.wait_ge(normed, u + 1)
                        if u >= 2:
                            pe.wait_ge(turned_read, u - 1)
                        for k in range(KD):
                            ins = pe.transpose(TP[:, u % 2, k * P:(k + 1) * P], out(u)[:, k * P:(k + 1) * P], ident[:, 0:P])
                        ins.then_inc(turned, 1)

            @block.vector
            def _(v):
                ch = Chain(v, dve_chain)
                for t in range(NT + 1):
                    u = t - 1
                    if t < NT:
                        v.wait_ge(residual_ready, t + 1)
                        v.tensor_tensor(total(t), R[:, t % RB, 0:D], base(t), ALU.add).then_inc(residual_read, 1)
                    if u >= 0:
                        v.wait_ge(std_ready, u + 1)
                        inverse = ch.mark(v.reciprocal(RS[:, u:u + 1], RS[:, u:u + 1]))
                    if t < NT:
                        v.wait_ge(residual_read, t + 1)
                        if t >= 2:
                            v.wait_ge(stats_ready, t - 1)
                        statistics = ch.mark(v.bn_stats(raw[:, t % 2, :], total(t)))
                        if also:
                            added = ch.mark(v.tensor_tensor(also(t), also(t), total(t), ALU.add))
                    if u >= 0:
                        ch.need(inverse)
                        v.tensor_scalar(out(u), total(u), MV[:, u, 0:1], RS[:, u:u + 1], ALU.subtract, ALU.mult).then_inc(normed, 1)
                    if t < NT:
                        ch.need(added if also else statistics)
                        v.bn_aggr(MV[:, t, :], raw[:, t % 2, :]).then_inc(stats_ready, 1)

            if affine is not None:
                @block.gpsimd
                def _(pool):
                    ch = Chain(pool, pool_chain)
                    for x in needs:
                        x.wait(pool)
                    for t in range(NT):
                        pool.wait_ge(normed, t + 1)
                        ch.link(pool.tensor_tensor(out(t), out(t), affine[:, 0, :], ALU.mult))
                        pool.tensor_tensor(out(t), out(t), affine[:, 1, :], ALU.add)

            @block.scalar
            def _(act):
                for t in range(NT + 2):
                    if t < NT:
                        act.wait_ge(stats_ready, t + 1)
                        act.activation(RS[:, t:t + 1], MV[:, t, 1:2], ACT.Sqrt, bias=ident[:, eps:eps + 1]).then_inc(std_ready, 1)
                    if t >= 2 and XT is not None:
                        u = t - 2
                        act.wait_ge(turned, u + 1)
                        if scale is None:
                            act.activation(XT[:, :, u * P:(u + 1) * P], TP[:, u % 2, 0:D].rearrange("p (k n) -> p k n", k=KD),
                                           ACT.Copy).then_inc(turned_read, 1)
                        else:
                            for k in range(KD):
                                ins = act.activation(XT[:, k, u * P:(u + 1) * P], TP[:, u % 2, k * P:(k + 1) * P],
                                                     ACT.Identity, scale=scale[:, k:k + 1], bias=bias[:, k:k + 1])
                            ins.then_inc(turned_read, 1)


GT = 4
POOL_TILE = 1


class NormBeside:

    def __init__(self, nc, st, x, out, ident):
        self.x, self.out, self.ident = x, out, ident
        self.raw = st.sb("norm_raw", [P, NT, 6])
        self.MV = st.sb("norm_MV", [P, NT, 2])
        self.RS = st.sb("norm_RS", [P, NT])
        self.stats_ready = st.sem("norm_stats_ready")
        self.std_ready = st.sem("norm_std_ready")
        self.scale_ready = st.sem("norm_scale_ready")
        self.chain = st.sem("norm_chain")

    def apply(self, eng, t):
        return eng.tensor_scalar(self.out[:, t, :], self.x[:, t, :], self.MV[:, t, 0:1], self.RS[:, t:t + 1], ALU.subtract, ALU.mult)

    def vector(self, v):
        ch = Chain(v, self.chain)
        for t in range(NT):
            ins = v.bn_stats(self.raw[:, t, :], self.x[:, t, :])
        ch.link(ins)
        for t in range(NT):
            ins = v.bn_aggr(self.MV[:, t, :], self.raw[:, t, :])
        ins.then_inc(self.stats_ready, 1)
        v.wait_ge(self.std_ready, 1)
        v.reciprocal(self.RS[:], self.RS[:]).then_inc(self.scale_ready, 1)
        v.wait_ge(self.scale_ready, 1)
        for t in range(0, NT, 2):
            self.apply(v, t)

    def gpsimd(self, pool):
        pool.wait_ge(self.scale_ready, 1)
        for t in range(1, NT, 2):
            self.apply(pool, t)

    def scalar(self, act):
        act.wait_ge(self.stats_ready, 1)
        act.activation(self.RS[:], self.MV[:, :, 1], ACT.Sqrt, bias=self.ident[:, EPS5:EPS5 + 1]).then_inc(self.std_ready, 1)


def norm_only(nc, name, x, out, XT, ident, base=None, eps=EPS5, scale=None, bias=None, loads=None, ahead=(),
              beside=None, store=None):
    with Stage(nc, name) as st:
        TP = st.ps("TP", [P, 4, 512])
        raw = st.sb("raw", [P, NT, 6])
        MV = st.sb("MV", [P, NT, 2])
        RS = st.sb("RS", [P, NT])
        stats_ready = st.sem("stats_ready")
        std_ready = st.sem("std_ready")
        scale_ready = st.sem("scale_ready")
        normed_dve = st.sem("normed_dve")
        normed_pool = st.sem("normed_pool")
        turned = st.sem("turned")
        turned_read = st.sem("turned_read")
        dve_chain = st.sem("dve_chain")

        def apply(eng, t):
            return eng.tensor_scalar(out[:, t, :], x[:, t, :], MV[:, t, 0:1], RS[:, t:t + 1], ALU.subtract, ALU.mult)

        with st.block() as block:
            @block.sync
            def _(sp):
                if loads:
                    loads.issue(sp)
                for a in ahead:
                    a.issue(sp)
                if beside:
                    beside.move(sp)
                if store:
                    result, stored = store
                    tiles_out = result.rearrange("b (h p) d -> p (b h) d", p=P)
                    for g in range(NT // GT):
                        sp.wait_ge(normed_dve, (g + 1) * (GT - 1))
                        sp.wait_ge(normed_pool, g + 1)
                        tiles = slice(g * GT, (g + 1) * GT)
                        sp.dma_start(tiles_out[:, tiles, :], out[:, tiles, :]).then_inc(stored, 16)
                    sp.wait_ge(stored, 16 * (NT // GT))

            @block.vector
            def _(v):
                ch = Chain(v, dve_chain)
                if beside:
                    beside.copy_kernel(v)
                for g in range(NT // GT + 1):
                    if g < NT // GT:
                        tiles = slice(g * GT, (g + 1) * GT)
                        if base is not None:
                            ch.link(v.tensor_tensor(x[:, tiles, :], x[:, tiles, :], base[:, tiles, :], ALU.add))
                        if beside:
                            ch.link(beside.add_answers(v, x, g))
                        for a in range(GT):
                            ins = v.bn_stats(raw[:, g * GT + a, :], x[:, g * GT + a, :])
                        ch.link(ins)
                        for a in range(GT):
                            ins = v.bn_aggr(MV[:, g * GT + a, :], raw[:, g * GT + a, :])
                        ins.then_inc(stats_ready, 1)
                    if g:
                        tiles = slice((g - 1) * GT, g * GT)
                        v.wait_ge(std_ready, g)
                        v.reciprocal(RS[:, tiles], RS[:, tiles]).then_inc(scale_ready, 1)
                        v.wait_ge(scale_ready, g)
                        for t in range((g - 1) * GT, g * GT):
                            if t % GT != POOL_TILE:
                                apply(v, t).then_inc(normed_dve, 1)
                if beside:
                    beside.copy_transform(v)

            @block.gpsimd
            def _(pool):
                if beside:
                    beside.gather(pool)
                for t in range(POOL_TILE, NT, GT):
                    pool.wait_ge(scale_ready, t // GT + 1)
                    apply(pool, t).then_inc(normed_pool, 1)

            @block.tensor
            def _(pe):
                if beside:
                    beside.kernel_products(pe)
                    beside.transform(pe)
                if XT is not None:
                    for t in range(NT):
                        if t % GT == POOL_TILE:
                            pe.wait_ge(normed_pool, t // GT + 1)
                        else:
                            pe.wait_ge(normed_dve, t // GT * (GT - 1) + t % GT + (t % GT < POOL_TILE))
                        if t >= 4:
                            pe.wait_ge(turned_read, t - 3)
                        for k in range(KD):
                            ins = pe.transpose(TP[:, t % 4, k * P:(k + 1) * P], out[:, t, k * P:(k + 1) * P], ident[:, 0:P])
                        ins.then_inc(turned, 1)

            @block.scalar
            def _(act):
                if loads:
                    loads.wait(act)
                for g in range(NT // GT + 1):
                    if g < NT // GT:
                        tiles = slice(g * GT, (g + 1) * GT)
                        act.wait_ge(stats_ready, g + 1)
                        act.activation(RS[:, tiles], MV[:, tiles, 1], ACT.Sqrt, bias=ident[:, eps:eps + 1]).then_inc(std_ready, 1)
                    if g and XT is not None:
                        for t in range((g - 1) * GT, g * GT):
                            act.wait_ge(turned, t + 1)
                            tok = slice(t * P, (t + 1) * P)
                            if scale is None:
                                act.activation(XT[:, :, tok], TP[:, t % 4, 0:D].rearrange("p (k n) -> p k n", k=KD),
                                               ACT.Copy).then_inc(turned_read, 1)
                            else:
                                for k in range(KD):
                                    ins = act.activation(XT[:, k, tok], TP[:, t % 4, k * P:(k + 1) * P], ACT.Identity,
                                                         scale=scale[:, k:k + 1], bias=bias[:, k:k + 1])
                                ins.then_inc(turned_read, 1)


DI, DS, DC = 512, 16, 4
NCH = DI // P
HALF = T // 2
NPASS = NCH * 2
BF16_ONE = 0x3F80


def stage_mamba(nc, io, X, XT, ident, KF, inputs):
    with ExitStack() as outer:
        U = outer.enter_context(nc.sbuf_tensor("mamba_U", [P, NPASS, HALF], F32))
        WO = outer.enter_context(nc.sbuf_tensor("mamba_WO", [P, NCH, D], F32))
        with Stage(nc, "mamba") as st:
            DU = st.sb("DU", [P, NPASS, HALF])
            E = st.sb("E", [P, NPASS, HALF])
            BC = st.sb("BC", [96, T], BF16)
            WD = st.sb("WD", [P, NCH, P])
            WBC = st.sb("WBC", [P, NCH, 96])
            SEL = st.sb("SEL", [96, 2 * DS, P], BF16)
            CW = st.sb("CW", [P, NCH, DC])
            VEC = st.sb("VEC", [P, 4, NCH])
            AA = st.sb("AA", [P, NPASS, DS])
            DV = st.sb("DV", [P, NPASS])
            with Stage(nc, "mamba_in") as s2:
                W = s2.sb("W", [P, KD, 2 * DI])
                SIL = s2.sb("SIL", [P, 2, G4])
                CV = s2.sb("CV", [P, 2, G4])
                R1 = s2.sb("R1", [96, 2, G4])
                MID = s2.sb("MID", [96, G4], BF16)
                UP = s2.ps("UP", [P, 2, G4])
                ZP = s2.ps("ZP", [P, 2, G4])
                PP = s2.ps("PP", [P, G4])
                DP = s2.ps("DP", [P, G4])
                loaded = s2.sem("loaded")
                uz_ready = s2.sem("uz_ready")
                u_read = s2.sem("u_read")
                silu_ready = s2.sem("silu_ready")
                gated = s2.sem("gated")
                proj_ready = s2.sem("proj_ready")
                bc_read = s2.sem("bc_read")
                exp_ready = s2.sem("exp_ready")
                a_exp = s2.sem("a_exp")
                dve_chain = s2.sem("dve_chain")
                w_loaded = s2.sem("w_loaded")
                x_load = Loads(nc, "x", [load_tokens(io, X)])
                NG = T // G4

                def group(buf, c, g):
                    return buf[:, 2 * c + g // 2, (g % 2) * G4:(g % 2 + 1) * G4]

                with s2.block() as block:
                    @block.sync
                    def _(sp):
                        sp.dma_start(W[:], io["L0_attn_in_projT"].rearrange("(k p) n -> p k n", p=P)).then_inc(w_loaded, 16)
                        sp.dma_start(WO[:], io["L0_attn_out_projT"].rearrange("(k p) n -> p k n", p=P)).then_inc(loaded, 16)
                        sp.dma_start(WD[:], io["L0_attn_x_delta"].rearrange("(k p) n -> p k n", p=P)).then_inc(loaded, 16)
                        sp.dma_start(WBC[:], io["L0_attn_x_bc"].rearrange("(k p) n -> p k n", p=P)).then_inc(loaded, 16)
                        sp.dma_start(SEL[:].bitcast(mybir.dt.uint16), io["sel_bc"]).then_inc(loaded, 16)
                        sp.dma_start(CW[:], io["L0_attn_conv_w"].rearrange("(k p) o n -> p k (o n)", p=P)).then_inc(loaded, 16)
                        sp.dma_start(VEC[:], io["L0_attn_vec"]).then_inc(loaded, 16)
                        for h in range(2):
                            sp.dma_start(AA[:].rearrange("p (c h) s -> p h c s", h=2)[:, h],
                                         io["L0_attn_A_log"].rearrange("(k p) s -> p k s", p=P)).then_inc(loaded, 16)
                        x_load.issue(sp)
                        x_load.wait(sp)

                    NLOAD = 8 * 16

                    @block.tensor
                    def _(pe):
                        pe.wait_ge(w_loaded, 16)
                        def project(g):
                            if g == 0:
                                pe.wait_ge(loaded, NLOAD)
                            pe.wait_ge(gated, (g + 1) * NCH)
                            if g:
                                pe.wait_ge(bc_read, g)
                                pe.wait_ge(exp_ready, g * NCH)
                            for dst, w, m in ((PP, WBC, 96), (DP, WD, P)):
                                for c in range(NCH):
                                    ins = pe.matmul(dst[0:m, :], w[:, c, :], group(U, c, g), start=(c == 0), stop=(c == NCH - 1))
                            ins.then_inc(proj_ready, 1)

                        for g in range(NG):
                            for c in range(NCH):
                                if c == 2 and g:
                                    project(g - 1)
                                n = g * NCH + c
                                if n >= 2:
                                    pe.wait_ge(u_read, n - 1)
                                    pe.wait_ge(silu_ready, n - 1)
                                for dst, col in ((UP, c * P), (ZP, DI + c * P)):
                                    for k in range(KD):
                                        ins = pe.matmul(dst[:, n % 2, :], W[:, k, col:col + P], XT[:, k, g * G4:(g + 1) * G4],
                                                        start=(k == 0), stop=(k == KD - 1))
                                ins.then_inc(uz_ready, 1)
                        project(NG - 1)

                    @block.scalar
                    def _(act):
                        act.wait_ge(loaded, NLOAD)
                        act.activation(AA[:], AA[:], ACT.Exp).then_inc(a_exp, 1)

                        def steps(g):
                            act.wait_ge(proj_ready, g + 1)
                            for c in range(NCH):
                                act.activation(group(E, c, g), DP[:], ACT.Exp, scale=VEC[:, 1, c:c + 1],
                                               bias=VEC[:, 2, c:c + 1]).then_inc(exp_ready, 1)

                        for g in range(NG):
                            for c in range(NCH):
                                n = g * NCH + c
                                act.wait_ge(uz_ready, n + 1)
                                if n >= 2:
                                    act.wait_ge(gated, n - 1)
                                act.activation(SIL[:, n % 2, :], ZP[:, n % 2, :], ACT.Silu).then_inc(silu_ready, 1)
                            if g:
                                steps(g - 1)
                        steps(NG - 1)

                    @block.vector
                    def _(v):
                        ch = Chain(v, dve_chain)
                        v.wait_ge(loaded, NLOAD)
                        v.wait_ge(a_exp, 1)
                        ch.link(v.tensor_scalar(AA[:], AA[:], -1.0, -3e38, ALU.mult, ALU.max))
                        for h in range(2):
                            ch.link(v.tensor_copy(DV[:].rearrange("p (c h) -> p h c", h=2)[:, h], VEC[:, 3, :]))
                        def split_rows(g):
                            v.wait_ge(gated, (g + 1) * NCH)
                            v.wait_ge(proj_ready, g + 1)
                            bc = BC[:, g * G4:(g + 1) * G4]
                            ch.link(v.tensor_copy(bc, PP[0:96, :]))
                            ch.link(v.tensor_tensor(R1[:, 0, :], PP[0:96, :], bc, ALU.subtract))
                            v.sem_inc(bc_read, 1)
                            ch.link(v.tensor_copy(MID[:], R1[:, 0, :]))
                            ch.link(v.tensor_tensor(R1[:, 1, :], R1[:, 0, :], MID[:], ALU.subtract))
                            ch.link(v.tensor_copy(bc[32:64], MID[32:64, :]))
                            ch.link(v.tensor_copy(bc[64:96], R1[64:96, 1, :]))
                            for c in range(NCH):
                                v.wait_ge(exp_ready, g * NCH + c + 1)
                                ch.link(v.scalar_tensor_tensor(group(DU, c, g), group(E, c, g), 1.0, group(U, c, g), ALU.add, ALU.mult))

                        for g in range(NG):
                            for c in range(NCH):
                                n = g * NCH + c
                                v.wait_ge(uz_ready, n + 1)
                                cv = CV[:, n % 2, :]
                                ch.link(v.tensor_scalar(cv, UP[:, n % 2, :], CW[:, c, DC - 1:DC], VEC[:, 0, c:c + 1], ALU.mult, ALU.add))
                                for s in range(1, DC):
                                    o = cv.rearrange("p (b t) -> p b t", t=S)[:, :, s:]
                                    i = UP[:, n % 2, :].rearrange("p (b t) -> p b t", t=S)[:, :, 0:S - s]
                                    ch.link(v.scalar_tensor_tensor(o, i, CW[:, c, DC - 1 - s:DC - s], o, ALU.mult, ALU.add))
                                v.sem_inc(u_read, 1)
                                v.wait_ge(silu_ready, n + 1)
                                v.tensor_tensor(group(U, c, g), cv, SIL[:, n % 2, :], ALU.mult).then_inc(gated, 1)
                            if g:
                                split_rows(g - 1)
                        split_rows(NG - 1)

            next_inputs = xattn_inputs(nc, io)
            with Stage(nc, "scan") as s3:
                NROW = (T // G4) * DS
                N = NROW * NCH
                RING = 3
                AB = s3.sb("AB", [P, 2, G4])
                BU = s3.sb("BU", [P, RING, G4])
                H = s3.sb("H", [P, RING, G4])
                CS = s3.sb("CS", [P, 2, G4])
                HC = s3.sb("HC", [P, RING, G4])
                YP = s3.ps("YP", [P, NCH, G4])
                BP = s3.ps("BP", [P, 2, G4])
                CP = s3.ps("CP", [P, 2, G4])
                zeroed = s3.sem("zeroed")
                b_ready = s3.sem("b_ready")
                c_ready = s3.sem("c_ready")
                decay_ready = s3.sem("decay_ready")
                c_copied = s3.sem("c_copied")
                bu_ready = s3.sem("bu_ready")
                h_ready = s3.sem("h_ready")
                hc_ready = s3.sem("hc_ready")
                y_added = s3.sem("y_added")
                y_read = s3.sem("y_read")

                def at(n):
                    r, c = divmod(n, NCH)
                    return r, r // DS, r % DS, c

                def tokens(buf, c, g):
                    return buf[:, 2 * c + g // 2, (g % 2) * G4:(g % 2 + 1) * G4]

                def later(x):
                    return x.rearrange("p (b t) -> p b t", t=S)[:, :, 1:]

                with s3.block() as block:
                    @block.sync
                    def _(sp):
                        next_inputs.loads.issue(sp)

                    @block.gpsimd
                    def _(pool):
                        pool.memset(AB[:], 0.0).then_inc(zeroed, 1)
                        for n in range(N):
                            r, g, s, c = at(n)
                            pool.wait_ge(h_ready, n + 1)
                            if c == 0:
                                pool.wait_ge(c_copied, r + 1)
                            if n >= RING:
                                pool.wait_ge(y_added, n - RING + 1)
                            pool.tensor_tensor(HC[:, n % RING, :], H[:, n % RING, :], CS[:, r % 2, :], ALU.mult).then_inc(hc_ready, 1)

                    @block.tensor
                    def _(pe):
                        def spread(r):
                            g, s = divmod(r, DS)
                            if r >= 2:
                                pe.wait_ge(bu_ready, NCH * (r - 1))
                            tok = slice(g * G4, (g + 1) * G4)
                            pe.matmul(BP[:, r % 2, :], SEL[:, s, :], BC[:, tok], start=True, stop=True).then_inc(b_ready, 1)
                            if r >= 2:
                                pe.wait_ge(c_copied, r - 1)
                            pe.matmul(CP[:, r % 2, :], SEL[:, DS + s, :], BC[:, tok], start=True, stop=True).then_inc(c_ready, 1)

                        spread(0)
                        spread(1)
                        for n in range(N):
                            r, g, s, c = at(n)
                            if c == NCH - 1 and r + 2 < NROW:
                                spread(r + 2)
                            pe.wait_ge(hc_ready, n + 1)
                            if g and s == 0:
                                pe.wait_ge(y_read, (g - 1) * NCH + c + 1)
                            pe.matmul(YP[:, c, :], ident[:, 0:P], HC[:, n % RING, :], start=(s == 0), stop=(s == DS - 1)).then_inc(y_added, 1)

                    @block.scalar
                    def _(act):
                        def copy_c(r):
                            act.wait_ge(c_ready, r + 1)
                            if r >= 2:
                                act.wait_ge(hc_ready, NCH * (r - 1))
                            act.activation(CS[:, r % 2, :], CP[:, r % 2, :], ACT.Copy).then_inc(c_copied, 1)

                        act.wait_ge(zeroed, 1)
                        copy_c(0)
                        for n in range(N):
                            r, g, s, c = at(n)
                            if n >= 2:
                                act.wait_ge(h_ready, n - 1)
                            act.activation(later(AB[:, n % 2, :]), later(tokens(E, c, g)), ACT.Exp, scale=AA[:, 2 * c, s:s + 1],
                                           bias=AA[:, 2 * c, s:s + 1]).then_inc(decay_ready, 1)
                            if c == NCH - 2 and r + 1 < NROW:
                                copy_c(r + 1)

                    @block.vector
                    def _(v):
                        def inputs(n):
                            r, g, s, c = at(n)
                            if c == 0:
                                v.wait_ge(b_ready, r + 1)
                            if n >= RING:
                                v.wait_ge(h_ready, n - RING + 1)
                            v.tensor_tensor(BU[:, n % RING, :], tokens(DU, c, g), BP[:, r % 2, :], ALU.mult).then_inc(bu_ready, 1)

                        def y_out(g, c):
                            v.wait_ge(y_added, ((g + 1) * DS - 1) * NCH + c + 1)
                            u = tokens(U, c, g)
                            v.scalar_tensor_tensor(u, u, DV[:, 2 * c:2 * c + 1], YP[:, c, :], ALU.mult, ALU.add).then_inc(y_read, 1)

                        inputs(0)
                        for n in range(N):
                            r, g, s, c = at(n)
                            if n + 1 < N:
                                inputs(n + 1)
                            v.wait_ge(bu_ready, n + 1)
                            v.wait_ge(decay_ready, n + 1)
                            if n >= RING:
                                v.wait_ge(hc_ready, n - RING + 1)
                            v.tensor_tensor_scan(H[:, n % RING, :], AB[:, n % 2, :], BU[:, n % RING, :], 0.0, ALU.mult, ALU.add).then_inc(h_ready, 1)
                            k = n - g * DS * NCH - 1
                            if g and 0 <= k < NCH:
                                y_out(g - 1, k)
                        for c in range(NCH):
                            y_out(T // G4 - 1, c)

        def out_product(pe, t, out):
            h, col = t // (NT // 2), (t % (NT // 2)) * P
            for c in range(NCH):
                ins = pe.matmul(out, U[:, 2 * c + h, col:col + P], WO[:, c, :], start=(c == 0), stop=(c == NCH - 1))
            return ins

        finish_norm(nc, "mamba_norm", X, XT, ident, out_product)
    return next_inputs


NHEAD, DH = 8, 64
INNER = NHEAD * DH
NIN = INNER // P
DCTX = 192
KC = [P, DCTX - P]


def load_context(io, CT):
    return [(CT[0:KC[k], k, :], io["ctxT"][k * P:k * P + KC[k], :]) for k in range(2)]


def load_split(W, src):
    return [(W[0:KC[k], k, :], src[k * P:k * P + KC[k], :]) for k in range(2)]


def xattn_inputs(nc, io):
    x = Inputs(nc, "xattn")
    x.CT = x.sb("CT", [P, 2, T])
    x.WQ = x.sb("WQ", [P, KD, INNER])
    x.WK = x.sb("WK", [P, 2, INNER])
    x.WV = x.sb("WV", [P, 2, INNER])
    x.pairs = load_context(io, x.CT) + load_split(x.WK, io["L0_xattn_Wk"]) + load_split(x.WV, io["L0_xattn_Wv"]) + [
        (x.WQ[:], io["L0_xattn_Wq"].rearrange("(k p) n -> p k n", p=P))]
    return x.ready()


def stage_xattn(nc, io, X, XT, ident, KF, inputs):
    with Stage(nc, "xa") as st:
        QT = st.sb("QT", [P, NIN, T])
        WO = st.sb("WO", [P, NIN, D])
        BO = st.sb("BO", [P, D])
        with Stage(nc, "xb") as s1:
            KT = s1.sb("KT", [P, NIN, T])
            V = s1.sb("V", [P, NT, INNER])
            CT, WQ, WK, WV = inputs.CT, inputs.WQ, inputs.WK, inputs.WV
            jobs = []
            for g in range(T // G4):
                tok = slice(g * G4, (g + 1) * G4)
                for c in range(NIN):
                    col = slice(c * P, (c + 1) * P)
                    jobs.append((QT[:, c, tok], [(WQ[:, k, col], XT[:, k, tok]) for k in range(KD)], copy_out))
                    jobs.append((KT[:, c, tok], [(WK[0:KC[k], k, col], CT[0:KC[k], k, tok]) for k in range(2)], copy_out))
            for t in range(NT):
                jobs.append((V[:, t, :], [(CT[0:KC[k], k, t * P:(t + 1) * P], WV[0:KC[k], k, :]) for k in range(2)], copy_out))
            out_loads = Loads(nc, "xout", [(WO[:], io["L0_xattn_Wo"].rearrange("(k p) n -> p k n", p=P)), (BO[:], io["L0_xattn_bo"])])
            products(nc, "xproj", jobs, inputs.loads, ahead=[out_loads])
            inputs.free()

            attention(nc, ident, QT, KT, V, X, BO, out_loads)

        def out_product(pe, t, out):
            for c in range(NIN):
                ins = pe.matmul(out, QT[:, c, t * P:(t + 1) * P], WO[:, c, :], start=(c == 0), stop=(c == NIN - 1))
            return ins

        finish_norm(nc, "xnorm", X, XT, ident, out_product, needs=[out_loads])


def attention(nc, ident, QT, KT, V, X, BO, out_loads):
    NU = B * NIN
    SCALE = float(DH) ** -0.5
    with Stage(nc, "attn") as st:
        PR = st.sb("PR", [P, 2, 4, S])
        PN = st.sb("PN", [P, 2, 4, S])
        PT = st.sb("PT", [P, 2, 2, 2, S])
        MX = st.sb("MX", [P, NU, 4])
        SM = st.sb("SM", [P, NU, 4])
        SC = st.ps("SC", [P, 2, 4, S])
        TP = st.ps("TP", [P, 2, 2, S])
        OT = st.ps("OT", [P, 2, 512])
        scores_ready = st.sem("scores_ready")
        max_ready = st.sem("max_ready")
        exp_ready = st.sem("exp_ready")
        sum_ready = st.sem("sum_ready")
        probs_ready = st.sem("probs_ready")
        turned = st.sem("turned")
        turned_act = st.sem("turned_act")
        turned_dve = st.sem("turned_dve")
        out_ready = st.sem("out_ready")
        out_copied = st.sem("out_copied")
        dve_chain = st.sem("dve_chain")
        with st.block() as block:
            @block.tensor
            def _(pe):
                def scores(m):
                    b, c = m // NIN, m % NIN
                    if m >= 2:
                        pe.wait_ge(exp_ready, m - 1)
                    for t in range(2):
                        for h in range(2):
                            r = slice(h * DH, (h + 1) * DH)
                            ins = pe.matmul(SC[:, m % 2, 2 * h + t, :], QT[r, c, b * S + t * P:b * S + (t + 1) * P],
                                            KT[r, c, b * S:(b + 1) * S], start=True, stop=True)
                    ins.then_inc(scores_ready, 1)

                def values(m):
                    b, c = m // NIN, m % NIN
                    pe.wait_ge(turned_act, m + 1)
                    pe.wait_ge(turned_dve, m + 1)
                    if m >= 2:
                        pe.wait_ge(out_copied, m - 1)
                    for h in range(2):
                        for k in range(2):
                            ins = pe.matmul(OT[h * DH:(h + 1) * DH, m % 2, 0:S], V[:, 2 * b + k, c * P + h * DH:c * P + (h + 1) * DH],
                                            PT[:, m % 2, h, k, :], start=(k == 0), stop=(k == 1))
                    ins.then_inc(out_ready, 1)

                scores(0)
                scores(1)
                for m in range(NU):
                    if m + 2 < NU:
                        scores(m + 2)
                    pe.wait_ge(probs_ready, m + 1)
                    if m:
                        pe.wait_ge(turned_act, m)
                        pe.wait_ge(turned_dve, m)
                    for h in range(2):
                        for k in range(2):
                            for t in range(2):
                                ins = pe.transpose(TP[:, h, k, t * P:(t + 1) * P], PN[:, m % 2, 2 * h + t, k * P:(k + 1) * P], ident[:, 0:P])
                        ins.then_inc(turned, 1)
                    if m:
                        values(m - 1)
                values(NU - 1)

            @block.scalar
            def _(act):
                def exps(m):
                    act.wait_ge(max_ready, m + 1)
                    if m >= 2:
                        act.wait_ge(probs_ready, m - 1)
                    for j in range(4):
                        ins = act.activation(PR[:, m % 2, j, :], SC[:, m % 2, j, :], ACT.Exp, scale=SCALE,
                                             bias=MX[:, m, j:j + 1], accum_out=SM[:, m, j:j + 1])
                    ins.then_inc(exp_ready, 1)

                def out_copy(m):
                    act.wait_ge(out_ready, m + 1)
                    b, c = m // NIN, m % NIN
                    act.activation(QT[:, c, b * S:(b + 1) * S], OT[:, m % 2, 0:S], ACT.Copy).then_inc(out_copied, 1)

                exps(0)
                for m in range(NU):
                    if m + 1 < NU:
                        exps(m + 1)
                    act.wait_ge(turned, 2 * m + 1)
                    if m >= 2:
                        act.wait_ge(out_ready, m - 1)
                    act.activation(PT[:, m % 2, 0], TP[:, 0], ACT.Copy).then_inc(turned_act, 1)
                    if m:
                        out_copy(m - 1)
                out_copy(NU - 1)


            @block.gpsimd
            def _(pool):
                out_loads.wait(pool)
                add_row(pool, X, BO)
                for m in range(NU):
                    pool.wait_ge(sum_ready, m + 1)
                    if m >= 2:
                        pool.wait_ge(turned, 2 * (m - 1))
                    pool.tensor_tensor(PN[:, m % 2], PR[:, m % 2], SM[:, m, :].rearrange("p (j o) -> p j o", o=1).to_broadcast([P, 4, S]),
                                       ALU.mult).then_inc(probs_ready, 1)

            @block.vector
            def _(v):
                ch = Chain(v, dve_chain)

                def maxima(m):
                    v.wait_ge(scores_ready, m + 1)
                    ch.link(v.tensor_reduce(MX[:, m, :], SC[:, m % 2], AX_X, ALU.max))
                    v.tensor_scalar(MX[:, m, :], MX[:, m, :], -SCALE, None, ALU.mult).then_inc(max_ready, 1)

                def sums(m):
                    v.wait_ge(exp_ready, m + 1)
                    v.reciprocal(SM[:, m, :], SM[:, m, :]).then_inc(sum_ready, 1)

                maxima(0)
                maxima(1)
                sums(0)
                for m in range(NU):
                    if m + 2 < NU:
                        maxima(m + 2)
                    if m + 1 < NU:
                        sums(m + 1)
                    v.wait_ge(turned, 2 * m + 2)
                    if m >= 2:
                        v.wait_ge(out_ready, m - 1)
                    v.tensor_copy(PT[:, m % 2, 1], TP[:, 1]).then_inc(turned_dve, 1)


NE, HID = 16, 1024
CAP = int(1.25 * T / NE)
SLOTS = NE * CAP
HC_ = CAP // 2
NHID = HID // P


NST = 64
LO = 16
NF = 2 * 2
MAGIC = 1.5 * 2 ** 23
TURN = 6.2831845
HI = S // LO
LB = P // HI


class S4dTables:

    def __init__(self, keep, st, io):
        self.io = io
        self.UU = keep.sb("UU", [P, D, LO])
        self.VV = keep.sb("VV", [P, D, LO])
        self.U2 = st.sb("U2", [P, D, LO])
        self.TT = st.sb("TT", [P, D, LO])
        self.HIGH = st.sb("HIGH", [P, D, LO])
        self.LOW = st.sb("LOW", [P, D, LO])
        self.PAR = st.sb("PAR", [P, 5, D])
        self.COL = st.sb("COL", [P, 4])
        self.AR = st.sb("AR", [P, D])
        self.AI = st.sb("AI", [P, D])
        self.W = st.sb("W", [P, 12, D])
        self.loaded = st.sem("tables_loaded")
        self.dt_ready = st.sem("dt_ready")
        self.exponents_ready = st.sem("exponents_ready")
        self.tanh_ready = st.sem("tanh_ready")
        self.phases_ready = st.sem("phases_ready")
        self.small_sines = st.sem("small_sines")
        self.moduli_ready = st.sem("moduli_ready")
        self.fraction_ready = st.sem("fraction_ready")
        self.sine_ready = st.sem("sine_ready")
        self.factor_ready = st.sem("factor_ready")
        self.pool_chain = st.sem("tables_pool_chain")
        self.small_chain = st.sem("tables_small_chain")

    def load(self, sp):
        sp.dma_start(self.PAR[:], self.io["L1_xattn_s4d"]).then_inc(self.loaded, 16)
        sp.dma_start(self.COL[:], self.io["phases"]).then_inc(self.loaded, 16)

    def powers(self, act, out, x, func, step, bias=0.0):
        for l in range(LO):
            ins = act.activation(out[:, :, l], x[:], func, scale=float(step * l), bias=bias)
        return ins

    def scalar_step(self, act, n):
        if n == 0:
            act.wait_ge(self.loaded, 32)
            act.activation(self.PAR[:, 0, :], self.PAR[:, 0, :], ACT.Exp).then_inc(self.dt_ready, 1)
            act.wait_ge(self.exponents_ready, 1)
            act.activation(self.W[:, 0, :], self.AR[:], ACT.Tanh, scale=0.5).then_inc(self.tanh_ready, 1)
            self.powers(act, self.UU, self.AI, ACT.Identity, LO, self.COL[:, 0:1]).then_inc(self.phases_ready, 1)
        elif n == 1:
            self.powers(act, self.U2, self.AI, ACT.Identity, LO, self.COL[:, 1:2]).then_inc(self.phases_ready, 1)
        elif n == 2:
            self.powers(act, self.VV, self.AI, ACT.Identity, 1, self.COL[:, 2:3]).then_inc(self.phases_ready, 1)
        elif n == 3:
            act.wait_ge(self.exponents_ready, 2)
            act.activation(self.W[:, 1:4, :], self.W[:, 1:4, :], ACT.Sin, scale=TURN).then_inc(self.small_sines, 1)
        elif n == 4:
            self.powers(act, self.HIGH, self.AR, ACT.Exp, LO).then_inc(self.moduli_ready, 1)
        elif n == 5:
            self.powers(act, self.LOW, self.AR, ACT.Exp, 1).then_inc(self.moduli_ready, 1)
        elif n in (9, 10, 11):
            act.wait_ge(self.fraction_ready, n - 8)
            x = (self.UU, self.U2, self.VV)[n - 9]
            act.activation(x[:], x[:], ACT.Sin, scale=TURN).then_inc(self.sine_ready, 1)

    def exponents(self, v):
        ch = self.small = Chain(v, self.small_chain)
        v.wait_ge(self.loaded, 32)
        v.wait_ge(self.dt_ready, 1)
        ch.link(v.tensor_tensor(self.AR[:], self.PAR[:, 1, :], self.PAR[:, 0, :], ALU.mult))
        ch.link(v.tensor_tensor(self.AI[:], self.PAR[:, 2, :], self.PAR[:, 0, :], ALU.mult))
        v.tensor_scalar(self.AI[:], self.AI[:], 1.0 / (2 * np.pi), None, ALU.mult).then_inc(self.exponents_ready, 1)
        v.wait_ge(self.exponents_ready, 1)
        W = self.W
        v.tensor_scalar(W[:, 1, :], self.AI[:], 0.25, None, ALU.add)
        v.tensor_copy(W[:, 2, :], self.AI[:])
        ch.link(v.tensor_scalar(W[:, 3, :], self.AI[:], 0.5, None, ALU.mult))
        ch.link(v.tensor_scalar(W[:, 4:7, :], W[:, 1:4, :], MAGIC, None, ALU.add))
        ch.link(v.tensor_scalar(W[:, 4:7, :], W[:, 4:7, :], MAGIC, None, ALU.subtract))
        v.tensor_tensor(W[:, 1:4, :], W[:, 1:4, :], W[:, 4:7, :], ALU.subtract).then_inc(self.exponents_ready, 1)

    def combine(self, v, out, a, b, c, d, op):
        t11, t4 = self.W[:, 11, :], self.W[:, 4, :]
        v.tensor_tensor(t11, a, b, ALU.mult)
        self.small.link(v.tensor_tensor(t4, c, d, ALU.mult))
        self.small.link(v.tensor_tensor(out, t11, t4, op))

    def factor_step(self, v, n):
        ch = self.small
        th, s1, s2, s3, t4, t5, er, ei, nr, ni, a2, t11 = (self.W[:, i, :] for i in range(12))
        Ar, Ai, Cr, Ci = (self.PAR[:, i, :] for i in range(1, 5))
        if n == 0:
            v.wait_ge(self.tanh_ready, 1)
            v.wait_ge(self.small_sines, 1)
            ch.link(v.tensor_scalar(t4, th, -1.0, 1.0, ALU.mult, ALU.add))
            ch.link(v.reciprocal(t4, t4))
            v.tensor_tensor(s3, s3, s3, ALU.mult)
            ch.link(v.scalar_tensor_tensor(t5, th, 2.0, t4, ALU.mult, ALU.mult))
            ch.link(v.tensor_tensor(er, t5, s1, ALU.mult))
            v.scalar_tensor_tensor(ei, t5, 1.0, s2, ALU.add, ALU.mult)
            ch.link(v.scalar_tensor_tensor(er, s3, -2.0, er, ALU.mult, ALU.add))
        elif n == 1:
            self.combine(v, nr, Cr, er, Ci, ei, ALU.subtract)
            self.combine(v, ni, Cr, ei, Ci, er, ALU.add)
            self.combine(v, a2, Ar, Ar, Ai, Ai, ALU.add)
        elif n == 2:
            ch.link(v.reciprocal(a2, a2))
            self.combine(v, er, nr, Ar, ni, Ai, ALU.add)
            self.combine(v, ei, ni, Ar, nr, Ai, ALU.subtract)
            ch.link(v.tensor_tensor(er, er, a2, ALU.mult))
            v.tensor_tensor(ei, ei, a2, ALU.mult).then_inc(self.factor_ready, 1)

    def gpsimd_program(self, pool):
        ch = Chain(pool, self.pool_chain)

        def wide(x):
            return x.rearrange("p (d o) -> p d o", o=1).to_broadcast([P, D, LO])

        for n, x in enumerate((self.UU, self.U2, self.VV)):
            pool.wait_ge(self.phases_ready, n + 1)
            ch.link(pool.tensor_scalar(self.TT[:], x[:], MAGIC, None, ALU.add))
            ch.link(pool.tensor_scalar(self.TT[:], self.TT[:], MAGIC, None, ALU.subtract))
            pool.tensor_tensor(x[:], x[:], self.TT[:], ALU.subtract).then_inc(self.fraction_ready, 1)
            pool.wait_ge(self.fraction_ready, n + 1)
        pool.wait_ge(self.moduli_ready, 2)
        for n, (x, modulus) in enumerate(((self.UU, self.HIGH), (self.U2, self.HIGH), (self.VV, self.LOW))):
            pool.wait_ge(self.sine_ready, n + 1)
            ch.link(pool.tensor_tensor(x[:], x[:], modulus[:], ALU.mult))
        pool.wait_ge(self.factor_ready, 1)
        er, ei = self.W[:, 6, :], self.W[:, 7, :]
        pool.tensor_tensor(self.UU[:], self.UU[:], wide(er), ALU.mult)
        ch.link(pool.tensor_tensor(self.U2[:], self.U2[:], wide(ei), ALU.mult))
        pool.tensor_tensor(self.UU[:], self.UU[:], self.U2[:], ALU.add)


class Combine:

    BANKS = 4
    DB = 512 // LO

    def __init__(self, nc, st, io, tables, answers, FROM, WT, GA, KF):
        self.tables, self.answers, self.FROM, self.WT, self.GA, self.KF = tables, answers, FROM, WT, GA, KF
        self.WK = st.sb("WK", [P, LO // LB, NF, P])
        self.KA = st.sb("KA", [HI, LO, D])
        self.KB = st.sb("KB", [P, LO // LB, D])
        self.KP = st.ps("KP", [P, self.BANKS, 512])
        self.loads = Loads(nc, "dft_kernel", [(self.WK[:], io["dft_kernel"])])
        self.gathered = [st.sem(f"gathered{g}") for g in range(NT // GT)]
        self.k_ready = st.sem("k_ready")
        self.k_copied = st.sem("k_copied")
        self.k_moved = st.sem("k_moved")
        self.kf_ready = st.sem("kf_ready")

    def gather(self, pool):
        for t in range(NT):
            pool.indirect_dma_start(out=self.GA[:, t, :], out_offset=None, in_=self.answers,
                                    in_offset=bass.IndirectOffsetOnAxis(ap=self.FROM[:, t:t + 1], axis=0)).then_inc(self.gathered[t // GT], 16)

    def add_answers(self, v, x, g):
        v.wait_ge(self.gathered[g], 16 * GT)
        for t in range(g * GT, (g + 1) * GT):
            ins = v.scalar_tensor_tensor(x[:, t, :], self.GA[:, t, :], self.WT[:, t:t + 1], x[:, t, :], ALU.mult, ALU.add)
        return ins

    def move(self, sp):
        self.loads.issue(sp)
        sp.wait_ge(self.k_copied, D // self.DB)
        for l in range(LO):
            sp.dma_start(self.KB[l % LB * HI:(l % LB + 1) * HI, l // LB, :], self.KA[:, l, :]).then_inc(self.k_moved, 16)

    def kernel_products(self, pe):
        for d in range(D):
            n, i = divmod(d, self.DB)
            if i == 0 and n >= self.BANKS:
                pe.wait_ge(self.k_copied, n - self.BANKS + 1)
            ins = pe.matmul(self.KP[0:HI, n % self.BANKS, i * LO:(i + 1) * LO], self.tables.UU[:, d, :], self.tables.VV[:, d, :], start=True, stop=True)
            if i == self.DB - 1:
                ins.then_inc(self.k_ready, 1)

    def transform(self, pe):
        pe.wait_ge(self.k_copied, D // self.DB)
        self.loads.wait(pe)
        pe.wait_ge(self.k_moved, 16 * LO)
        for q in range(NF):
            for i in range(LO // LB):
                ins = pe.matmul(self.KP[:, q, 0:D], self.WK[:, i, q, :], self.KB[:, i, :], start=(i == 0), stop=(i == LO // LB - 1))
            ins.then_inc(self.kf_ready, 1)

    def copy_kernel(self, v):
        for n in range(D // self.DB):
            v.wait_ge(self.k_ready, n + 1)
            v.tensor_scalar(self.KA[:, :, n * self.DB:(n + 1) * self.DB].rearrange("p l d -> p d l"),
                            self.KP[0:HI, n % self.BANKS, :].rearrange("p (d l) -> p d l", l=LO), 2.0, None, ALU.mult).then_inc(self.k_copied, 1)

    def copy_transform(self, v):
        for q in range(NF):
            v.wait_ge(self.kf_ready, q + 1)
            v.tensor_copy(self.KF[:, q, :], self.KP[:, q, 0:D])


def stage_moe(nc, io, X, XT, ident, KF, inputs):
    dispatch = nc.dram_tensor("moe_dispatch", (SLOTS + T, D), F32).ap()
    answers = nc.dram_tensor("moe_answers", (SLOTS, D), F32).ap()
    with Stage(nc, "moe") as st:
        TO = st.sb("TO", [P, NT], I32)
        FROM = st.sb("FROM", [P, NT], I32)
        WT = st.sb("WT", [P, NT])
        W1 = st.sb("W1", [P, 2, KD, HID])
        W2 = st.sb("W2", [P, 2, NHID, D])
        first_loads = Loads(nc, "first_experts", [(W[:, e], io[n][e].rearrange("(k p) n -> p k n", p=P)) for e in range(2)
                                                  for W, n in ((W1, "L0_ffn_w1"), (W2, "L0_ffn_w2"))])
        moe_route(nc, io, X, XT, TO, FROM, WT, dispatch, first_loads)
        with Stage(nc, "s4") as keep:
            with Stage(nc, "s4t") as s1:
                tables = S4dTables(keep, s1, io)
                moe_experts(nc, io, ident, dispatch, answers, tables, W1, W2, first_loads)
            GA = keep.sb("GA", [P, NT, D])
            with Stage(nc, "combine") as s1:
                norm_only(nc, "moenorm", X, X, None, ident, beside=Combine(nc, s1, io, tables, answers, FROM, WT, GA, KF))


def moe_route(nc, io, X, XT, TO, FROM, WT, dispatch, first_loads):
    with Stage(nc, "route") as st:
        GW = st.sb("GW", [P, KD, NE])
        TRI = st.sb("TRI", [P, 2, P])
        EI = st.sb("EI", [P, NE])
        TI = st.sb("TI", [P, NT])
        ZERO = st.sb("ZERO", [P, SLOTS // P * D])
        MX = st.sb("MX", [P, NT, 8])
        MI = st.sb("MI", [P, NT, 8], U32)
        NM = st.sb("NM", [P, NT])
        EX = st.sb("EX", [P, NT, NE])
        SM = st.sb("SM", [P, NT])
        OH = st.sb("OH", [P, NT, NE])
        RUN = st.sb("RUN", [P, 2, NT, NE])
        FI = st.sb("FI", [P, NT])
        LOC = st.sb("LOC", [P, NT])
        KEEP = st.sb("KEEP", [P, NT])
        FT = st.sb("FT", [P, NT])
        LG = st.ps("LG", [P, NT, NE])
        CS = st.ps("CS", [P, NT, NE])
        loaded = st.sem("loaded")
        zero_ready = st.sem("zero_ready")
        zeroed = st.sem("zeroed")
        logits_ready = st.sem("logits_ready")
        max_ready = st.sem("max_ready")
        exp_ready = st.sem("exp_ready")
        onehot_ready = st.sem("onehot_ready")
        counted = st.sem("counted")
        routed = st.sem("routed")
        sent = st.sem("sent")
        dve_chain = st.sem("dve_chain")
        with st.block() as block:
            @block.sync
            def _(sp):
                sp.dma_start(GW[:], io["L0_ffn_gateT"].rearrange("(k p) n -> p k n", p=P)).then_inc(loaded, 16)
                sp.dma_start(TRI[:], io["tri"]).then_inc(loaded, 16)
                sp.dma_start(EI[:], io["expert_numbers"]).then_inc(loaded, 16)
                sp.dma_start(TI[:], io["spill_rows"]).then_inc(loaded, 16)
                sp.wait_ge(zero_ready, 1)
                sp.dma_start(dispatch[0:SLOTS, :].rearrange("(p r) d -> p (r d)", p=P), ZERO[:]).then_inc(zeroed, 16)
                first_loads.issue(sp)

            @block.tensor
            def _(pe):
                pe.wait_ge(loaded, 64)
                for t in range(NT):
                    for k in range(KD):
                        ins = pe.matmul(LG[:, t, :], XT[:, k, t * P:(t + 1) * P], GW[:, k, :], start=(k == 0), stop=(k == KD - 1))
                ins.then_inc(logits_ready, 1)
                pe.wait_ge(onehot_ready, 1)
                for t in range(NT):
                    if t:
                        pe.matmul(CS[:, t, :], TRI[:, 1, :], RUN[:, 0, t, :], start=True, stop=False)
                    ins = pe.matmul(CS[:, t, :], TRI[:, 0, :], OH[:, t, :], start=(t == 0), stop=True)
                ins.then_inc(counted, 1)

            @block.scalar
            def _(act):
                act.wait_ge(max_ready, 1)
                for t in range(NT):
                    ins = act.activation(EX[:, t, :], LG[:, t, :], ACT.Exp, bias=NM[:, t:t + 1], accum_out=SM[:, t:t + 1])
                ins.then_inc(exp_ready, 1)

            @block.vector
            def _(v):
                ch = Chain(v, dve_chain)
                v.memset(ZERO[:], 0.0).then_inc(zero_ready, 1)
                v.wait_ge(loaded, 64)
                v.wait_ge(logits_ready, 1)
                for t in range(NT):
                    ins = v.max(MX[:, t, :], LG[:, t, :])
                ch.link(ins)
                for t in range(NT):
                    ins = v.max_index(MI[:, t, :], MX[:, t, :], LG[:, t, :])
                ch.link(ins)
                v.tensor_scalar(NM[:], MX[:, :, 0], -1.0, None, ALU.mult).then_inc(max_ready, 1)
                ch.link(v.tensor_copy(FI[:], MI[:, :, 0]))
                ch.link(v.tensor_tensor(OH[:], EI[:].rearrange("p (o e) -> p o e", o=1).to_broadcast([P, NT, NE]),
                                        FI[:].rearrange("p (t o) -> p t o", o=1).to_broadcast([P, NT, NE]), ALU.is_equal))
                v.memset(RUN[:, 0, 0, :], 0.0)
                v.memset(RUN[:, 1, 0, :], 0.0)
                ch.link(v.tensor_copy(RUN[:, 0, 1:, :], OH[:, 0:NT - 1, :]))
                for i in range(4):
                    d, old, new = 2 ** i, i % 2, (i + 1) % 2
                    v.tensor_copy(RUN[:, new, 1:1 + d, :], RUN[:, old, 1:1 + d, :])
                    ch.link(v.tensor_tensor(RUN[:, new, 1 + d:, :], RUN[:, old, 1 + d:, :], RUN[:, old, 1:NT - d, :], ALU.add))
                v.sem_inc(onehot_ready, 1)
                v.wait_ge(counted, 1)
                ch.link(v.tensor_tensor(OH[:], OH[:], CS[:], ALU.mult))
                ch.link(v.tensor_reduce(LOC[:], OH[:], AX_X, ALU.add))
                ch.link(v.tensor_scalar(LOC[:], LOC[:], 1.0, None, ALU.subtract))
                ch.link(v.tensor_scalar(KEEP[:], LOC[:], float(CAP), None, ALU.is_lt))
                ch.link(v.scalar_tensor_tensor(FI[:], FI[:], float(CAP), LOC[:], ALU.mult, ALU.add))
                ch.link(v.tensor_tensor(FT[:], FI[:], KEEP[:], ALU.mult))
                ch.link(v.tensor_copy(FROM[:], FT[:]))
                ch.link(v.tensor_tensor(FI[:], FI[:], TI[:], ALU.subtract))
                ch.link(v.tensor_tensor(FI[:], FI[:], KEEP[:], ALU.mult))
                ch.link(v.tensor_tensor(FI[:], FI[:], TI[:], ALU.add))
                v.tensor_copy(TO[:], FI[:]).then_inc(routed, 1)
                v.wait_ge(exp_ready, 1)
                ch.link(v.reciprocal(SM[:], SM[:]))
                ch.link(v.tensor_tensor(WT[:], SM[:], KEEP[:], ALU.mult))

            @block.gpsimd
            def _(pool):
                pool.wait_ge(routed, 1)
                pool.wait_ge(zeroed, 16)
                for t in range(NT):
                    pool.indirect_dma_start(out=dispatch, out_offset=bass.IndirectOffsetOnAxis(ap=TO[:, t:t + 1], axis=0),
                                            in_=X[:, t, :], in_offset=None).then_inc(sent, 16)
                pool.wait_ge(sent, 16 * NT)


def moe_experts(nc, io, ident, dispatch, answers, tables, W1, W2, first_loads):
    with Stage(nc, "experts") as st:
        XE = st.sb("XE", [HC_, 2, 2, D])
        XET = st.sb("XET", [P, 2, KD, CAP])
        HT = st.sb("HT", [P, 2, NHID, CAP])
        YS = st.sb("YS", [P, 2, KD, CAP])
        YE = st.sb("YE", [HC_, 2, 2, D])
        TP = st.ps("TP", [P, 512])
        HP = st.ps("HP", [P, 4, 512])
        YT = st.ps("YT", [P, 2, 512])
        YP = st.ps("YP", [HC_, 2, D])
        w_loaded = [st.sem(f"w_loaded{i}") for i in range(2)]
        x_loaded = [st.sem(f"x_loaded{i}") for i in range(2)]
        stored = [st.sem(f"stored{i}") for i in range(2)]
        turned = st.sem("turned")
        turned_read = st.sem("turned_read")
        hid_ready = st.sem("hid_ready")
        relu_act = st.sem("relu_act")
        relu_dve = st.sem("relu_dve")
        y_ready = st.sem("y_ready")
        ys_copied = st.sem("ys_copied")
        y_turned = st.sem("y_turned")
        y_copied = st.sem("y_copied")
        with st.block() as block:
            @block.sync
            def _(sp):
                def store(e):
                    sp.wait_ge(y_copied, e + 1)
                    sp.dma_start(answers[e * CAP:(e + 1) * CAP, :].rearrange("(a p) d -> p a d", p=HC_), YE[:, e % 2]).then_inc(stored[e % 2], 16)

                tables.load(sp)
                for e in range(NE):
                    if e >= 2:
                        sp.wait_ge(y_ready, e - 1)
                    sp.dma_start(XE[:, e % 2], dispatch[e * CAP:(e + 1) * CAP, :].rearrange("(a p) d -> p a d", p=HC_)).then_inc(x_loaded[e % 2], 16)
                    if e >= 2:
                        sp.dma_start(W1[:, e % 2], io["L0_ffn_w1"][e].rearrange("(k p) n -> p k n", p=P)).then_inc(w_loaded[e % 2], 16)
                        sp.dma_start(W2[:, e % 2], io["L0_ffn_w2"][e].rearrange("(k p) n -> p k n", p=P)).then_inc(w_loaded[e % 2], 16)
                    if e >= 2:
                        store(e - 2)
                store(NE - 2)
                store(NE - 1)
                for i in range(2):
                    sp.wait_ge(stored[i], 16 * (NE // 2))

            @block.tensor
            def _(pe):
                def turn(e):
                    pe.wait_ge(x_loaded[e % 2], 16 * (e // 2 + 1))
                    if e:
                        pe.wait_ge(turned_read, e)
                    for k in range(KD):
                        for a in range(2):
                            ins = pe.transpose(TP[:, k * CAP + a * HC_:k * CAP + (a + 1) * HC_], XE[:, e % 2, a, k * P:(k + 1) * P],
                                               ident[0:HC_, 0:HC_])
                    ins.then_inc(turned, 1)

                def turn_back(e):
                    pe.wait_ge(ys_copied, e + 1)
                    if e:
                        pe.wait_ge(y_copied, e)
                    for a in range(2):
                        for k in range(KD):
                            ins = pe.transpose(YP[:, a, k * P:(k + 1) * P], YS[:, e % 2, k, a * HC_:(a + 1) * HC_], ident[:, 0:P])
                    ins.then_inc(y_turned, 1)

                turn(0)
                for e in range(NE):
                    if e >= 2:
                        pe.wait_ge(w_loaded[e % 2], 32 * (e // 2))
                    else:
                        first_loads.wait(pe)
                    pe.wait_ge(turned_read, e + 1)
                    for q in range(NHID // 2):
                        n = e * 4 + q
                        if n >= 4:
                            pe.wait_ge(relu_dve if q % 2 else relu_act, (n - 4) // 2 + 1)
                        for a in range(2):
                            c = 2 * q + a
                            for k in range(KD):
                                ins = pe.matmul(HP[:, q, a * CAP:(a + 1) * CAP], W1[:, e % 2, k, c * P:(c + 1) * P], XET[:, e % 2, k, :],
                                                start=(k == 0), stop=(k == KD - 1))
                        ins.then_inc(hid_ready, 1)
                    if e + 1 < NE:
                        turn(e + 1)
                    if e:
                        turn_back(e - 1)
                    pe.wait_ge(relu_act, 2 * (e + 1))
                    pe.wait_ge(relu_dve, 2 * (e + 1))
                    if e >= 2:
                        pe.wait_ge(ys_copied, e - 1)
                    for k in range(KD):
                        for c in range(NHID):
                            ins = pe.matmul(YT[:, e % 2, k * CAP:(k + 1) * CAP], W2[:, e % 2, c, k * P:(k + 1) * P], HT[:, e % 2, c, :],
                                            start=(c == 0), stop=(c == NHID - 1))
                    ins.then_inc(y_ready, 1)
                turn_back(NE - 1)

            def relu_out(e, q):
                return HT[:, e % 2, 2 * q:2 * q + 2, :], HP[:, q, 0:2 * CAP].rearrange("p (a n) -> p a n", a=2)

            @block.scalar
            def _(act):
                tables.scalar_step(act, 0)
                for e in range(NE):
                    for q in (0, 2):
                        act.wait_ge(hid_ready, 4 * e + q + 1)
                        if e >= 2:
                            act.wait_ge(y_ready, e - 1)
                        out, hid = relu_out(e, q)
                        act.activation(out, hid, ACT.Relu).then_inc(relu_act, 1)
                    act.wait_ge(y_ready, e + 1)
                    if e >= 2:
                        act.wait_ge(y_turned, e - 1)
                    act.activation(YS[:, e % 2].rearrange("p k n -> p (k n)"), YT[:, e % 2, 0:KD * CAP], ACT.Copy).then_inc(ys_copied, 1)
                    tables.scalar_step(act, e + 1)

            @block.vector
            def _(v):
                def take(e):
                    v.wait_ge(turned, e + 1)
                    if e >= 2:
                        v.wait_ge(hid_ready, 4 * (e - 1))
                    v.tensor_copy(XET[:, e % 2].rearrange("p k n -> p (k n)"), TP[:, 0:KD * CAP]).then_inc(turned_read, 1)

                def answers_out(e):
                    v.wait_ge(y_turned, e + 1)
                    if e >= 2:
                        v.wait_ge(stored[e % 2], 16 * (e // 2))
                    v.tensor_copy(YE[:, e % 2], YP[:]).then_inc(y_copied, 1)

                tables.exponents(v)
                take(0)
                for e in range(NE):
                    for q in (1, 3):
                        v.wait_ge(hid_ready, 4 * e + q + 1)
                        if e >= 2:
                            v.wait_ge(y_ready, e - 1)
                        out, hid = relu_out(e, q)
                        v.tensor_scalar(out, hid, 0.0, None, ALU.max).then_inc(relu_dve, 1)
                    if e + 1 < NE:
                        take(e + 1)
                    if e:
                        answers_out(e - 1)
                    if 4 <= e < 7:
                        tables.factor_step(v, e - 4)
                answers_out(NE - 1)

            @block.gpsimd
            def _(pool):
                tables.gpsimd_program(pool)


LH, LD = 16, 16
LPAD = 32
LC = LH * LPAD // P
LHC = LH // LC
PHI_EPS = 1e-3


def phi_out(v, out, product):
    return v.tensor_scalar(out, product, 0.0, PHI_EPS, ALU.max, ALU.add)


def mlp(nc, name, XT, W1, B1, HT, func, loads, base, B2, ahead):
    with Stage(nc, name) as st:
        ring = st.ps("ring", [P, 8, G4])
        ready = st.sem("ready")
        read = st.sem("read")
        steps = [(g, c) for g in range(T // G4) for c in range(NHID)]
        with st.block() as block:
            @block.tensor
            def _(pe):
                loads.wait(pe)
                for n, (g, c) in enumerate(steps):
                    if n >= 8:
                        pe.wait_ge(read, n - 7)
                    for k in range(KD):
                        ins = pe.matmul(ring[:, n % 8, :], W1[:, k, c * P:(c + 1) * P], XT[:, k, g * G4:(g + 1) * G4],
                                        start=(k == 0), stop=(k == KD - 1))
                    ins.then_inc(ready, 1)

            @block.sync
            def _(sp):
                ahead.issue(sp)

            @block.gpsimd
            def _(pool):
                loads.wait(pool)
                add_row(pool, base, B2)

            @block.scalar
            def _(act):
                loads.wait(act)
                for n, (g, c) in enumerate(steps):
                    act.wait_ge(ready, n + 1)
                    act.activation(HT[:, c, g * G4:(g + 1) * G4], ring[:, n % 8, :], func, bias=B1[:, 0, c:c + 1]).then_inc(read, 1)


def mlp_product(HT, W2):
    def product(pe, t, out):
        for c in range(NHID):
            ins = pe.matmul(out, HT[:, c, t * P:(t + 1) * P], W2[:, c, :], start=(c == 0), stop=(c == NHID - 1))
        return ins
    return product


def stage_performer(nc, io, X, XT, ident, KF, inputs):
    with Stage(nc, "pf") as st:
        LN = st.sb("LN", [P, 4, KD])
        WO = st.sb("WO", [P, KD, D])
        X1 = st.sb("X1", [P, NT, D])
        W2 = st.sb("W2", [P, NHID, D])
        B2 = st.sb("B2", [P, D])
        W1 = st.sb("W1", [P, KD, HID])
        B1 = st.sb("B1", [P, 1, NHID])
        mlp_loads = Loads(nc, "pfmlp", [(W1[:], io["L1_attn_w1"].rearrange("(k p) n -> p k n", p=P)), (B1[:], io["L1_attn_b1"]),
                                        (W2[:], io["L1_attn_w2"].rearrange("(k p) n -> p k n", p=P)), (B2[:], io["L1_attn_b2"])])
        with Stage(nc, "pg") as s1:
            QT = s1.sb("QT", [P, LC, T])
            KT = s1.sb("KT", [P, LC, T])
            VA = s1.sb("VA", [P, NT, LH, 2 * LD])
            WQ = s1.sb("WQ", [P, KD, LC * P])
            WK = s1.sb("WK", [P, KD, LC * P])
            WV = s1.sb("WV", [P, KD, D])
            MASK = s1.sb("MASK", [P, 2, P])
            loads = Loads(nc, "pfproj", [(WQ[:], io["L1_attn_wq"].rearrange("(k p) n -> p k n", p=P)),
                     (WK[:], io["L1_attn_wk"].rearrange("(k p) n -> p k n", p=P)),
                     (WV[:], io["L1_attn_wv"].rearrange("(k p) n -> p k n", p=P)),
                     (WO[:], io["L1_attn_wo"].rearrange("(k p) n -> p k n", p=P)),
                     (MASK[:], io["tri"])])
            norm_only(nc, "pfln1", X, X1, XT, ident, eps=EPS6, scale=LN[:, 0, :], bias=LN[:, 1, :],
                      loads=Loads(nc, "pfln1", [(LN[:], io["L1_attn_ln"])]), ahead=[loads])
            with s1.block() as block:
                @block.gpsimd
                def _(pool):
                    pool.memset(VA[:].rearrange("p t h d -> p (t h) d")[:, :, LD:2 * LD], 1.0)
            jobs = []
            for g in range(T // G4):
                tok = slice(g * G4, (g + 1) * G4)
                for W, OUT in ((WQ, QT), (WK, KT)):
                    for c in range(LC):
                        jobs.append((OUT[:, c, tok], [(W[:, k, c * P:(c + 1) * P], XT[:, k, tok]) for k in range(KD)], phi_out))

            def value_out(v, out, product):
                return v.tensor_copy(out, product.rearrange("p (h d) -> p h d", h=LH))

            for t in range(NT):
                jobs.append((VA[:, t, :, 0:LD], [(XT[:, k, t * P:(t + 1) * P], WV[:, k, :]) for k in range(KD)], value_out))
            products(nc, "pfproj", jobs, loads, dve_only=True, ahead=[mlp_loads])
            performer_core(nc, ident, QT, KT, VA, MASK, X1)
            turn_tiles(nc, "pfturn", X1, XT, ident)

        def out_product(pe, t, out):
            for k in range(KD):
                ins = pe.matmul(out, XT[:, k, t * P:(t + 1) * P], WO[:, k, :], start=(k == 0), stop=(k == KD - 1))
            return ins

        with Stage(nc, "ph") as s1:
            HT = s1.sb("HT", [P, NHID, T])
            with Stage(nc, "pi") as s2:
                YT = s2.sb("YT", [P, KD, T])
                finish_norm(nc, "pfln2", X, YT, ident, out_product, total=lambda t: X1[:, t, :], also=lambda t: X[:, t, :],
                            out=lambda t: X1[:, t, :], eps=EPS6, scale=LN[:, 2, :], bias=LN[:, 3, :])
                next_inputs = topk_inputs(nc, io)
                mlp(nc, "pfmlp", YT, W1, B1, HT, ACT.Gelu_apprx_tanh, mlp_loads, X, B2, next_inputs.loads)
            finish_norm(nc, "pfnorm", X, XT, ident, mlp_product(HT, W2))
    return next_inputs


def turn_tiles(nc, name, Y, YT, ident):
    with Stage(nc, name) as st:
        TP = st.ps("TP", [P, 4, 512])
        turned = st.sem("turned")
        read = st.sem("read")
        with st.block() as block:
            @block.tensor
            def _(pe):
                for t in range(NT):
                    if t >= 4:
                        pe.wait_ge(read, t - 3)
                    for k in range(KD):
                        ins = pe.transpose(TP[:, t % 4, k * P:(k + 1) * P], Y[:, t, k * P:(k + 1) * P], ident[:, 0:P])
                    ins.then_inc(turned, 1)

            @block.scalar
            def _(act):
                for t in range(NT):
                    act.wait_ge(turned, t + 1)
                    act.activation(YT[:, :, t * P:(t + 1) * P], TP[:, t % 4, 0:D].rearrange("p (k n) -> p k n", k=KD), ACT.Copy).then_inc(read, 1)


def performer_core(nc, ident, QT, KT, VA, MASK, AO):
    NU = B * LC
    with Stage(nc, "pfcore") as st:
        A = st.sb("A", [P, 2, LHC, 3, P])
        OS = st.sb("OS", [P, 2, S])
        RD = st.sb("RD", [P, 2, LHC])
        SC = st.ps("SC", [P, LHC, 512])
        OP = st.ps("OP", [P, 2, 512])
        TP = st.ps("TP", [P, 2, 512])
        scores_ready = st.sem("scores_ready")
        masked = st.sem("masked")
        out_ready = st.sem("out_ready")
        out_copied = st.sem("out_copied")
        turned = st.sem("turned")
        normed = st.sem("normed")
        dve_chain = st.sem("dve_chain")
        with st.block() as block:
            @block.tensor
            def _(pe):
                def turn(m):
                    pe.wait_ge(out_copied, m + 1)
                    if m >= 2:
                        pe.wait_ge(normed, m - 1)
                    for a in range(2):
                        ins = pe.transpose(TP[:, m % 2, a * P:(a + 1) * P], OS[:, m % 2, a * P:(a + 1) * P], ident[:, 0:P])
                    ins.then_inc(turned, 1)

                def outs(m):
                    b, c = m // LC, m % LC
                    pe.wait_ge(masked, m + 1)
                    if m >= 2:
                        pe.wait_ge(out_copied, m - 1)
                    for h in range(LHC):
                        hd = c * LHC + h
                        r = slice(h * LPAD, (h + 1) * LPAD)
                        pe.matmul(OP[r, m % 2, 0:S], VA[:, 2 * b, hd, :], A[:, m % 2, h, 0:2, :], start=True, stop=False)
                        ins = pe.matmul(OP[r, m % 2, P:S], VA[:, 2 * b + 1, hd, :], A[:, m % 2, h, 2, :], start=False, stop=True)
                    ins.then_inc(out_ready, 1)

                for m in range(NU):
                    b, c = m // LC, m % LC
                    if m:
                        pe.wait_ge(masked, m)
                    for h in range(LHC):
                        r = slice(h * LPAD, h * LPAD + LD)
                        pe.matmul(SC[:, h, 0:S], KT[r, c, b * S:b * S + P], QT[r, c, b * S:(b + 1) * S], start=True, stop=True,
                                  tile_position=(h * LPAD, 0))
                        ins = pe.matmul(SC[:, h, S:S + P], KT[r, c, b * S + P:(b + 1) * S], QT[r, c, b * S + P:(b + 1) * S], start=True, stop=True,
                                        tile_position=(h * LPAD, 0))
                    ins.then_inc(scores_ready, 1)
                    if m >= 1:
                        outs(m - 1)
                    if m >= 2:
                        turn(m - 2)
                outs(NU - 1)
                turn(NU - 2)
                turn(NU - 1)

            @block.scalar
            def _(act):
                for m in range(NU):
                    act.wait_ge(out_ready, m + 1)
                    if m >= 2:
                        act.wait_ge(turned, m - 1)
                    act.activation(OS[:, m % 2, :], OP[:, m % 2, 0:S], ACT.Copy).then_inc(out_copied, 1)

            @block.vector
            def _(v):
                ch = Chain(v, dve_chain)

                def norm(m):
                    b, c = m // LC, m % LC
                    v.wait_ge(turned, m + 1)
                    tp = TP[:, m % 2, 0:S].rearrange("p (a h d) -> p a h d", a=2, h=LHC)
                    ch.link(v.reciprocal(RD[:], tp[:, :, :, LD]))
                    for a in range(2):
                        ch.link(v.tensor_tensor(AO[:, 2 * b + a, c * LHC * LD:(c + 1) * LHC * LD].rearrange("p (h d) -> p h d", h=LHC),
                                                tp[:, a, :, 0:LD], RD[:, a, :].rearrange("p (h o) -> p h o", o=1).to_broadcast([P, LHC, LD]),
                                                ALU.mult))
                    v.sem_inc(normed, 1)

                for m in range(NU):
                    v.wait_ge(scores_ready, m + 1)
                    if m >= 2:
                        v.wait_ge(out_ready, m - 1)
                    sc = SC[:, :, 0:3 * P].rearrange("p h (a q) -> p h a q", a=3)
                    a = A[:, m % 2]
                    tri = MASK[:, 0:1, :].to_broadcast([P, LHC, P])
                    v.tensor_tensor(a[:, :, 0, :], sc[:, :, 0, :], tri, ALU.mult)
                    v.tensor_tensor(a[:, :, 2, :], sc[:, :, 2, :], tri, ALU.mult)
                    v.tensor_copy(a[:, :, 1, :], sc[:, :, 1, :]).then_inc(masked, 1)
                    if m >= 3:
                        norm(m - 3)
                for m in range(NU - 3, NU):
                    norm(m)


XH, XD = 4, 32
TOPK = 32
MASKED, TAKEN = -3e38, -3.4e38


def stage_s4d(nc, io, X, XT, ident, KF, inputs):
    with Stage(nc, "s4") as st:
        Z = st.sb("Z", [P, NT, D])
        FO = st.sb("FO", [P, NT, 2 * D])
        DFT = st.sb("DFT", [P, 2, NF, P])
        INV = st.sb("INV", [P, NF, 2, P])
        SK = st.sb("SK", [P, D])
        conv_loads = Loads(nc, "cv", [(DFT[:], io["dft"]), (INV[:], io["dft_inverse"]), (SK[:], io["L1_xattn_D_skip"])])
        with Stage(nc, "s5") as s1:
            CTT = s1.sb("CTT", [P, KD, T])
            topk_attention(nc, io, X, XT, ident, CTT, Z, FO, conv_loads, inputs)
        s4d_convolve(nc, DFT, INV, SK, KF, X, Z, FO, conv_loads)
        with Stage(nc, "s6") as s1:
            HT = s1.sb("HT", [P, NHID, T])
            W1 = s1.sb("W1", [P, KD, HID])
            B1 = s1.sb("B1", [P, 1, NHID])
            W2 = s1.sb("W2", [P, NHID, D])
            B2 = s1.sb("B2", [P, D])
            LN = s1.sb("LN", [P, 2, KD])
            GB = s1.sb("GB", [P, 2, D])
            mlp_loads = Loads(nc, "s4mlp", [(W1[:], io["L1_xattn_W1"].rearrange("(k p) n -> p k n", p=P)), (B1[:], io["L1_xattn_b1"]),
                                            (W2[:], io["L1_xattn_W2"].rearrange("(k p) n -> p k n", p=P)), (B2[:], io["L1_xattn_b2"]),
                                            (GB[:], io["L1_xattn_norm_out"])])
            norm_only(nc, "s4ln2", Z, FO[:, :, 0:D], XT, ident, scale=LN[:, 0, :], bias=LN[:, 1, :],
                      loads=Loads(nc, "s4ln2", [(LN[:], io["L1_xattn_ffn_ln"])]), ahead=[mlp_loads])
            next_inputs = sides_inputs(nc, io)
            mlp(nc, "s4mlp", XT, W1, B1, HT, ACT.Gelu, mlp_loads, Z, B2, next_inputs.loads)
            finish_norm(nc, "s4ln3", X, None, ident, mlp_product(HT, W2), total=lambda t: Z[:, t, :],
                        base=lambda t: Z[:, t, :], out=lambda t: Z[:, t, :], affine=GB, needs=[mlp_loads])
        norm_only(nc, "s4norm", X, X, XT, ident, base=Z)
    return next_inputs


def topk_inputs(nc, io):
    x = Inputs(nc, "topk")
    x.CT = x.sb("CT", [P, 2, T])
    x.WQ = x.sb("WQ", [P, KD, P])
    x.WK = x.sb("WK", [P, 2, P])
    x.WV = x.sb("WV", [P, 2, D])
    x.M8 = x.sb("M8", [P, 2, T], U8)
    x.pairs = load_context(io, x.CT) + load_split(x.WK, io["L1_xattn_Wk"]) + load_split(x.WV, io["L1_xattn_Wv"]) + [
        (x.WQ[:], io["L1_xattn_Wq"].rearrange("(k p) n -> p k n", p=P)), (x.M8[:, 0, :], io["text_mask"]), (x.M8[:, 1, :], io["vision_mask"])]
    return x.ready()


def topk_attention(nc, io, X, XT, ident, CTT, Z, FO, conv_loads, inputs):
    with Stage(nc, "tk") as st:
        QT = st.sb("QT", [P, T])
        KT = st.sb("KT", [P, T])
        V = st.sb("V", [P, NT, D])
        MB = st.sb("MB", [P, T])
        TM = st.sb("TM", [P, T])
        WI = st.sb("WI", [P, 2, KD, 2 * D])
        BI = st.sb("BI", [1, 2, 2 * D])
        GB = st.sb("GB", [P, 2, D])
        GATE = st.sb("GATE", [P, 1])
        film_pairs = [(GB[:], io["L1_xattn_norm_in"]), (GATE[:], io["L1_xattn_gate"])]
        for n, name in enumerate(("in", "out")):
            film_pairs += [(WI[:, n], io["L1_xattn_W_film_" + name].rearrange("(k p) n -> p k n", p=P)),
                           (BI[:, n, :], io["L1_xattn_b_film_" + name])]
        film_loads = Loads(nc, "film", film_pairs)
        CT, WQ, WK, WV, M8 = inputs.CT, inputs.WQ, inputs.WK, inputs.WV, inputs.M8
        with Stage(nc, "tl") as s2:
            jobs = []
            for g in range(T // G4):
                tok = slice(g * G4, (g + 1) * G4)
                jobs.append((QT[:, tok], [(WQ[:, k, :], XT[:, k, tok]) for k in range(KD)], copy_out))
                jobs.append((KT[:, tok], [(WK[0:KC[k], k, :], CT[0:KC[k], k, tok]) for k in range(2)], copy_out))
            for t in range(NT):
                jobs.append((V[:, t, :], [(CT[0:KC[k], k, t * P:(t + 1) * P], WV[0:KC[k], k, :]) for k in range(2)], copy_out))
            products(nc, "tkproj", jobs, inputs.loads, ahead=[film_loads], beside=NormBeside(nc, s2, X, Z, ident))
            with s2.block() as block:
                @block.vector
                def _(v):
                    v.tensor_scalar(TM[:], M8[:, 0, :], 1.0 / XH, None, ALU.mult)
                    v.tensor_scalar(MB[:], M8[:, 1, :], -MASKED, MASKED, ALU.mult, ALU.add)
        inputs.free()

        SS = st.sb("SS", [P, 2, XH, S])
        WW = st.sb("WW", [P, XH, S])
        EX = st.sb("EX", [P, XH, S])
        PP = st.sb("PP", [P, 2, XH, S])
        DG = st.sb("DG", [P, XH, P])
        AT = st.sb("AT", [P, 2, 2, P])
        MX = st.sb("MX", [P, XH, TOPK])
        NM = st.sb("NM", [P, 2, XH])
        SM = st.sb("SM", [P, 2, XH])
        SC = st.ps("SC", [P, XH, 512])
        TP = st.ps("TP", [P, 2, 2, D])
        FP = st.ps("FP", [P, 2, 2 * D])
        FI = st.sb("FI", [P, 2, 2 * D])
        film_ready = st.sem("film_ready")
        film_read = st.sem("film_read")
        updated = st.sem("updated")
        pool_chain = st.sem("pool_chain")
        scores_ready = st.sem("scores_ready")
        scores_read = st.sem("scores_read")
        masked = st.sem("masked")
        max_ready = st.sem("max_ready")
        exp_ready = st.sem("exp_ready")
        sums_ready = st.sem("sums_ready")
        scale_ready = st.sem("scale_ready")
        turned = st.sem("turned")
        turned_read = st.sem("turned_read")
        pooled = st.sem("pooled")
        pooled_read = st.sem("pooled_read")
        dve_chain = st.sem("dve_chain")
        with st.block() as block:
            @block.tensor
            def _(pe):
                def scores(n):
                    if n:
                        pe.wait_ge(scores_read, n)
                    b = n // 2
                    for h in range(XH):
                        r = slice(h * XD, (h + 1) * XD)
                        ins = pe.matmul(SC[:, h, 0:S], QT[r, n * P:(n + 1) * P], KT[r, b * S:(b + 1) * S], start=True, stop=True,
                                        tile_position=(h * XD, 0))
                    ins.then_inc(scores_ready, 1)

                def turn(n):
                    pe.wait_ge(scale_ready, n + 1)
                    if n >= 2:
                        pe.wait_ge(pooled_read, n - 1)
                    for k in range(2):
                        for h in range(XH):
                            ins = pe.matmul(TP[:, n % 2, 0, k * P:(k + 1) * P], PP[:, n % 2, h, k * P:(k + 1) * P], DG[:, h, :],
                                            start=(h == 0), stop=(h == XH - 1))
                    ins.then_inc(turned, 1)

                def pool_context(n):
                    pe.wait_ge(turned_read, n + 1)
                    for c in range(KD):
                        for k in range(2):
                            ins = pe.matmul(TP[:, n % 2, 1, c * P:(c + 1) * P], V[:, (n // 2) * 2 + k, c * P:(c + 1) * P], AT[:, n % 2, k, :],
                                            start=(k == 0), stop=(k == 1))
                    ins.then_inc(pooled, 1)

                def film(n):
                    pe.wait_ge(pooled_read, n + 1)
                    if n:
                        pe.wait_ge(film_read, n)
                    for i in range(2):
                        for k in range(KD):
                            pe.matmul(FP[:, i, :], CTT[:, k, n * P:(n + 1) * P], WI[:, i, k, :], start=(k == 0), stop=False)
                        ins = add_bias(pe, ident, FP[:, i, :], BI[:, i, :])
                    ins.then_inc(film_ready, 1)

                scores(0)
                scores(1)
                film_loads.wait(pe)
                for n in range(NT):
                    if n + 2 < NT:
                        scores(n + 2)
                    turn(n)
                    pool_context(n)
                    if n:
                        film(n - 1)
                film(NT - 1)

            @block.sync
            def _(sp):
                conv_loads.issue(sp)

            @block.gpsimd
            def _(pool):
                ch = Chain(pool, pool_chain)
                film_loads.wait(pool)
                LATE = 3

                def mask(n):
                    pool.wait_ge(scores_read, n + 1)
                    b = n // 2
                    pool.tensor_tensor(SS[:, n % 2], SS[:, n % 2], MB[:, b * S:(b + 1) * S].rearrange("p (o q) -> p o q", o=1).to_broadcast([P, XH, S]),
                                       ALU.add).then_inc(masked, 1)

                def film(n):
                    ch.link(pool.tensor_tensor(Z[:, n, :], Z[:, n, :], GB[:, 0, :], ALU.mult))
                    ch.link(pool.tensor_tensor(Z[:, n, :], Z[:, n, :], GB[:, 1, :], ALU.add))
                    pool.wait_ge(film_read, n + 1)
                    ch.link(pool.tensor_tensor(Z[:, n, :], Z[:, n, :], FI[:, n % 2, 0:D], ALU.mult))
                    pool.tensor_tensor(Z[:, n, :], Z[:, n, :], FI[:, n % 2, D:2 * D], ALU.add).then_inc(updated, 1)

                for n in range(NT + LATE):
                    if n < NT:
                        mask(n)
                    if n >= LATE:
                        film(n - LATE)

            @block.scalar
            def _(act):
                def film(n):
                    act.wait_ge(film_ready, n + 1)
                    if n >= 2:
                        act.wait_ge(updated, n - 1)
                    act.activation(FI[:, n % 2, 0:D], FP[:, 0, 0:D], ACT.Identity, scale=GATE[:], bias=ident[:, ONES:ONES + 1])
                    act.activation(FI[:, n % 2, D:2 * D], FP[:, 0, D:2 * D], ACT.Copy, scale=GATE[:])
                    act.activation(FO[:, n, :], FP[:, 1, :], ACT.Copy, scale=GATE[:]).then_inc(film_read, 1)

                def scale(n):
                    act.wait_ge(scores_ready, n + 1)
                    if n >= 2:
                        act.wait_ge(sums_ready, n - 1)
                        act.wait_ge(exp_ready, n - 1)
                    act.activation(SS[:, n % 2], SC[:, :, 0:S], ACT.Copy, scale=float(XD) ** -0.5).then_inc(scores_read, 1)

                film_loads.wait(act)
                scale(0)
                for n in range(NT):
                    act.wait_ge(max_ready, n + 1)
                    for h in range(XH):
                        ins = act.activation(EX[:, h, :], SS[:, n % 2, h, :], ACT.Exp, bias=NM[:, n % 2, h:h + 1])
                    ins.then_inc(exp_ready, 1)
                    if n + 1 < NT:
                        scale(n + 1)
                    if n >= 2:
                        film(n - 2)
                    act.wait_ge(sums_ready, n + 1)
                    for h in range(XH):
                        ins = act.activation(DG[:, h, :], ident[:, 0:P], ACT.Copy, scale=SM[:, n % 2, h:h + 1])
                    ins.then_inc(scale_ready, 1)
                    act.wait_ge(turned, n + 1)
                    act.activation(AT[:, n % 2], TP[:, n % 2, 0, :].rearrange("p (k q) -> p k q", k=2), ACT.Copy).then_inc(turned_read, 1)
                film(NT - 2)
                film(NT - 1)

            @block.vector
            def _(v):
                ch = Chain(v, dve_chain)

                def pooled_out(n):
                    v.wait_ge(pooled, n + 1)
                    tok = slice(n * P, (n + 1) * P)
                    v.tensor_tensor(CTT[:, :, tok], TP[:, n % 2, 1, :].rearrange("p (c q) -> p c q", c=KD),
                                    TM[:, tok].rearrange("p (o q) -> p o q", o=1).to_broadcast([P, KD, P]), ALU.mult).then_inc(pooled_read, 1)

                for n in range(NT):
                    v.wait_ge(masked, n + 1)
                    ss = SS[:, n % 2]
                    PAIRS = ((0, 1), (2, 3))
                    struck = [0, 0]
                    for r in range(TOPK // 8):
                        src = ss if r == 0 else WW[:]
                        found = [0, 0]
                        for i, pair in enumerate(PAIRS):
                            if r:
                                ch.need(struck[i])
                            for h in pair:
                                ins = v.max(MX[:, h, 8 * r:8 * r + 8], src[:, h, :])
                            found[i] = ch.mark(ins)
                        for i, pair in enumerate(PAIRS):
                            ch.need(found[i])
                            for h in pair:
                                ins = v.match_replace(WW[:, h, :], MX[:, h, 8 * r:8 * r + 8], src[:, h, :], TAKEN)
                            struck[i] = ch.mark(ins)
                        if r == 0:
                            v.tensor_scalar(NM[:, n % 2, :], MX[:, :, 0], -1.0, None, ALU.mult).then_inc(max_ready, 1)
                    if n:
                        pooled_out(n - 1)
                    ch.need(struck[1])
                    v.wait_ge(exp_ready, n + 1)
                    if n >= 2:
                        v.wait_ge(turned, n - 1)
                    for h in range(XH):
                        ins = v.scalar_tensor_tensor(PP[:, n % 2, h, :], WW[:, h, :], 0.5 * (TAKEN + MASKED), EX[:, h, :], ALU.is_le, ALU.mult,
                                                     accum_out=SM[:, n % 2, h:h + 1])
                    ch.link(ins)
                    v.reciprocal(SM[:, n % 2, :], SM[:, n % 2, :]).then_inc(sums_ready, 1)
                pooled_out(NT - 1)


def s4d_convolve(nc, DFT, INV, SK, KF, X, Z, FO, loads):
    NP = B // 2
    with Stage(nc, "cv") as st:
        MM = st.sb("MM", [P, 4, 2, D])
        YF = st.sb("YF", [P, 2, NF, 2, D])
        XD = st.sb("XD", [P, 4, D])
        XF = st.ps("XF", [P, NF, 2, D])
        YP = st.ps("YP", [P, 2, 2, D])
        xf_ready = st.sem("xf_ready")
        xf_read = st.sem("xf_read")
        prod_ready = st.sem("prod_ready")
        prod_used = st.sem("prod_used")
        skip_ready = st.sem("skip_ready")
        y_ready = st.sem("y_ready")
        y_read = st.sem("y_read")
        done = st.sem("done")
        dve_chain = st.sem("dve_chain")
        pool_chain = st.sem("pool_chain")
        with st.block() as block:
            def tiles(buf, pr):
                return buf[:, 4 * pr:4 * pr + 4, :].rearrange("p (b h) d -> p b h d", h=2)

            @block.tensor
            def _(pe):
                loads.wait(pe)
                def forward(pr):
                    for ft in range(2):
                        for q in (2 * ft, 2 * ft + 1):
                            if pr:
                                pe.wait_ge(xf_read, 2 * (pr - 1) + ft + 1)
                            for h in range(2):
                                ins = pe.matmul(XF[:, q], DFT[:, h, q, :], tiles(Z, pr)[:, :, h, :], start=(h == 0), stop=(h == 1))
                        ins.then_inc(xf_ready, 1)

                forward(0)
                for pr in range(NP):
                    if pr + 1 < NP:
                        forward(pr + 1)
                    pe.wait_ge(prod_used, 2 * (pr + 1))
                    for h in range(2):
                        if pr:
                            pe.wait_ge(y_read, 2 * (pr - 1) + h + 1)
                        for q in range(NF):
                            ins = pe.matmul(YP[:, h], INV[:, q, h, :], YF[:, pr % 2, q], start=(q == 0), stop=(q == NF - 1))
                        ins.then_inc(y_ready, 1)

            @block.gpsimd
            def _(pool):
                ch = Chain(pool, pool_chain)
                loads.wait(pool)
                for pr in range(NP):
                    if pr >= 2:
                        pool.wait_ge(y_ready, 2 * (pr - 1))
                    for ft in range(2):
                        pool.wait_ge(prod_ready, 2 * pr + ft + 1)
                        ch.link(pool.tensor_tensor(YF[:, pr % 2, 2 * ft], MM[:, 0], MM[:, 1], ALU.subtract))
                        pool.tensor_tensor(YF[:, pr % 2, 2 * ft + 1], MM[:, 2], MM[:, 3], ALU.add).then_inc(prod_used, 1)
                    if pr:
                        pool.wait_ge(y_read, 2 * pr)
                    pool.tensor_tensor(XD[:], Z[:, 4 * pr:4 * pr + 4, :], SK[:].rearrange("p (o d) -> p o d", o=1).to_broadcast([P, 4, D]),
                                       ALU.mult).then_inc(skip_ready, 1)

            @block.vector
            def _(v):
                ch = Chain(v, dve_chain)
                def multiply(pr):
                    for ft in range(2):
                        n = 2 * pr + ft
                        v.wait_ge(xf_ready, n + 1)
                        if n:
                            v.wait_ge(prod_used, n)
                        for i, (x, k) in enumerate(((0, 0), (1, 1), (0, 1), (1, 0))):
                            ins = v.tensor_tensor(MM[:, i], XF[:, 2 * ft + x],
                                                  KF[:, 2 * ft + k:2 * ft + k + 1, :].to_broadcast([P, 2, D]), ALU.mult)
                            ch.link(ins)
                        v.sem_inc(prod_ready, 1)
                        v.sem_inc(xf_read, 1)

                multiply(0)
                for pr in range(NP):
                    if pr + 1 < NP:
                        multiply(pr + 1)
                    v.wait_ge(skip_ready, pr + 1)
                    for h in range(2):
                        v.wait_ge(y_ready, 2 * pr + h + 1)
                        z = tiles(Z, pr)[:, :, h, :]
                        fo = tiles(FO, pr)[:, :, h, :]
                        xd = XD[:].rearrange("p (b h) d -> p b h d", h=2)[:, :, h, :]
                        ch.link(v.tensor_tensor(z, YP[:, h], xd, ALU.add))
                        v.sem_inc(y_read, 1)
                        ch.link(v.scalar_tensor_tensor(z, fo[:, :, 0:D], 1.0, z, ALU.add, ALU.mult))
                        ch.link(v.tensor_tensor(z, z, fo[:, :, D:2 * D], ALU.add))
                        ch.link(v.tensor_tensor(z, z, tiles(X, pr)[:, :, h, :], ALU.add))


PH, PK, NK = 8, 8, 64
NC_ = 2 * PH
HK = PH * PK
J2 = NK // 2
BLK = 256
UNIT = 32
PSCALE = 2.0 ** 14
F16 = mybir.dt.float16


def stage_peer(nc, io, X, XT, ident, KF, inputs):
    with Stage(nc, "pe") as st:
        DOWN = st.sb("DOWN", [P, KD, J2, P])
        UP = st.sb("UP", [P, J2, D])
        expert_loads = Loads(nc, "ex", [(DOWN[:], io["L1_ffn_down"]), (UP[:], io["L1_ffn_up"])])
        SV = st.sb("SV", [P, NT, NC_, PK])
        IV = st.sb("IV", [P, NT, NC_, PK], F16)
        peer_sides(nc, XT, ident, SV, IV, expert_loads, inputs)
        inputs.free()
        peer_experts(nc, io, X, XT, ident, SV, IV, DOWN, UP, expert_loads)


def sides_inputs(nc, io):
    x = Inputs(nc, "sides")
    x.WQ = x.sb("WQ", [P, KD, NC_ * P])
    x.KEYS = x.sb("KEYS", [P, NC_, NK])
    x.BN = x.sb("BN", [P, 2, NC_])
    x.pairs = [(x.WQ[:], io["L1_ffn_w_q"].rearrange("(k p) n -> p k n", p=P)), (x.KEYS[:], io["L1_ffn_keysT"]), (x.BN[:], io["L1_ffn_bn"])]
    return x.ready()


def peer_sides(nc, XT, ident, SV, IV, expert_loads, inputs):
    with Stage(nc, "sides") as st:
        WQ, KEYS, BN = inputs.WQ, inputs.KEYS, inputs.BN
        QN = st.sb("QN", [P, 2, T])
        I32_ = st.sb("I32", [P, 2, NT, PK], U32)
        RAW = st.sb("RAW", [P, 4, 6])
        MV = st.sb("MV", [P, NC_, 2])
        SD = st.sb("SD", [P, NC_])
        SB_ = st.sb("SB_", [P, NC_, 2])
        QP = st.ps("QP", [P, 4, G4])
        SP_ = st.ps("SP_", [P, 2, NT, NK])
        q_ready = st.sem("q_ready")
        var_ready = st.sem("var_ready")
        std_ready = st.sem("std_ready")
        affine_ready = st.sem("affine_ready")
        q_normed = st.sem("q_normed")
        sims_ready = st.sem("sims_ready")
        sims_read = st.sem("sims_read")
        index_kept = st.sem("index_kept")
        dve_chain = st.sem("dve_chain")
        with st.block() as block:
            @block.sync
            def _(sp):
                expert_loads.issue(sp)

            @block.tensor
            def _(pe):
                def query(c):
                    for g in range(4):
                        if c:
                            pe.wait_ge(q_normed, 4 * (c - 1) + g + 1)
                        for k in range(KD):
                            ins = pe.matmul(QP[:, g, :], WQ[:, k, c * P:(c + 1) * P], XT[:, k, g * G4:(g + 1) * G4],
                                            start=(k == 0), stop=(k == KD - 1))
                        ins.then_inc(q_ready, 1)

                inputs.loads.wait(pe)
                query(0)
                for c in range(NC_):
                    if c + 1 < NC_:
                        query(c + 1)
                    pe.wait_ge(q_normed, 4 * (c + 1))
                    if c >= 2:
                        pe.wait_ge(sims_read, c - 1)
                    for t in range(NT):
                        ins = pe.matmul(SP_[:, c % 2, t, :], QN[:, c % 2, t * P:(t + 1) * P], KEYS[:, c, :], start=True, stop=True)
                    ins.then_inc(sims_ready, 1)

            @block.scalar
            def _(act):
                for c in range(NC_):
                    act.wait_ge(var_ready, c + 1)
                    act.activation(SD[:, c:c + 1], MV[:, c, 1:2], ACT.Sqrt, bias=ident[:, EPS5:EPS5 + 1]).then_inc(std_ready, 1)
                    act.wait_ge(affine_ready, c + 1)
                    if c >= 2:
                        act.wait_ge(sims_ready, c - 1)
                    for g in range(4):
                        act.activation(QN[:, c % 2, g * G4:(g + 1) * G4], QP[:, g, :], ACT.Identity, scale=SB_[:, c, 0:1],
                                       bias=SB_[:, c, 1:2]).then_inc(q_normed, 1)

            @block.vector
            def _(v):
                ch = Chain(v, dve_chain)

                def norm(c):
                    for g in range(4):
                        v.wait_ge(q_ready, 4 * c + g + 1)
                        ins = v.bn_stats(RAW[:, g, :], QP[:, g, :])
                    ch.link(ins)
                    v.bn_aggr(MV[:, c, :], RAW[:].rearrange("p g s -> p (g s)")).then_inc(var_ready, 1)
                    v.wait_ge(std_ready, c + 1)
                    ch.link(v.reciprocal(SD[:, c:c + 1], SD[:, c:c + 1]))
                    ch.link(v.tensor_tensor(SB_[:, c, 0:1], SD[:, c:c + 1], BN[:, 0, c:c + 1], ALU.mult))
                    ch.link(v.tensor_tensor(SB_[:, c, 1:2], SB_[:, c, 0:1], MV[:, c, 0:1], ALU.mult))
                    v.tensor_tensor(SB_[:, c, 1:2], BN[:, 1, c:c + 1], SB_[:, c, 1:2], ALU.subtract).then_inc(affine_ready, 1)

                inputs.loads.wait(v)
                norm(0)
                for c in range(NC_):
                    if c + 1 < NC_:
                        norm(c + 1)
                    v.wait_ge(sims_ready, c + 1)
                    if c >= 2:
                        v.wait_ge(index_kept, c - 1)
                    for t in range(NT):
                        ins = v.max(SV[:, t, c, :], SP_[:, c % 2, t, :])
                    ch.link(ins)
                    for t in range(NT):
                        ins = v.max_index(I32_[:, c % 2, t, :], SV[:, t, c, :], SP_[:, c % 2, t, :])
                    ins.then_inc(sims_read, 1)

            @block.gpsimd
            def _(pool):
                for c in range(NC_):
                    pool.wait_ge(sims_read, c + 1)
                    pool.tensor_copy(IV[:, :, c, :], I32_[:, c % 2]).then_inc(index_kept, 1)


def peer_experts(nc, io, X, XT, ident, SV, IV, DOWN, UP, expert_loads):
    NB = T // BLK
    UB = BLK // UNIT
    NU = NB * UB
    NP = J2 // 2
    PU = NP // UB
    TB = BLK // P
    N = TB * PH
    TURN_AT, EXP_AT = 5, 2
    RING = NP + 2

    def place(b, q):
        return b * RING + q + (2 if q >= (TURN_AT + 1) * PU else 0)

    def turn_place(b, part):
        return b * RING + (TURN_AT + 1) * PU + part

    with Stage(nc, "ex") as st:
        GH = st.sb("GH", [P, 2, J2, BLK])
        IOTA = st.sb("IOTA", [P, NK, UNIT], F16)
        L = st.sb("L", [P, 2, NK, UNIT], F16)
        R = st.sb("R", [P, 2, NK, UNIT], F16)
        RANKS = st.sb("RANKS", [P, PK], F16)
        AS = st.sb("AS", [P, TB, PH, PK, PK])
        TV = st.sb("TV", [P, N, PK])
        AB = st.sb("AB", [P, 3, N * PK], U32)
        RF = st.sb("RF", [P, 2, N * PK], F16)
        HIT = AS[:].rearrange("p a h x y -> p (a h x y)").bitcast(F16).rearrange("p (s a n r) -> p s a n r", s=2, a=TB, r=PK)
        PR = st.sb("PR", [P, N, PK])
        SM = st.sb("SM", [P, N])
        H16 = st.sb("H16", [P, N, PK], F16)
        DUP = st.sb("DUP", [P, 3, TB, 2, HK])
        KEYS = st.sb("KEYS", [P, 2, 3, BLK], F16)
        HP = st.ps("HP", [P, 2, 2, BLK])
        GP = st.ps("GP", [P, 2, UNIT, J2])
        OP = st.ps("OP", [P, 2, 512])
        loaded = st.sem("loaded")
        hidden = st.sem("hidden")
        hidden_read = st.sem("hidden_read")
        left_ready = st.sem("left_ready")
        right_ready = st.sem("right_ready")
        gates_ready = st.sem("gates_ready")
        gated = st.sem("gated")
        out_ready = st.sem("out_ready")
        out_read = st.sem("out_read")
        summed = st.sem("summed")
        picked = st.sem("picked")
        ranks_ready = st.sem("ranks_ready")
        hits_ready = st.sem("hits_ready")
        hits_read = st.sem("hits_read")
        exp_ready = st.sem("exp_ready")
        arranged = st.sem("arranged")
        dve_chain = st.sem("dve_chain")
        with st.block() as block:
            @block.sync
            def _(sp):
                sp.dma_start(IOTA[:], io["key_numbers"]).then_inc(loaded, 16)
                sp.dma_start(RANKS[:], io["rank_numbers"]).then_inc(loaded, 16)

            @block.tensor
            def _(pe):
                def hid(b, q):
                    n = place(b, q)
                    if n >= 2:
                        pe.wait_ge(hidden_read, n - 1)
                    for a in range(2):
                        for k in range(KD):
                            ins = pe.matmul(HP[:, n % 2, a, :], DOWN[:, k, 2 * q + a, :], XT[:, k, b * BLK:(b + 1) * BLK],
                                            start=(k == 0), stop=(k == KD - 1))
                    ins.then_inc(hidden, 1)

                def turn(b):
                    pe.wait_ge(arranged, b + 1)
                    for part, qs in ((0, (0, 1)), (1, (2,))):
                        n = turn_place(b, part)
                        pe.wait_ge(hidden_read, n - 1)
                        for q in qs:
                            for a in range(TB):
                                ins = pe.transpose(HP[:, n % 2, q % 2, a * P:(a + 1) * P], DUP[:, q, a].rearrange("p a k -> p (a k)"), ident[:, 0:P])
                        ins.then_inc(hidden, 1)

                def gates(n):
                    pe.wait_ge(left_ready, n + 1)
                    pe.wait_ge(right_ready, n + 1)
                    if n >= 2:
                        pe.wait_ge(gated, n - 1)
                    for t in range(UNIT):
                        for jp in range(2):
                            ins = pe.matmul(GP[jp * NK:(jp + 1) * NK, n % 2, t, :], L[:, n % 2, :, t], R[:, n % 2, jp * J2:(jp + 1) * J2, t],
                                            start=True, stop=True, tile_position=(0, jp * NK))
                    ins.then_inc(gates_ready, 1)

                def answer(m):
                    b, a = m // TB, m % TB
                    pe.wait_ge(gated, (m + 1) * P // UNIT)
                    if m >= 2:
                        pe.wait_ge(out_read, m - 1)
                    for j in range(J2):
                        ins = pe.matmul(OP[:, m % 2, 0:D], GH[:, b % 2, j, a * P:(a + 1) * P], UP[:, j, :], start=(j == 0), stop=(j == J2 - 1))
                    ins.then_inc(out_ready, 1)

                expert_loads.wait(pe)
                for u in range(UB):
                    for q in range(PU):
                        hid(0, u * PU + q)
                    if u == TURN_AT:
                        turn(0)
                for n in range(NU):
                    b, u = n // UB, n % UB
                    gates(n)
                    if n % (P // UNIT) == 1 and n > P // UNIT:
                        answer(n // (P // UNIT) - 1)
                    if b + 1 < NB:
                        for q in range(PU):
                            hid(b + 1, u * PU + q)
                        if u == TURN_AT:
                            turn(b + 1)
                answer(NT - 1)

            @block.scalar
            def _(act):
                for b in range(NB):
                    for q in range(NP):
                        n = place(b, q)
                        act.wait_ge(hidden, n + 1)
                        if b >= 2:
                            act.wait_ge(out_ready, (b - 1) * TB)
                        act.activation(GH[:, b % 2, 2 * q:2 * q + 2, :], HP[:, n % 2], ACT.Gelu_apprx_tanh).then_inc(hidden_read, 1)
                        if q == EXP_AT * PU:
                            act.wait_ge(picked, b + 1)
                            act.activation(PR[:], PR[:], ACT.Exp).then_inc(exp_ready, 1)
                        if q == TURN_AT * PU + PU - 1:
                            n = turn_place(b, 0)
                            act.wait_ge(hidden, n + 1)
                            act.activation(KEYS[:, b % 2, 0:2, :], HP[:, n % 2], ACT.Copy).then_inc(hidden_read, 1)
                            act.wait_ge(hidden, n + 2)
                            act.activation(KEYS[:, b % 2, 2, :], HP[:, (n + 1) % 2, 0, :], ACT.Copy).then_inc(hidden_read, 1)

            @block.gpsimd
            def _(pool):
                for b in range(NB):
                    if b:
                        pool.wait_ge(hits_read, b)
                    for a in range(TB):
                        t = b * TB + a
                        sx = SV[:, t, 0:PH, :].rearrange("p h (a o) -> p h a o", o=1).to_broadcast([P, PH, PK, PK])
                        sy = SV[:, t, PH:, :].rearrange("p h (o b) -> p h o b", o=1).to_broadcast([P, PH, PK, PK])
                        pool.tensor_tensor(AS[:, a], sx, sy, ALU.add).then_inc(summed, 1)
                    pool.wait_ge(ranks_ready, b + 1)
                    for side in range(2):
                        for a in range(TB):
                            hit = HIT[:, side, a].rearrange("p (h k) r -> p h k r", h=PH)
                            key = IV[:, b * TB + a, side * PH:(side + 1) * PH, :].rearrange("p h (o r) -> p h o r", o=1).to_broadcast([P, PH, PK, PK])
                            ins = pool.tensor_tensor(hit, hit, key, ALU.mult)
                    ins.then_inc(hits_ready, 1)

            @block.vector
            def _(v):
                ch = Chain(v, dve_chain)

                def answer_out(v, m):
                    v.wait_ge(out_ready, m + 1)
                    v.tensor_tensor(X[:, m, :], X[:, m, :], OP[:, m % 2, 0:D], ALU.add).then_inc(out_read, 1)

                def sides(n):
                    b, tok = n // UB, slice(n % UB * UNIT, (n % UB + 1) * UNIT)

                    def along(q):
                        return KEYS[:, b % 2, q, tok].rearrange("p (o t) -> p o t", o=1).to_broadcast([P, NK, UNIT])

                    if n % UB == 0:
                        v.wait_ge(hidden_read, turn_place(b, 1) + 1)
                    if n >= 2:
                        v.wait_ge(gates_ready, n - 1)
                    ch.link(v.tensor_tensor(R[:, n % 2], IOTA[:], along(1), ALU.is_equal))
                    v.tensor_tensor(L[:, n % 2], IOTA[:], along(0), ALU.is_equal).then_inc(left_ready, 1)
                    v.tensor_tensor(R[:, n % 2], R[:, n % 2], along(2), ALU.mult).then_inc(right_ready, 1)
                    v.wait_ge(right_ready, n + 1)

                def pick(b, a):
                    v.wait_ge(summed, b * TB + a + 1)
                    for h in range(PH):
                        ins = v.max(TV[:, a * PH + h, :], AS[:, a, h].rearrange("p a b -> p (a b)"))
                    ch.link(ins)
                    flat = AB[:, 0].rearrange("p (n k) -> p n k", k=PK)
                    for h in range(PH):
                        ins = v.max_index(flat[:, a * PH + h, :], TV[:, a * PH + h, :], AS[:, a, h].rearrange("p a b -> p (a b)"))
                    ch.link(ins)
                    if a == TB - 1:
                        v.tensor_tensor(PR[:], TV[:], TV[:, :, 0:1].to_broadcast([P, N, PK]), ALU.subtract).then_inc(picked, 1)

                def ranks():
                    v.tensor_scalar(AB[:, 1], AB[:, 0], 3, None, ALU.logical_shift_right)
                    ch.link(v.tensor_scalar(AB[:, 2], AB[:, 0], PK - 1, None, ALU.bitwise_and))
                    ch.link(v.tensor_copy(RF[:], AB[:, 1:3]))
                    for side in range(2):
                        rank = RF[:, side].rearrange("p (n o) -> p n o", o=1).to_broadcast([P, TB * HK, PK])
                        ins = v.tensor_tensor(HIT[:, side].rearrange("p a n r -> p (a n) r"), rank,
                                              RANKS[:].rearrange("p (o r) -> p o r", o=1).to_broadcast([P, TB * HK, PK]), ALU.is_equal)
                    ins.then_inc(ranks_ready, 1)

                def keys(b):
                    v.wait_ge(hits_ready, b + 1)
                    for side in range(2):
                        for a in range(TB):
                            ins = v.tensor_reduce(DUP[:, side, a, 0, :], HIT[:, side, a], AX_X, ALU.add)
                    ins.then_inc(hits_read, 1)
                    v.wait_ge(hits_read, b + 1)
                    for side in range(2):
                        v.tensor_copy(DUP[:, side, :, 1, :], DUP[:, side, :, 0, :])

                def probabilities(b):
                    v.wait_ge(exp_ready, b + 1)
                    ch.link(v.tensor_reduce(SM[:], PR[:], AX_X, ALU.add))
                    ch.link(v.reciprocal(SM[:], SM[:]))
                    ch.link(v.tensor_scalar(SM[:], SM[:], PSCALE, None, ALU.mult))
                    ch.link(v.tensor_tensor(PR[:], PR[:], SM[:].rearrange("p (n o) -> p n o", o=1).to_broadcast([P, N, PK]), ALU.mult))
                    ch.link(v.tensor_copy(H16[:], PR[:]))
                    pr, h16 = (x[:].rearrange("p (t h) k -> p t (h k)", t=TB) for x in (PR, H16))
                    v.tensor_copy(DUP[:, 2, :, 0, :], h16)
                    v.tensor_tensor(DUP[:, 2, :, 1, :], pr, h16, ALU.subtract).then_inc(arranged, 1)

                def select_step(b, u):
                    if u < TB:
                        pick(b, u)
                        if u == TB - 1:
                            ranks()
                    elif u == 3:
                        keys(b)
                    elif u == 4:
                        probabilities(b)

                v.wait_ge(loaded, 32)
                for u in range(UB):
                    select_step(0, u)
                sides(0)
                for n in range(NU):
                    b, u = n // UB, n % UB
                    if n + 1 < NU:
                        sides(n + 1)
                    v.wait_ge(gates_ready, n + 1)
                    v.wait_ge(hidden_read, (b + 1) * RING)
                    gh = GH[:, b % 2, :, u * UNIT:(u + 1) * UNIT]
                    v.scalar_tensor_tensor(gh, GP[:, n % 2].rearrange("p t j -> p j t"), 1.0 / PSCALE, gh, ALU.mult, ALU.mult).then_inc(gated, 1)
                    if n % (P // UNIT) == 2 and n > P // UNIT:
                        answer_out(v, n // (P // UNIT) - 1)
                    if b + 1 < NB:
                        select_step(b + 1, u)
                answer_out(v, NT - 1)


STAGES = [stage_mamba, stage_xattn, stage_moe, stage_performer, stage_s4d, stage_peer]


FIRST_INPUTS = {stage_xattn: xattn_inputs, stage_s4d: topk_inputs, stage_peer: sides_inputs}


def issue_inputs(nc, inputs):
    with Stage(nc, "inputs") as st:
        with st.block() as block:
            @block.sync
            def _(sp):
                inputs.loads.issue(sp)


def build(nc, io, out, stages=None):
    with nc.sbuf_tensor("X", [P, NT, D], F32) as X, nc.sbuf_tensor("XT", [P, KD, T], F32) as XT, \
            nc.sbuf_tensor("ident", [P, NI], F32) as ident, ExitStack() as until_peer:
        KF = until_peer.enter_context(nc.sbuf_tensor("KF", [P, NF, D], F32))
        stored = nc.alloc_semaphore("stored")
        stages = STAGES if stages is None else stages
        stage_load(nc, io, X, XT, ident, with_x=stage_mamba not in stages)
        inputs = None
        for stage in stages:
            if stage is stage_peer:
                until_peer.close()
            if inputs is None and stage in FIRST_INPUTS:
                inputs = FIRST_INPUTS[stage](nc, io)
                issue_inputs(nc, inputs)
            inputs = stage(nc, io, X, XT, ident, KF, inputs)
            nc.clear_and_free_semaphores(list(Stage.semaphores))
            Stage.semaphores.clear()
            nc.all_engine_barrier()
        if stages[-1] is stage_peer:
            norm_only(nc, "last", X, X, None, ident, store=(out, stored))
        else:
            stage_store(nc, out, X, stored)


def columns(*vectors):
    return np.stack([v.reshape(-1, P).T for v in vectors], axis=1)


def rows(*vectors):
    return np.tile(np.stack(vectors), (P, 1, 1))


def layouts(inputs):
    a = {k: np.asarray(v) for k, v in inputs.items()}
    io = {}
    io["x"] = a["x"]
    io["xT"] = a["x"].reshape(T, D).T
    io["ident"] = np.concatenate([np.eye(P), np.full((P, 1), 1e-5), np.full((P, 1), 1e-6), np.ones((P, P))], axis=1).astype(np.float32)
    io["L0_attn_in_projT"] = a["L0_attn_in_proj_w"].T
    io["L0_attn_out_projT"] = a["L0_attn_out_proj_w"].T
    xp = a["L0_attn_x_proj_w"]
    io["L0_attn_x_delta"] = np.repeat(xp[0:1].T, P, axis=1)
    io["L0_attn_x_bc"] = np.concatenate([xp[1:].T] * 3, axis=1)
    sel = np.zeros((96, 32, P), np.uint16)
    for r in range(96):
        sel[r, r % 32, :] = BF16_ONE
    io["sel_bc"] = sel
    io["L0_attn_conv_w"] = a["L0_attn_conv_w"]
    io["L0_attn_vec"] = columns(a["L0_attn_conv_b"], a["L0_attn_dt_proj_w"][:, 0], a["L0_attn_dt_proj_b"], a["L0_attn_D"])
    io["L0_attn_A_log"] = a["L0_attn_A_log"]
    io["ctxT"] = a["ctx_768"].reshape(T, DCTX).T
    for n in ("Wq", "Wk", "Wv", "Wo"):
        io["L0_xattn_" + n] = a["L0_xattn_" + n]
    io["L0_xattn_bo"] = np.tile(a["L0_xattn_bo"], (P, 1))
    io["L0_ffn_gateT"] = a["L0_ffn_gate_w"].T
    io["L0_ffn_w1"] = a["L0_ffn_w1"]
    io["L0_ffn_w2"] = a["L0_ffn_w2"]
    io["tri"] = np.stack([np.triu(np.ones((P, P))), np.ones((P, P))], axis=1).astype(np.float32)
    io["expert_numbers"] = np.tile(np.arange(NE, dtype=np.float32), (P, 1))
    io["spill_rows"] = (SLOTS + np.arange(T).reshape(NT, P).T).astype(np.float32)
    io["L1_attn_ln"] = columns(a["L1_attn_ln1_scale"], a["L1_attn_ln1_bias"], a["L1_attn_ln2_scale"], a["L1_attn_ln2_bias"])
    for n in ("wq", "wk"):
        io["L1_attn_" + n] = np.pad(a["L1_attn_" + n], ((0, 0), (0, 0), (0, LPAD - LD))).reshape(D, LH * LPAD)
    io["L1_attn_wv"] = a["L1_attn_wv"].reshape(D, D)
    io["L1_attn_wo"] = a["L1_attn_wo"].reshape(D, D)
    io["L1_attn_w1"] = a["L1_attn_w1"]
    io["L1_attn_w2"] = a["L1_attn_w2"]
    io["L1_attn_b1"] = columns(a["L1_attn_b1"])
    io["L1_attn_b2"] = np.tile(a["L1_attn_b2"], (P, 1))
    for n in ("Wq", "Wk", "Wv", "W_film_in", "W_film_out", "W1", "W2"):
        io["L1_xattn_" + n] = a["L1_xattn_" + n]
    for n in ("b_film_in", "b_film_out"):
        io["L1_xattn_" + n] = a["L1_xattn_" + n][None]
    io["L1_xattn_b2"] = np.tile(a["L1_xattn_b2"], (P, 1))
    io["L1_xattn_b1"] = columns(a["L1_xattn_b1"])
    io["L1_xattn_ffn_ln"] = columns(a["L1_xattn_g_ffn"], a["L1_xattn_b_ffn"])
    io["L1_xattn_norm_in"] = rows(a["L1_xattn_g_norm_in"], a["L1_xattn_b_norm_in"])
    io["L1_xattn_norm_out"] = rows(a["L1_xattn_g_norm_out"], a["L1_xattn_b_norm_out"])
    io["L1_xattn_D_skip"] = np.tile(a["L1_xattn_D_skip"], (P, 1))
    io["L1_xattn_gate"] = np.tile(a["L1_xattn_mod_gate"].reshape(1, 1), (P, 1))
    for n, m in (("text_mask", "mask_BxS_bf1"), ("vision_mask", "mask_BxS2_bf1")):
        io[n] = np.tile(a[m].reshape(1, T).view(np.uint8), (P, 1))
    io["L1_xattn_s4d"] = np.stack([np.tile(a["L1_xattn_log_dt"], (P, 1))] +
                                  [np.concatenate([a["L1_xattn_" + n].T] * 2) for n in ("A_re", "A_im", "C_re", "C_im")], axis=1)
    low = (np.arange(P) < NST)[:, None]
    io["phases"] = np.concatenate([np.where(low, x, y) for x, y in ((0.25, 0.0), (0.5, 0.25), (0.25, 0.5), (0, 0))], axis=1).astype(np.float32)
    angle = 2 * np.pi * np.outer(np.arange(S), np.arange(S) + 0.5) / (2 * S)
    forward = np.stack([np.cos(angle).reshape(S, 2, P), -np.sin(angle).reshape(S, 2, P)], axis=2).reshape(S, NF, P)
    io["dft_kernel"] = forward.reshape(HI, LO // LB, LB, NF, P).transpose(2, 0, 1, 3, 4).reshape(P, LO // LB, NF, P).astype(np.float32)
    io["dft"] = forward.reshape(2, P, NF, P).transpose(1, 0, 2, 3).astype(np.float32)
    io["dft_inverse"] = (forward.reshape(2, P, NF, P).transpose(3, 2, 0, 1) / S).astype(np.float32)
    io["L1_ffn_w_q"] = a["L1_ffn_w_q"]
    io["L1_ffn_bn"] = columns(a["L1_ffn_bn_gamma"], a["L1_ffn_bn_beta"])
    io["L1_ffn_keysT"] = a["L1_ffn_keys"].transpose(3, 2, 0, 1).reshape(P, NC_, NK)
    tiles = (NK, 2, J2, D)
    io["L1_ffn_down"] = a["L1_ffn_down_embed"].reshape(tiles).transpose(3, 2, 1, 0).reshape(KD, P, J2, P).transpose(1, 0, 2, 3)
    io["L1_ffn_up"] = a["L1_ffn_up_embed"].reshape(tiles).transpose(1, 0, 2, 3).reshape(P, J2, D)
    io["rank_numbers"] = np.tile(np.arange(PK, dtype=np.float16), (P, 1))
    io["key_numbers"] = np.tile(np.arange(NK, dtype=np.float16)[None, :, None], (P, 1, UNIT))
    return {k: np.ascontiguousarray(v) for k, v in io.items()}


def kernel(**inputs):
    import concourse.bacc as bacc
    from concourse.bass_utils import run_bass_kernel_spmd

    nc = bacc.Bacc("TRN2", target_bir_lowering=False, num_devices=1)
    arrays = layouts(inputs)
    io = {name: nc.dram_tensor(f"in_{name}", a.shape, mybir.dt.from_np(a.dtype), kind="ExternalInput").ap()
          for name, a in arrays.items()}
    out = nc.dram_tensor("out_0", (B, S, D), F32, kind="ExternalOutput").ap()
    build(nc, io, out)
    r = run_bass_kernel_spmd(nc, [{f"in_{k}": a for k, a in arrays.items()}], core_ids=[0])
    return r.results[0]["out_0"]
```
